# Optimizing a Trainium2 kernel written in Bass

```python
import numpy as np
import jax
import jax.numpy as jnp

def _softmax(x, axis=-1):
    return jax.nn.softmax(x, axis=axis)

def _gelu(x):
    return jax.nn.gelu(x, approximate=True)

def _silu(x):
    return jax.nn.silu(x)

def _sigmoid(x):
    return jax.nn.sigmoid(x)

def _layernorm(x, axis=-1, eps=1e-05):
    m = jnp.mean(x, axis=axis, keepdims=True)
    v = jnp.var(x, axis=axis, keepdims=True)
    return (x - m) / jnp.sqrt(v + eps)

def _scatter_add(tgt, idx, src, axis=0):
    return tgt.at[idx].add(src)

def _segment_sum(src, seg, n):
    return jax.ops.segment_sum(src, seg, n)
kernel_name = 'mk_adaln_d2_jaxref_r8_0090d8'

def setup_inputs(seed: int=0):
    np.random.seed(seed)
    _w = jnp.asarray

    def _L0_attn_setup():
        import jax, jax.numpy as jnp
        import numpy as np
        B, S, E, H, G = (2, 256, 256, 16, 4)
        D = E // H
        key = jax.random.key(seed)
        ks = jax.random.split(key, 7)
        scale = 1.0 / np.sqrt(E)
        x = jax.random.normal(ks[0], (B, S, E), dtype=jnp.float32)
        Wq = jax.random.normal(ks[1], (H, E, D), dtype=jnp.float32) * scale
        bq = jax.random.normal(ks[2], (H, D), dtype=jnp.float32) * 0.02
        Wk = jax.random.normal(ks[3], (G, E, D), dtype=jnp.float32) * scale
        bk = jax.random.normal(ks[4], (G, D), dtype=jnp.float32) * 0.02
        Wv = jax.random.normal(ks[5], (G, E, D), dtype=jnp.float32) * scale
        bv = jax.random.normal(ks[6], (G, D), dtype=jnp.float32) * 0.02
        return {'x': x, 'Wq': Wq, 'bq': bq, 'Wk': Wk, 'bk': bk, 'Wv': Wv, 'bv': bv}
    _L0_attn_in = _L0_attn_setup()

    def _L0_ffn_setup():
        import jax, jax.numpy as jnp
        import numpy as np
        from jax import lax
        HIDDEN = 256
        N_EXPERTS = 64
        TOP_K = 6
        N_GROUP = 8
        TOPK_GROUP = 4
        MOE_INTER = 128
        SHARED_INTER = 512
        ROUTED_SCALE = 2.5

        def relu2(x):
            r = jax.nn.relu(x)
            return r * r

        def _route(x2d, gate_w, gate_bias):
            T = x2d.shape[0]
            logits = jnp.einsum('th,eh->te', x2d.astype(jnp.float32), gate_w.astype(jnp.float32))
            scores = jax.nn.sigmoid(logits)
            scores_b = scores + gate_bias[None, :]
            grp = scores_b.reshape(T, N_GROUP, N_EXPERTS // N_GROUP)
            grp_score = lax.top_k(grp, 2)[0].sum(axis=-1)
            _, gidx = lax.top_k(grp_score, TOPK_GROUP)
            gmask = jax.nn.one_hot(gidx, N_GROUP, dtype=jnp.float32).sum(axis=1)
            emask = jnp.repeat(gmask, N_EXPERTS // N_GROUP, axis=1)
            masked = jnp.where(emask > 0, scores_b, -jnp.inf)
            _, eidx = lax.top_k(masked, TOP_K)
            w = jnp.take_along_axis(scores, eidx, axis=1)
            w = w / (w.sum(axis=-1, keepdims=True) + 1e-20) * ROUTED_SCALE
            route_w = jnp.zeros((T, N_EXPERTS), jnp.float32).at[jnp.arange(T)[:, None], eidx].set(w)
            return route_w
        key = jax.random.key(seed)
        ks = jax.random.split(key, 7)
        s_h = 1.0 / np.sqrt(HIDDEN)
        s_i = 1.0 / np.sqrt(MOE_INTER)
        s_s = 1.0 / np.sqrt(SHARED_INTER)
        return {'hidden_states': jax.random.normal(ks[0], (2, 64, HIDDEN), jnp.float32), 'gate_w': jax.random.normal(ks[1], (N_EXPERTS, HIDDEN), jnp.float32) * s_h, 'gate_bias': jax.random.normal(ks[2], (N_EXPERTS,), jnp.float32) * 0.1, 'w_up_shared': jax.random.normal(ks[3], (HIDDEN, SHARED_INTER), jnp.float32) * s_h, 'w_down_shared': jax.random.normal(ks[4], (SHARED_INTER, HIDDEN), jnp.float32) * s_s, 'w1_experts': jax.random.normal(ks[5], (N_EXPERTS, HIDDEN, MOE_INTER), jnp.float32) * s_h, 'w2_experts': jax.random.normal(ks[6], (N_EXPERTS, MOE_INTER, HIDDEN), jnp.float32) * s_i}
    _L0_ffn_in = _L0_ffn_setup()
    _L0_c = _w((lambda *s: np.random.randn(*s).astype(np.float32) * 0.05)(8, 256))
    _L0_wmod = _w((lambda *s: np.random.randn(*s).astype(np.float32) * 0.05)(256, 6 * 256) * 256 ** (-0.5))

    def _L1_attn_setup():
        import jax, jax.numpy as jnp
        import numpy as np
        D_MODEL = 256
        N_QUERY = 4
        N_HEAD = 8
        D_HEAD = D_MODEL // (N_QUERY * N_HEAD)
        D_KV = D_HEAD * N_HEAD
        BATCH, SEQ = (2, 256)
        key = jax.random.key(seed)
        ks = jax.random.split(key, 5)
        w_scale = 1.0 / np.sqrt(D_MODEL).astype(np.float32)
        x = jax.random.normal(ks[0], (BATCH, SEQ, D_MODEL), jnp.float32)
        Wq = jax.random.normal(ks[1], (D_MODEL, D_MODEL), jnp.float32) * w_scale
        Wk = jax.random.normal(ks[2], (D_KV, D_MODEL), jnp.float32) * w_scale
        Wv = jax.random.normal(ks[3], (D_KV, D_MODEL), jnp.float32) * w_scale
        memory = jax.random.normal(ks[4], (D_KV, D_KV), jnp.float32) * 0.02
        memory_norm = jnp.ones((D_KV, 1), jnp.float32)
        memory_weight = jnp.ones((1,), jnp.float32)
        return dict(x=x, Wq=Wq, Wk=Wk, Wv=Wv, memory=memory, memory_norm=memory_norm, memory_weight=memory_weight)
    _L1_attn_in = _L1_attn_setup()

    def _L1_ffn_setup():
        import math
        import jax, jax.numpy as jnp
        import numpy as np
        from jax import lax
        D = 256
        I = 128
        E = 32
        K = 4
        NG = 8
        TKG = 3
        NSH = 2
        SCALE = 2.5
        CF = 1.25
        B, S = (2, 256)

        def _router(x, router_w, e_bias):
            scores = jax.nn.sigmoid(x @ router_w.T)
            sc = scores + e_bias[None, :]
            T = x.shape[0]
            gs = sc.reshape(T, NG, E // NG)
            group_scores = lax.top_k(gs, 2)[0].sum(-1)
            _, gidx = lax.top_k(group_scores, TKG)
            gmask = jnp.zeros((T, NG), sc.dtype).at[jnp.arange(T)[:, None], gidx].set(1.0)
            smask = jnp.repeat(gmask, E // NG, axis=1)
            masked = jnp.where(smask > 0, sc, 0.0)
            _, topk_idx = lax.top_k(masked, K)
            topk_w = jnp.take_along_axis(scores, topk_idx, axis=1)
            topk_w = topk_w / (topk_w.sum(-1, keepdims=True) + 1e-20)
            topk_w = topk_w * SCALE
            return (topk_idx.astype(jnp.int32), topk_w)

        def _moe_forward(hidden_states, router_w, e_bias, W_gate, W_up, W_down, shared_gate, shared_up, shared_down):
            b, s, d = hidden_states.shape
            T = b * s
            C = int(math.ceil(CF * T / E))
            EC = E * C
            x = hidden_states.reshape(T, d)
            topk_idx, topk_w = _router(x, router_w, e_bias)
            expert_flat = topk_idx.reshape(-1)
            w_flat = topk_w.reshape(-1)
            tok_flat = jnp.repeat(jnp.arange(T, dtype=jnp.int32), K)
            sort_ix = jnp.argsort(expert_flat)
            e_sorted = expert_flat[sort_ix]
            tok_s = tok_flat[sort_ix]
            w_s = w_flat[sort_ix]
            counts = jnp.zeros(E, jnp.int32).at[e_sorted].add(1)
            group_start = jnp.concatenate([jnp.zeros(1, jnp.int32), jnp.cumsum(counts)[:-1].astype(jnp.int32)])
            pos = jnp.arange(T * K, dtype=jnp.int32) - group_start[e_sorted]
            valid = pos < C
            dest = e_sorted * C + jnp.where(valid, pos, 0)
            slots_token = jnp.zeros(EC, jnp.int32).at[dest].add(jnp.where(valid, tok_s, 0))
            slots_w = jnp.zeros(EC, w_s.dtype).at[dest].add(jnp.where(valid, w_s, 0.0))
            Xp = x[slots_token].reshape(E, C, d)
            G = jnp.einsum('ecd,edi->eci', Xp, W_gate)
            U = jnp.einsum('ecd,edi->eci', Xp, W_up)
            Y = jnp.einsum('eci,eid->ecd', jax.nn.silu(G) * U, W_down)
            Yf = Y.reshape(EC, d) * slots_w[:, None]
            out = jnp.zeros((T, d), x.dtype).at[slots_token].add(Yf)
            shared = jax.nn.silu(x @ shared_gate.T) * (x @ shared_up.T) @ shared_down.T
            return (out + shared).reshape(b, s, d)
        key = jax.random.key(seed)
        ks = jax.random.split(key, 8)

        def rn(k, shape, scale=0.02):
            return jax.random.normal(k, shape, jnp.float32) * scale
        return {'hidden_states': jax.random.normal(ks[0], (B, S, D), jnp.float32), 'router_w': rn(ks[1], (E, D)), 'e_bias': jnp.zeros((E,), jnp.float32), 'W_gate': rn(ks[2], (E, D, I)), 'W_up': rn(ks[3], (E, D, I)), 'W_down': rn(ks[4], (E, I, D)), 'shared_gate': rn(ks[5], (I * NSH, D)), 'shared_up': rn(ks[6], (I * NSH, D)), 'shared_down': rn(ks[7], (D, I * NSH))}
    _L1_ffn_in = _L1_ffn_setup()
    _L1_c = _w((lambda *s: np.random.randn(*s).astype(np.float32) * 0.05)(8, 256))
    _L1_wmod = _w((lambda *s: np.random.randn(*s).astype(np.float32) * 0.05)(256, 6 * 256) * 256 ** (-0.5))
    _d = {'L0_attn_x': _L0_attn_in['x'], 'L0_attn_Wq': _L0_attn_in['Wq'], 'L0_attn_bq': _L0_attn_in['bq'], 'L0_attn_Wk': _L0_attn_in['Wk'], 'L0_attn_bk': _L0_attn_in['bk'], 'L0_attn_Wv': _L0_attn_in['Wv'], 'L0_attn_bv': _L0_attn_in['bv'], 'L0_ffn_gate_w': _L0_ffn_in['gate_w'], 'L0_ffn_gate_bias': _L0_ffn_in['gate_bias'], 'L0_ffn_w_up_shared': _L0_ffn_in['w_up_shared'], 'L0_ffn_w_down_shared': _L0_ffn_in['w_down_shared'], 'L0_ffn_w1_experts': _L0_ffn_in['w1_experts'], 'L0_ffn_w2_experts': _L0_ffn_in['w2_experts'], 'L0_c': _L0_c, 'L0_wmod': _L0_wmod, 'L1_attn_Wq': _L1_attn_in['Wq'], 'L1_attn_Wk': _L1_attn_in['Wk'], 'L1_attn_Wv': _L1_attn_in['Wv'], 'L1_attn_memory': _L1_attn_in['memory'], 'L1_attn_memory_norm': _L1_attn_in['memory_norm'], 'L1_attn_memory_weight': _L1_attn_in['memory_weight'], 'L1_ffn_router_w': _L1_ffn_in['router_w'], 'L1_ffn_e_bias': _L1_ffn_in['e_bias'], 'L1_ffn_W_gate': _L1_ffn_in['W_gate'], 'L1_ffn_W_up': _L1_ffn_in['W_up'], 'L1_ffn_W_down': _L1_ffn_in['W_down'], 'L1_ffn_shared_gate': _L1_ffn_in['shared_gate'], 'L1_ffn_shared_up': _L1_ffn_in['shared_up'], 'L1_ffn_shared_down': _L1_ffn_in['shared_down'], 'L1_c': _L1_c, 'L1_wmod': _L1_wmod}
    _x0 = _d['L0_attn_x']
    _d['L0_attn_x'] = jax.random.normal(jax.random.fold_in(jax.random.key(seed), 1), (8, 512, 256), dtype=_x0.dtype)
    del _x0
    return _d

def reference(L0_attn_x, L0_attn_Wq, L0_attn_bq, L0_attn_Wk, L0_attn_bk, L0_attn_Wv, L0_attn_bv, L0_ffn_gate_w, L0_ffn_gate_bias, L0_ffn_w_up_shared, L0_ffn_w_down_shared, L0_ffn_w1_experts, L0_ffn_w2_experts, L0_c, L0_wmod, L1_attn_Wq, L1_attn_Wk, L1_attn_Wv, L1_attn_memory, L1_attn_memory_norm, L1_attn_memory_weight, L1_ffn_router_w, L1_ffn_e_bias, L1_ffn_W_gate, L1_ffn_W_up, L1_ffn_W_down, L1_ffn_shared_gate, L1_ffn_shared_up, L1_ffn_shared_down, L1_c, L1_wmod):

    def _L0_attn_ref(x, Wq, bq, Wk, bk, Wv, bv):
        import jax, jax.numpy as jnp
        import numpy as np
        B, S, E, H, G = (2, 256, 256, 16, 4)
        D = E // H
        h, e, d = Wq.shape
        g = Wk.shape[0]
        per = h // g
        s = x.shape[1]
        q = jnp.einsum('bse,hed->bhsd', x, Wq) + bq[None, :, None, :]
        kg = jnp.einsum('bse,ged->bgsd', x, Wk) + bk[None, :, None, :]
        vg = jnp.einsum('bse,ged->bgsd', x, Wv) + bv[None, :, None, :]
        k = jnp.repeat(kg, per, axis=1)
        v = jnp.repeat(vg, per, axis=1)
        scores = jnp.einsum('bhqd,bhkd->bhqk', q, k) * (1.0 / np.sqrt(d))
        causal = jnp.triu(jnp.ones((s, s), dtype=bool), k=1)
        scores = jnp.where(causal[None, None, :, :], -jnp.inf, scores)
        attn = jax.nn.softmax(scores, axis=-1)
        out = jnp.einsum('bhqk,bhkd->bhqd', attn, v)
        return out.transpose(0, 2, 1, 3).reshape(x.shape[0], s, h * d)

    def _L0_ffn_ref(hidden_states, gate_w, gate_bias, w_up_shared, w_down_shared, w1_experts, w2_experts):
        import jax, jax.numpy as jnp
        import numpy as np
        from jax import lax
        HIDDEN = 256
        N_EXPERTS = 64
        TOP_K = 6
        N_GROUP = 8
        TOPK_GROUP = 4
        MOE_INTER = 128
        SHARED_INTER = 512
        ROUTED_SCALE = 2.5

        def relu2(x):
            r = jax.nn.relu(x)
            return r * r

        def _route(x2d, gate_w, gate_bias):
            T = x2d.shape[0]
            logits = jnp.einsum('th,eh->te', x2d.astype(jnp.float32), gate_w.astype(jnp.float32))
            scores = jax.nn.sigmoid(logits)
            scores_b = scores + gate_bias[None, :]
            grp = scores_b.reshape(T, N_GROUP, N_EXPERTS // N_GROUP)
            grp_score = lax.top_k(grp, 2)[0].sum(axis=-1)
            _, gidx = lax.top_k(grp_score, TOPK_GROUP)
            gmask = jax.nn.one_hot(gidx, N_GROUP, dtype=jnp.float32).sum(axis=1)
            emask = jnp.repeat(gmask, N_EXPERTS // N_GROUP, axis=1)
            masked = jnp.where(emask > 0, scores_b, -jnp.inf)
            _, eidx = lax.top_k(masked, TOP_K)
            w = jnp.take_along_axis(scores, eidx, axis=1)
            w = w / (w.sum(axis=-1, keepdims=True) + 1e-20) * ROUTED_SCALE
            route_w = jnp.zeros((T, N_EXPERTS), jnp.float32).at[jnp.arange(T)[:, None], eidx].set(w)
            return route_w
        orig_shape = hidden_states.shape
        x2d = hidden_states.reshape(-1, HIDDEN)
        shared = jnp.einsum('ti,ih->th', relu2(jnp.einsum('th,hi->ti', x2d, w_up_shared)), w_down_shared)
        route_w = _route(x2d, gate_w, gate_bias)
        h = jnp.einsum('th,ehi->tei', x2d, w1_experts)
        a = relu2(h) * route_w[:, :, None].astype(x2d.dtype)
        routed = jnp.einsum('tei,eih->th', a, w2_experts)
        return (shared + routed).reshape(orig_shape)

    def _L1_attn_ref(x, Wq, Wk, Wv, memory, memory_norm, memory_weight):
        import jax, jax.numpy as jnp
        import numpy as np
        D_MODEL = 256
        N_QUERY = 4
        N_HEAD = 8
        D_HEAD = D_MODEL // (N_QUERY * N_HEAD)
        D_KV = D_HEAD * N_HEAD
        BATCH, SEQ = (2, 256)
        b, s, d = x.shape
        q = x @ Wq.T
        k = x @ Wk.T
        v = x @ Wv.T
        qh = q.reshape(b, s, N_QUERY, N_HEAD, D_HEAD)
        kh = k.reshape(b, s, N_HEAD, D_HEAD)
        vh = v.reshape(b, s, N_HEAD, D_HEAD)
        scale = np.float32(1.0 / np.sqrt(np.float32(D_HEAD)))
        scores = jnp.einsum('bsqhd,bthd->bqhst', qh, kh) * scale
        probs = jax.nn.softmax(scores, axis=-1)
        a_dot = jnp.einsum('bqhst,bthd->bsqhd', probs, vh)
        a_dot = a_dot.reshape(b, s, N_QUERY * N_HEAD, D_HEAD)
        sigma_q = jax.nn.elu(q.reshape(b, s, N_QUERY, D_KV))
        a_mem = sigma_q @ memory / (sigma_q @ memory_norm)
        a_mem = a_mem.reshape(b, s, N_QUERY * N_HEAD, D_HEAD)
        w = jax.nn.sigmoid(memory_weight)
        out = a_dot * (1.0 - w) + a_mem * w
        return out.reshape(b, s, D_MODEL)

    def _L1_ffn_ref(hidden_states, router_w, e_bias, W_gate, W_up, W_down, shared_gate, shared_up, shared_down):
        import math
        import jax, jax.numpy as jnp
        import numpy as np
        from jax import lax
        D = 256
        I = 128
        E = 32
        K = 4
        NG = 8
        TKG = 3
        NSH = 2
        SCALE = 2.5
        CF = 1.25
        B, S = (2, 256)

        def _router(x, router_w, e_bias):
            scores = jax.nn.sigmoid(x @ router_w.T)
            sc = scores + e_bias[None, :]
            T = x.shape[0]
            gs = sc.reshape(T, NG, E // NG)
            group_scores = lax.top_k(gs, 2)[0].sum(-1)
            _, gidx = lax.top_k(group_scores, TKG)
            gmask = jnp.zeros((T, NG), sc.dtype).at[jnp.arange(T)[:, None], gidx].set(1.0)
            smask = jnp.repeat(gmask, E // NG, axis=1)
            masked = jnp.where(smask > 0, sc, 0.0)
            _, topk_idx = lax.top_k(masked, K)
            topk_w = jnp.take_along_axis(scores, topk_idx, axis=1)
            topk_w = topk_w / (topk_w.sum(-1, keepdims=True) + 1e-20)
            topk_w = topk_w * SCALE
            return (topk_idx.astype(jnp.int32), topk_w)

        def _moe_forward(hidden_states, router_w, e_bias, W_gate, W_up, W_down, shared_gate, shared_up, shared_down):
            b, s, d = hidden_states.shape
            T = b * s
            C = int(math.ceil(CF * T / E))
            EC = E * C
            x = hidden_states.reshape(T, d)
            topk_idx, topk_w = _router(x, router_w, e_bias)
            expert_flat = topk_idx.reshape(-1)
            w_flat = topk_w.reshape(-1)
            tok_flat = jnp.repeat(jnp.arange(T, dtype=jnp.int32), K)
            sort_ix = jnp.argsort(expert_flat)
            e_sorted = expert_flat[sort_ix]
            tok_s = tok_flat[sort_ix]
            w_s = w_flat[sort_ix]
            counts = jnp.zeros(E, jnp.int32).at[e_sorted].add(1)
            group_start = jnp.concatenate([jnp.zeros(1, jnp.int32), jnp.cumsum(counts)[:-1].astype(jnp.int32)])
            pos = jnp.arange(T * K, dtype=jnp.int32) - group_start[e_sorted]
            valid = pos < C
            dest = e_sorted * C + jnp.where(valid, pos, 0)
            slots_token = jnp.zeros(EC, jnp.int32).at[dest].add(jnp.where(valid, tok_s, 0))
            slots_w = jnp.zeros(EC, w_s.dtype).at[dest].add(jnp.where(valid, w_s, 0.0))
            Xp = x[slots_token].reshape(E, C, d)
            G = jnp.einsum('ecd,edi->eci', Xp, W_gate)
            U = jnp.einsum('ecd,edi->eci', Xp, W_up)
            Y = jnp.einsum('eci,eid->ecd', jax.nn.silu(G) * U, W_down)
            Yf = Y.reshape(EC, d) * slots_w[:, None]
            out = jnp.zeros((T, d), x.dtype).at[slots_token].add(Yf)
            shared = jax.nn.silu(x @ shared_gate.T) * (x @ shared_up.T) @ shared_down.T
            return (out + shared).reshape(b, s, d)
        return _moe_forward(hidden_states, router_w, e_bias, W_gate, W_up, W_down, shared_gate, shared_up, shared_down)
    x = L0_attn_x
    mod = (_silu(L0_c) @ L0_wmod).reshape(L0_c.shape[0], 6, 1, -1)
    sa, ca, ga, sb, cb, gb = (mod[:, 0], mod[:, 1], mod[:, 2], mod[:, 3], mod[:, 4], mod[:, 5])
    ga = (2 * (ga >= 0) - 1) * jnp.maximum(jnp.abs(ga), 0.25)
    gb = (2 * (gb >= 0) - 1) * jnp.maximum(jnp.abs(gb), 0.25)
    h = _layernorm(x, axis=-1) * (1 + ca) + sa
    x = x + ga * _L0_attn_ref(h, L0_attn_Wq, L0_attn_bq, L0_attn_Wk, L0_attn_bk, L0_attn_Wv, L0_attn_bv)
    h = _layernorm(x, axis=-1) * (1 + cb) + sb
    x = x + gb * _L0_ffn_ref(h, L0_ffn_gate_w, L0_ffn_gate_bias, L0_ffn_w_up_shared, L0_ffn_w_down_shared, L0_ffn_w1_experts, L0_ffn_w2_experts)
    mod = (_silu(L1_c) @ L1_wmod).reshape(L1_c.shape[0], 6, 1, -1)
    sa, ca, ga, sb, cb, gb = (mod[:, 0], mod[:, 1], mod[:, 2], mod[:, 3], mod[:, 4], mod[:, 5])
    ga = (2 * (ga >= 0) - 1) * jnp.maximum(jnp.abs(ga), 0.25)
    gb = (2 * (gb >= 0) - 1) * jnp.maximum(jnp.abs(gb), 0.25)
    h = _layernorm(x, axis=-1) * (1 + ca) + sa
    x = x + ga * _L1_attn_ref(h, L1_attn_Wq, L1_attn_Wk, L1_attn_Wv, L1_attn_memory, L1_attn_memory_norm, L1_attn_memory_weight)
    h = _layernorm(x, axis=-1) * (1 + cb) + sb
    x = x + gb * _L1_ffn_ref(h, L1_ffn_router_w, L1_ffn_e_bias, L1_ffn_W_gate, L1_ffn_W_up, L1_ffn_W_down, L1_ffn_shared_gate, L1_ffn_shared_up, L1_ffn_shared_down)
    return x

_drawn_inputs = setup_inputs


def setup_inputs(seed=0):
    import zlib

    import numpy as np

    out = dict(_drawn_inputs(seed))
    spreads = {'L1_attn_memory_norm': (1.0, 0.2), 'L1_ffn_e_bias': (0.0, 0.8)}
    factors = {'L0_attn_bk': 8.0,
     'L1_attn_Wk': 8.0,
     'L1_attn_Wv': 5.647,
     'L1_ffn_router_w': 8.0,
     'L1_ffn_W_gate': 8.0,
     'L1_ffn_W_up': 8.0,
     'L1_ffn_W_down': 8.0,
     'L1_ffn_shared_gate': 8.0,
     'L1_ffn_shared_up': 8.0,
     'L1_ffn_shared_down': 8.0}
    for name, (base, spread) in spreads.items():
        noise = np.random.default_rng([zlib.crc32(name.encode()), seed]).standard_normal(out[name].shape)
        drawn = base * np.exp(spread * noise) if base else spread * noise
        out[name] = jnp.asarray(drawn.astype(out[name].dtype))
    for name, factor in factors.items():
        out[name] = (out[name] * factor).astype(out[name].dtype)
    return out
```

```python
from contextlib import ExitStack

import numpy as np
import concourse.bass as bass
from concourse import mybir

F32 = mybir.dt.float32
BF16 = mybir.dt.bfloat16
I32 = mybir.dt.int32
ALU = mybir.AluOpType
ACT = mybir.ActivationFunctionType
AX = mybir.AxisListType

P = 128
B, S, C = 8, 512, 256
T = B * S
NT = T // P
QB = S // P
CC = C // P
NEG = -1.0e30
EPS = 1e-5
VW = 32
MROW = 96
KROWS = MROW + 3
NBUF = 4

PAIRS6 = [(0, 0), (0, 1), (1, 0), (1, 1), (0, 2), (2, 0)]
PAIRS9 = PAIRS6 + [(1, 2), (2, 1), (2, 2)]
ATT = [dict(g=4, d=16, pairs=PAIRS6, causal=True, scale=0.25),
       dict(g=8, d=8, pairs=PAIRS9, causal=False, scale=float(np.float32(1.0 / np.sqrt(np.float32(8)))))]
MOE = [dict(e=64, n=8, kg=4, k=6, scale=2.5, cap=None, tiles=T * 6 // P + 64),
       dict(e=32, n=8, kg=3, k=4, scale=2.5, cap=160, tiles=None)]
SLOTS = [MOE[0]["tiles"] * P, MOE[1]["e"] * MOE[1]["cap"]]


class Chain:

    def __init__(self, engine, sem, base=0):
        self.engine, self.sem, self.base, self.n = engine, sem, base, 0

    def __call__(self, instruction):
        self.n += 1
        instruction.then_inc(self.sem, 1)
        self.engine.wait_ge(self.sem, self.base + self.n)


def setup(nc, mem, A):
    sb, d = mem.sb, mem.dram
    mem.ident = sb("ident", [P, P], F32)
    mem.identb = sb("identb", [P, P], BF16)
    mem.mask_q = sb("mask_q", [P, P], BF16)
    mem.mask_k = sb("mask_k", [P, P], BF16)
    mem.before = sb("before", [P, P], BF16)
    mem.onesb = sb("onesb", [P, P], BF16)
    mem.modT = sb("modT", [P, 2, 6 * CC, B], F32)
    mem.wq0 = sb("wq0", [P, CC, C], F32)
    mem.wk0 = sb("wk0", [P, CC, 64], F32)
    mem.wv0 = sb("wv0", [P, CC, 64], F32)
    mem.bq0 = sb("bq0", [P, CC], F32)
    mem.bk0 = sb("bk0", [64, 1], F32)
    mem.bv0 = sb("bv0", [P, 64], F32)
    mem.gbias = [sb("gbias0", [P, 64], F32), sb("gbias1", [P, 32], F32)]
    mem.wmem = sb("wmem", [P, 2], F32)
    mem.memr = sb("memr", [P, 2, 65], F32)
    turned = [("gwT", A["L0_ffn_gate_w"], 64), ("wqT", A["L1_attn_Wq"], 256), ("wkT", A["L1_attn_Wk"], 64),
              ("wvT", A["L1_attn_Wv"], 64), ("rwT", A["L1_ffn_router_w"], 32),
              ("sgT", A["L1_ffn_shared_gate"], 256), ("suT", A["L1_ffn_shared_up"], 256),
              ("sdT", A["L1_ffn_shared_down"], 256)]
    for name, _, rows in turned:
        mem.named[name] = sb(name, [P, CC, rows], F32)
    blocks = [(name, src, r, min(P, rows - r)) for name, src, rows in turned for r in range(0, rows, P)]
    NBK = len(blocks)
    mem.mod_d = d("mod_d", [2, B, 6 * C], F32)

    with ExitStack() as c:
        rows_in = c.enter_context(nc.sbuf_tensor("rows_in", [P, NBK, C], F32))
        c_in = c.enter_context(nc.sbuf_tensor("c_in", [B, 2, C], F32))
        c_e = c.enter_context(nc.sbuf_tensor("c_e", [B, 2, C], F32))
        cT = c.enter_context(nc.sbuf_tensor("cT", [P, 2 * CC, B], F32))
        wmod = c.enter_context(nc.sbuf_tensor("wmod", [P, 2, CC, 6 * C], F32))
        mod = c.enter_context(nc.sbuf_tensor("mod", [B, 2, 6 * C], F32))
        tmp = c.enter_context(nc.sbuf_tensor("tmp_s", [B, 2, 2 * C], F32))
        ps = c.enter_context(nc.psum_tensor("ps_s", [P, 2, 512], F32))
        psm = c.enter_context(nc.psum_tensor("psm_s", [P, 3, 512], F32))
        pst = c.enter_context(nc.psum_tensor("pst_s", [P, 512], F32))
        loaded = mem.sem("s_loaded")
        small = mem.sem("s_small")
        rows_ld = mem.sem("s_rows")
        wmod_ld = mem.sem("s_wmod")
        consts = mem.sem("s_consts")
        dve = mem.sem("s_dve")
        act = mem.sem("s_act")
        pe = mem.sem("s_pe")
        stored = mem.sem("s_stored")
        ready = mem.sem("s_ready")
        memw = mem.sem("s_memw")
        zero0 = mem.sem("s_zero0")
        block = c.enter_context(nc.Block())

        @block.sync
        def _(sp):
            for l in range(2):
                sp.dma_start(c_in[:, l, :], A[f"L{l}_c"]).then_inc(small, 16)
            for i, (_, src, r, n) in enumerate(blocks):
                sp.dma_start(rows_in[0:n, i, :], src[r:r + n, :]).then_inc(rows_ld, 16)
            for l in range(2):
                sp.dma_start(wmod[:, l, :, :], A[f"L{l}_wmod"].rearrange("(c p) n -> p c n", p=P)).then_inc(wmod_ld, 16)
            sp.wait_ge(ready, 1)
            sp.dma_start(mem.mod_d.rearrange("l b n -> b l n"), mod[:, :, :]).then_inc(stored, 16)
            sp.wait_ge(stored, 16)
            sp.wait_ge(loaded, 16 * 15)

        @block.gpsimd
        def _(pool):
            g = nc.gpsimd
            n = 0
            for t, v in ((mem.ident, 0.0), (mem.identb, 0.0), (mem.mask_q, 0.0), (mem.mask_k, 0.0),
                         (mem.before, 1.0), (mem.onesb, 1.0), (mem.memr, 0.0)):
                g.memset(t[:], v).then_inc(consts, 1)
                n += 1
            pool.wait_ge(consts, n)
            for t in (mem.ident, mem.identb):
                g.affine_select(out=t[:, :], in_=t[:, :], compare_op=ALU.not_equal, fill=1.0, base=0,
                                pattern=[[-1, P]], channel_multiplier=1).then_inc(consts, 1)
            g.affine_select(out=mem.mask_q[:, :], in_=mem.mask_q[:, :], compare_op=ALU.is_ge, fill=NEG, base=0,
                            pattern=[[-1, P]], channel_multiplier=1).then_inc(consts, 1)
            g.affine_select(out=mem.mask_k[:, :], in_=mem.mask_k[:, :], compare_op=ALU.is_ge, fill=NEG, base=0,
                            pattern=[[1, P]], channel_multiplier=-1).then_inc(consts, 1)
            g.affine_select(out=mem.before[:, :], in_=mem.before[:, :], compare_op=ALU.is_gt, fill=0.0, base=0,
                            pattern=[[1, P]], channel_multiplier=-1).then_inc(consts, 1)

        @block.scalar
        def _(s):
            q = s.dma_start
            q(mem.wq0[:, :, :].rearrange("p c (h d) -> p c h d", d=16)[:, 0], A["L0_attn_Wq"].rearrange("h (c p) d -> c p h d", p=P)[0]).then_inc(loaded, 16)
            q(mem.wq0[:, :, :].rearrange("p c (h d) -> p c h d", d=16)[:, 1], A["L0_attn_Wq"].rearrange("h (c p) d -> c p h d", p=P)[1]).then_inc(loaded, 16)
            for w, n in ((mem.wk0, "k"), (mem.wv0, "v")):
                for cc in range(CC):
                    q(w[:, :, :].rearrange("p c (h d) -> p c h d", d=16)[:, cc], A[f"L0_attn_W{n}"].rearrange("h (c p) d -> c p h d", p=P)[cc]).then_inc(loaded, 16)
            with nc.allow_non_contiguous_dma(reason="small"):
                q(mem.bq0[:, :], A["L0_attn_bq"].rearrange("h d -> (h d)").rearrange("(c p) -> p c", p=P)).then_inc(loaded, 16)
                q(mem.bk0[:, :], A["L0_attn_bk"].rearrange("h d -> (h d)").rearrange("(p o) -> p o", o=1)).then_inc(loaded, 16)
            q(mem.bv0[:, :], A["L0_attn_bv"].rearrange("h d -> (h d)").partition_broadcast(P)).then_inc(loaded, 16)
            q(mem.gbias[0][:, :], A["L0_ffn_gate_bias"].partition_broadcast(P)).then_inc(loaded, 16)
            q(mem.gbias[1][:, :], A["L1_ffn_e_bias"].partition_broadcast(P)).then_inc(loaded, 16)
            q(mem.wmem[:, 0:1], A["L1_attn_memory_weight"].partition_broadcast(P)).then_inc(memw, 16)
            s.wait_ge(consts, 7)
            for h in range(2):
                q(mem.memr[64 * h:64 * h + 64, h, 0:64], A["L1_attn_memory"]).then_inc(loaded, 16)
                q(mem.memr[64 * h:64 * h + 64, h, 64:65], A["L1_attn_memory_norm"]).then_inc(loaded, 16)
            s.wait_ge(small, 32)
            nc.scalar.activation(c_e[:, :, :], c_in[:, :, :], ACT.Exp, scale=-1.0).then_inc(act, 1)
            s.wait_ge(memw, 16)
            nc.scalar.activation(mem.wmem[:, 1:2], mem.wmem[:, 0:1], ACT.Exp, scale=-1.0).then_inc(act, 1)

        @block.vector
        def _(v):
            do = Chain(v, dve)
            V = nc.vector
            v.wait_ge(act, 2)
            do(V.tensor_scalar(c_e[:, :, :], c_e[:, :, :], 1.0, None, ALU.add))
            do(V.reciprocal(c_e[:, :, :], c_e[:, :, :]))
            do(V.tensor_tensor(c_in[:, :, :], c_in[:, :, :], c_e[:, :, :], ALU.mult))
            do(V.tensor_scalar(mem.wmem[:, 1:2], mem.wmem[:, 1:2], 1.0, None, ALU.add))
            do(V.reciprocal(mem.wmem[:, 0:1], mem.wmem[:, 1:2]))
            do(V.tensor_scalar(mem.wmem[:, 1:2], mem.wmem[:, 0:1], -1.0, 1.0, ALU.mult, ALU.add))
            v.wait_ge(pe, 1)
            do(V.tensor_copy(cT[:, :, :], pst[:, 0:2 * CC * B].rearrange("p (a b) -> p a b", b=B)))
            for l in range(2):
                v.wait_ge(pe, 2 + l)
                do(V.tensor_copy(mod[:, l, :], psm[0:B, :, :].rearrange("p a n -> p (a n)")))
            for l in range(2):
                for j in (2, 5):
                    g = mod[:, l, j * C:(j + 1) * C]
                    do(V.tensor_scalar(tmp[:, 0, 0:C], g, 0.0, 2.0, ALU.is_ge, ALU.mult))
                    do(V.tensor_scalar(tmp[:, 0, 0:C], tmp[:, 0, 0:C], -1.0, None, ALU.add))
                    do(V.tensor_scalar(tmp[:, 1, 0:C], g, -1.0, None, ALU.mult))
                    do(V.tensor_tensor(g, g, tmp[:, 1, 0:C], ALU.max))
                    do(V.tensor_scalar(g, g, 0.25, None, ALU.max))
                    do(V.tensor_tensor(g, g, tmp[:, 0, 0:C], ALU.mult))
                for j in (1, 4):
                    g = mod[:, l, j * C:(j + 1) * C]
                    do(V.tensor_scalar(g, g, 1.0, None, ALU.add))
            V.tensor_copy(tmp[:, 0, 0:1], tmp[:, 0, 1:2]).then_inc(ready, 1)
            v.wait_ge(pe, 4)
            do(V.tensor_copy(mem.modT[:, :, :, :], pst[:, 64:64 + 24 * B].rearrange("p (l a b) -> p l a b", l=2, b=B)))
            for i, (name, _, r, n) in enumerate(blocks):
                v.wait_ge(pe, 5 + i)
                do(V.tensor_copy(mem.named[name][:, :, r:r + n], ps[:, i % 2, 0:2 * P].rearrange("p (c t) -> p c t", t=P)[:, :, 0:n]))

        @block.tensor
        def _(t):
            t.wait_ge(consts, 12)
            t.wait_ge(dve, 6)
            for l in range(2):
                for cc in range(CC):
                    a = 2 * l + cc
                    last = nc.tensor.transpose(pst[:, a * B:(a + 1) * B], c_in[:, l, cc * P:(cc + 1) * P], mem.ident[0:B, 0:B])
            last.then_inc(pe, 1)
            t.wait_ge(dve, 7)
            t.wait_ge(wmod_ld, 32)
            for l in range(2):
                if l:
                    t.wait_ge(dve, 7 + l)
                for n in range(3):
                    for cc in range(CC):
                        last = nc.tensor.matmul(psm[0:B, n, :], cT[:, 2 * l + cc, :], wmod[:, l, cc, n * 512:(n + 1) * 512],
                                                start=(cc == 0), stop=(cc == CC - 1))
                last.then_inc(pe, 1)
            t.wait_ge(ready, 1)
            for l in range(2):
                for a in range(12):
                    o = 64 + (12 * l + a) * B
                    last = nc.tensor.transpose(pst[:, o:o + B], mod[:, l, a * P:(a + 1) * P], mem.ident[0:B, 0:B])
            last.then_inc(pe, 1)
            t.wait_ge(rows_ld, 16 * NBK)
            base = 9 + 2 * (2 * 6 + 2) + 1
            for i, (name, _, r, n) in enumerate(blocks):
                if i >= 2:
                    t.wait_ge(dve, base + i - 1)
                for cc in range(CC):
                    last = nc.tensor.transpose(ps[:, i % 2, cc * P:cc * P + n], rows_in[0:n, i, cc * P:(cc + 1) * P], mem.ident[0:n, 0:n])
                last.then_inc(pe, 1)


def prime(nc, sems):
    with nc.Block() as block:
        @block.gpsimd
        def _(pool):
            for sem in sems:
                nc.gpsimd.sem_inc(sem, 1)


def projections(nc, mem, l, x_src):
    a = ATT[l]
    G, D, R = a["g"], a["d"], len(a["pairs"])
    GD = G * D
    q_stack, k_stack, v_blocks = mem.q_stack[l], mem.k_stack[l], mem.v_blocks[l]
    wq = mem.wq0 if l == 0 else mem.named["wqT"]
    wk = mem.wk0 if l == 0 else mem.named["wkT"]
    wv = mem.wv0 if l == 0 else mem.named["wvT"]
    with ExitStack() as c:
        def sb(n, s, t):
            return c.enter_context(nc.sbuf_tensor(f"{n}_a{l}", s, t))

        def sem(n):
            return mem.sem(f"a{l}_{n}")
        x4 = sb("x4", [P, QB, C], F32)
        stats = sb("stats", [P, QB, 6], F32)
        mv = sb("mv", [P, QB, 2], F32)
        rstd = sb("rstd", [P, QB], F32)
        mark = sb("mark", [P, 1], F32)
        half = sb("half", [P, QB], F32)
        xn = sb("xn", [P, QB, C], F32)
        hT = sb("hT", [P, CC, S], F32)
        full = sb("full", [P, 3, S], F32)
        rest = sb("rest", [P, 3, S], F32)
        parts = sb("parts", [P, 3, 3, S], BF16)
        vs = sb("vs", [P, QB, G, VW], F32)
        ps_t = c.enter_context(nc.psum_tensor(f"ps_t_a{l}", [P, CC, 512], F32))
        ps_q = c.enter_context(nc.psum_tensor(f"ps_q_a{l}", [P, 3, 512], F32))
        ps_v = c.enter_context(nc.psum_tensor(f"ps_v_a{l}", [P, 512], F32))
        if l == 1:
            elu = sb("elu", [P, CC, S], F32)
            low = sb("low", [P, CC, S], F32)
            rden = sb("rden", [P, QB, 2], F32)
            amem = sb("amem", [P, QB, C], F32)
            ps_m = c.enter_context(nc.psum_tensor(f"ps_m_a{l}", [P, 2, 2, 256], F32))
        x_in, var_ok, rstd_ok, xn_ok, turned, h_ok = (sem(n) for n in ("x_in", "var", "rstd", "xn", "turned", "h"))
        proj, q_full, part1, rest1, part2, part3 = (sem(n) for n in ("proj", "full", "p1", "r1", "p2", "p3"))
        v_ok, stored, own, low_ok, exp_ok, elu_ok, mem_ps, mem_ok, vset, st2 = (
            sem(n) for n in ("v", "stored", "own", "low", "exp", "elu", "memps", "mem", "vset", "pst"))
        NST = (4 + 1) * R + 1 + l
        prime(nc, [xn_ok, turned, proj, stored, part3,
                   elu_ok, h_ok, q_full, v_ok, mem_ok])
        block = c.enter_context(nc.Block())

        @block.sync
        def _(sp):
            with nc.sync.Fori(0, B) as b:
                sp.wait_ge(xn_ok, b * QB + 1)
                sp.dma_start(x4[:, :, :], x_src[bass.ds(b, 1), :, :].rearrange("a (i p) c -> (a p) i c", p=P)).then_inc(x_in, 16)

        @block.gpsimd
        def _(pool):
            nc.gpsimd.memset(half[:, :], -0.5).then_inc(st2, 1)
            pool.wait_ge(st2, 1)
            with nc.gpsimd.Fori(0, B) as b:
                pool.wait_ge(var_ok, b + 1)
                nc.gpsimd.tensor_tensor(rstd[:, :], mv[:, :, 1], half[:, :], ALU.pow).then_inc(rstd_ok, 1)

        @block.vector
        def _(v):
            V = nc.vector
            V.memset(vs[:, :, :, :], 0.0).then_inc(vset, 1)
            v.wait_ge(vset, 1)
            V.memset(vs[:, :, :, D:D + 1], 1.0).then_inc(vset, 1)
            v.wait_ge(vset, 2)
            with V.Fori(0, B) as b:
                do = Chain(v, own, b * (2 + l))
                v.wait_ge(x_in, b * 16 + 16)
                for i in range(QB):
                    last = V.bn_stats(stats[:, i, :], x4[:, i, :])
                do(last)
                V.memset(mark[:, :], 0.0)
                for i in range(QB):
                    last = V.bn_aggr(mv[:, i, :], stats[:, i, :])
                do(last)
                V.tensor_scalar(mv[:, :, 1], mv[:, :, 1], EPS, None, ALU.add).then_inc(var_ok, 1)
                v.wait_ge(rstd_ok, b + 1)
                v.wait_ge(turned, b * CC + 1)
                for i in range(QB):
                    V.tensor_scalar(xn[:, i, :], x4[:, i, :], mv[:, i, 0:1], rstd[:, i:i + 1],
                                    ALU.subtract, ALU.mult).then_inc(xn_ok, 1)
                v.wait_ge(proj, b * 4 + 1)
                for cc in range(CC):
                    v.wait_ge(turned, b * CC + cc + 2)
                    V.tensor_scalar(hT[:, cc, :], ps_t[:, cc, :], mem.modT[:, l, 2 + cc, bass.ds(b, 1)],
                                    mem.modT[:, l, 0 + cc, bass.ds(b, 1)], ALU.mult, ALU.add).then_inc(h_ok, 1)
                for m in range(3):
                    n = P if m < 2 else GD
                    v.wait_ge(part1, b * 3 + m + 1)
                    V.tensor_tensor(rest[0:n, m, :], full[0:n, m, :], parts[0:n, m, 0, :], ALU.subtract).then_inc(rest1, 1)
                v.wait_ge(proj, b * 4 + 4 + 1)
                v.wait_ge(stored, b * 16 * NST + 1)
                o = vs[:, :, :, 0:D]
                i = ps_v[:, 0:QB * GD].rearrange("p (i g d) -> p i g d", g=G, d=D)
                if l == 0:
                    for t in range(QB):
                        last = V.tensor_tensor(o[:, t], i[:, t], mem.bv0[:, :].rearrange("p (g d) -> p g d", d=D), ALU.add)
                else:
                    last = V.tensor_copy(o, i)
                last.then_inc(v_ok, 1)
                for m in range(3):
                    n = P if m < 2 else GD
                    v.wait_ge(part2, b * 3 + m + 1)
                    V.tensor_tensor(parts[0:n, m, 2, :], rest[0:n, m, :], parts[0:n, m, 1, :], ALU.subtract).then_inc(part3, 1)
                if l == 1:
                    V.tensor_scalar(low[:, :, :], full[:, 0:2, :], 0.0, None, ALU.min).then_inc(low_ok, 1)
                    v.wait_ge(exp_ok, b + 1)
                    do(V.scalar_tensor_tensor(out=elu[:, :, :], in0=full[:, 0:2, :], scalar=0.0, in1=low[:, :, :],
                                              op0=ALU.max, op1=ALU.add))
                    V.tensor_scalar(elu[:, :, :], elu[:, :, :], -1.0, None, ALU.add).then_inc(elu_ok, 1)
                    for m in range(CC):
                        v.wait_ge(mem_ps, b * CC + m + 1)
                        for h in range(2):
                            den = ps_m[:, :, :, :].rearrange("p a i n -> p (a i) n")[:, :, 65 * h + 64]
                            last = V.reciprocal(rden[:, :, h], den)
                        last.then_inc(mem_ok, 1)
                        v.wait_ge(mem_ok, b * 4 + 2 * m + 2)
                        for i in range(QB):
                            for h in range(2):
                                qn = 2 * m + h
                                last = V.scalar_tensor_tensor(
                                    out=amem[:, i, qn * 64:(qn + 1) * 64], in0=ps_m[:, i // 2, i % 2, 65 * h:65 * h + 64],
                                    scalar=mem.wmem[:, 0:1], in1=rden[:, i, h:h + 1].to_broadcast([P, 64]),
                                    op0=ALU.mult, op1=ALU.mult)
                        last.then_inc(mem_ok, 1)

        @block.scalar
        def _(s):
            with nc.scalar.Fori(0, B) as b:
                s.wait_ge(stored, b * 16 * NST + 1)
                s.wait_ge(part3, b * 3 + 1)
                s.wait_ge(elu_ok, b * l + 1)
                for m in range(3):
                    n = P if m < 2 else GD
                    s.wait_ge(proj, b * 4 + m + 2)
                    bias = (mem.bq0[:, m:m + 1] if m < 2 else mem.bk0[:, :]) if l == 0 else 0.0
                    if l == 0:
                        nc.scalar.activation(full[0:n, m, :], ps_q[0:n, m, :], ACT.Identity, bias=bias).then_inc(q_full, 1)
                    else:
                        nc.scalar.activation(full[0:n, m, :], ps_q[0:n, m, :], ACT.Copy).then_inc(q_full, 1)
                    s.wait_ge(q_full, b * 3 + m + 2)
                    nc.scalar.activation(parts[0:n, m, 0, :], full[0:n, m, :], ACT.Copy).then_inc(part1, 1)
                for m in range(3):
                    n = P if m < 2 else GD
                    s.wait_ge(rest1, b * 3 + m + 1)
                    nc.scalar.activation(parts[0:n, m, 1, :], rest[0:n, m, :], ACT.Copy).then_inc(part2, 1)
                if l == 1:
                    s.wait_ge(low_ok, b + 1)
                    nc.scalar.activation(low[:, :, :], low[:, :, :], ACT.Exp).then_inc(exp_ok, 1)
                s.wait_ge(part2, b * 3 + 3)
                s.wait_ge(part3, b * 3 + 3 + 1)
                s.wait_ge(v_ok, b + 2)
                for r, (qp, kp) in enumerate(a["pairs"]):
                    for m in range(CC):
                        for half_m in range(2):
                            n = 2 * m + half_m
                            dst = q_stack[bass.ds(b, 1), :, r * D:(r + 1) * D, :, :]
                            if l == 0:
                                dst = dst[:, n:n + 1].rearrange("b g d j s -> (b g j) d s")
                            else:
                                dst = dst[:, :, :, n:n + 1].rearrange("b g d j s -> (b j g) d s")
                            s.dma_start(dst, parts[64 * half_m:64 * half_m + 64, m, qp, :]).then_inc(stored, 16)
                    s.dma_start(k_stack[bass.ds(b, 1), :, r * D:(r + 1) * D, :].rearrange("b g d s -> (b g) d s"),
                                parts[0:GD, 2, kp, :]).then_inc(stored, 16)
                s.dma_start(v_blocks[bass.ds(b, 1)].rearrange("b g p i w -> (b p) i g w"), vs[:, :, :, :]).then_inc(stored, 16)
                if l == 1:
                    s.wait_ge(mem_ok, b * 4 + 4 + 1)
                    s.dma_start(mem.amem_d[bass.ds(b, 1)].rearrange("b (i p) c -> (b p) i c", p=P), amem[:, :, :]).then_inc(stored, 16)
            s.wait_ge(stored, B * 16 * NST + 1)

        @block.tensor
        def _(t):
            with nc.tensor.Fori(0, B) as b:
                t.wait_ge(xn_ok, b * QB + QB + 1)
                t.wait_ge(h_ok, b * CC + 1)
                for cc in range(CC):
                    for i in range(QB):
                        last = nc.tensor.transpose(ps_t[:, cc, i * P:(i + 1) * P], xn[:, i, cc * P:(cc + 1) * P], mem.ident[:, :])
                    last.then_inc(turned, 1)
                t.wait_ge(h_ok, b * CC + CC + 1)
                t.wait_ge(q_full, b * 3 + 1)
                t.wait_ge(v_ok, b + 1)
                for m in range(3):
                    n = P if m < 2 else GD
                    w = wq[:, :, m * P:(m + 1) * P] if m < 2 else wk[:, :, :]
                    for cc in range(CC):
                        last = nc.tensor.matmul(ps_q[0:n, m, :], w[:, cc, :], hT[:, cc, :], start=(cc == 0), stop=(cc == CC - 1))
                    last.then_inc(proj, 1)
                for i in range(QB):
                    for cc in range(CC):
                        last = nc.tensor.matmul(ps_v[:, i * GD:(i + 1) * GD], hT[:, cc, i * P:(i + 1) * P], wv[:, cc, :],
                                                start=(cc == 0), stop=(cc == CC - 1))
                last.then_inc(proj, 1)
                if l == 1:
                    t.wait_ge(elu_ok, b + 2)
                    for m in range(CC):
                        t.wait_ge(mem_ok, b * 4 + 2 * m + 1)
                        for i in range(QB):
                            last = nc.tensor.matmul(ps_m[:, i // 2, i % 2, 0:130], elu[:, m, i * P:(i + 1) * P],
                                                    mem.memr[:, :, :].rearrange("p a n -> p (a n)"), start=True, stop=True)
                        last.then_inc(mem_ps, 1)


def attention(nc, mem, l):
    a = ATT[l]
    G, D, R, causal, scale = a["g"], a["d"], len(a["pairs"]), a["causal"], a["scale"]
    RD, U, NI = R * D, B * G, B * G // NBUF
    q_stack = mem.q_stack[l].rearrange("b g r j s -> (b g) r (j s)")
    k_stack = mem.k_stack[l].rearrange("b g r s -> (b g) r s")
    v_blocks = mem.v_blocks[l].rearrange("b g p i w -> (b g) p (i w)")
    out_d = mem.att_d[l].rearrange("b g p n -> (b g) p n")
    with ExitStack() as c:
        def sb(n, s, t):
            return c.enter_context(nc.sbuf_tensor(f"{n}_b{l}", s, t))

        def sem(n):
            return mem.sem(f"b{l}_{n}")
        qs = [sb(f"qs{k}", [P, 4, S], BF16) for k in range(NBUF)]
        ks = [sb(f"ks{k}", [P, S], BF16) for k in range(NBUF)]
        vb = [sb(f"vb{k}", [P, QB, VW], F32) for k in range(NBUF)]
        pt = sb("pt", [P, 2, 4, S], F32)
        negmax = sb("negmax", [P, 2, 4, QB], F32)
        mparts = sb("mparts", [16, 3, P], BF16)
        mrest = sb("mrest", [16, P], F32)
        oT = sb("oT", [P, S], F32)
        rsum = sb("rsum", [P, QB, 4], F32)
        o_out = sb("o_out", [P, 2, QB, 4, D], F32)
        st = c.enter_context(nc.psum_tensor(f"st_b{l}", [P, 4, 512], F32))
        mx = c.enter_context(nc.psum_tensor(f"mx_b{l}", [P, 2, 512], F32))
        pv = c.enter_context(nc.psum_tensor(f"pv_b{l}", [P, 512], F32))
        turn = c.enter_context(nc.psum_tensor(f"turn_b{l}", [P, 512], F32))
        ld = [sem(f"loaded{k}") for k in range(NBUF)]
        mrow = [sem(f"mrow{k}") for k in range(NBUF)]
        mx_done, reduced, st_done, exp_done, pv_done = (sem(n) for n in ("mx", "red", "st", "exp", "pv"))
        m_turned, m_ready, own, evac, o_turned, o_ready_pre, o_ready, init, cleared = (
            sem(n) for n in ("mT", "mready", "own", "evac", "oT", "rsum", "oready", "init", "cleared"))
        o_stored = [sem(f"ostored{k}") for k in range(2)]
        block = c.enter_context(nc.Block())

        def slots(engine, slot):
            for k in range(NBUF):
                slot(k, 0, k, True, False)
            with engine.Fori(1, NI - 1) as it:
                for k in range(NBUF):
                    slot(it * NBUF + k, it, k, False, False)
            for k in range(NBUF):
                slot(U - NBUF + k, NI - 1, k, False, True)

        def ahead(it, k, n):
            return (k + n) % NBUF, it + (k + n) // NBUF

        def cols(s):
            return (s * P if causal else 0, S)

        @block.sync
        def _(sp):
            def load(u, k):
                sp.dma_start(qs[k][0:RD, :, :].rearrange("r j s -> r (j s)"), q_stack[bass.ds(u, 1)].rearrange("u r n -> (u r) n")).then_inc(ld[k], 16)
                sp.dma_start(ks[k][0:RD, :], k_stack[bass.ds(u, 1)].rearrange("u r n -> (u r) n")).then_inc(ld[k], 16)
                sp.dma_start(vb[k][:, :, :].rearrange("p i w -> p (i w)"), v_blocks[bass.ds(u, 1)].rearrange("u r n -> (u r) n")).then_inc(ld[k], 16)

            def max_rows(k):
                for p in range(3):
                    sp.dma_start(qs[k][MROW + p:MROW + p + 1, :, :].rearrange("a j (i q) -> a (j i) q", q=P),
                                 mparts[:, p, :]).then_inc(mrow[k], 16)

            def store(u, k):
                sp.dma_start(out_d[bass.ds(u, 1)].rearrange("u p n -> (u p) n"),
                             o_out[:, k % 2].rearrange("p i j d -> p (i j d)")).then_inc(o_stored[k % 2], 16)

            sp.wait_ge(init, NBUF)
            for k in range(NBUF):
                load(k, k)
            sp.wait_ge(m_ready, 1)
            max_rows(0)

            def slot(u, it, k, first, last):
                k1, _ = ahead(it, k, 1)
                if not (last and k == NBUF - 1):
                    sp.wait_ge(m_ready, u + 2)
                    max_rows(k1)
                if not (first and k == 0):
                    sp.wait_ge(o_ready, u)
                    store(u - 1, (k - 1) % NBUF)
                if not last:
                    sp.wait_ge(pv_done, u * QB + QB)
                    load(u + NBUF, k)
            slots(nc.sync, slot)
            sp.wait_ge(o_ready, U)
            store(U - 1, NBUF - 1)
            for k in range(2):
                sp.wait_ge(o_stored[k], 8 * U)

        @block.gpsimd
        def _(pool):
            for k in range(NBUF):
                nc.gpsimd.memset(qs[k][:, :, :], 0.0).then_inc(cleared, 1)
                nc.gpsimd.memset(ks[k][:, :], 0.0).then_inc(cleared, 1)
            pool.wait_ge(cleared, 2 * NBUF)
            for k in range(NBUF):
                nc.gpsimd.memset(ks[k][96:128, :], 1.0).then_inc(init, 1)

        @block.scalar
        def _(sc):
            def slot(u, it, k, first, last):
                for s in range(QB):
                    g = u * QB + s
                    lo, hi = cols(s)
                    if not (first and k == 0 and s < 2):
                        sc.wait_ge(pv_done, g - 1)
                    for pair in range(2):
                        sc.wait_ge(st_done, g * 2 + pair + 1)
                        nc.scalar.activation(pt[:, s % 2, 2 * pair:2 * pair + 2, lo:hi], st[:, 2 * pair:2 * pair + 2, lo:hi],
                                             ACT.Exp, scale=scale).then_inc(exp_done, 1)
            slots(nc.scalar, slot)

        @block.vector
        def _(v):
            V = nc.vector

            def reduce_max(vu, k, s):
                w = (s + 1) * P if causal else S
                for j in range(4):
                    n = vu * 16 + s * 4 + j
                    v.wait_ge(mx_done, n + 1)
                    V.tensor_reduce(negmax[:, k % 2, j, s:s + 1], mx[:, j % 2, 0:w], axis=AX.X, op=ALU.max, negate=True).then_inc(reduced, 1)

            def split_max(u, it, k, never_sent):
                v.wait_ge(m_turned, u + 1)
                if not never_sent:
                    kp, ip = (k - 1) % NBUF, it - (1 if k == 0 else 0)
                    v.wait_ge(mrow[kp], ip * 48 + 48)
                do = Chain(v, own, u * 3)
                do(V.tensor_copy(mparts[:, 0, :], turn[0:16, 0:P]))
                do(V.tensor_tensor(mrest[:, :], turn[0:16, 0:P], mparts[:, 0, :], ALU.subtract))
                do(V.tensor_copy(mparts[:, 1, :], mrest[:, :]))
                V.tensor_tensor(mparts[:, 2, :], mrest[:, :], mparts[:, 1, :], ALU.subtract).then_inc(m_ready, 1)

            def evacuate(u):
                v.wait_ge(pv_done, u * QB + QB)
                V.tensor_copy(oT[:, :], pv[:, :]).then_inc(evac, 1)

            def finish(u, it, k, early):
                v.wait_ge(o_turned, u + 1)
                if not early:
                    v.wait_ge(o_stored[k % 2], it * 32 + 16 * (k // 2))
                t4 = turn[:, :].rearrange("p (i j w) -> p i j w", i=QB, w=VW)
                V.reciprocal(rsum[:, :, :], t4[:, :, :, D]).then_inc(o_ready_pre, 1)
                v.wait_ge(o_ready_pre, u + 1)
                V.tensor_tensor(o_out[:, k % 2], t4[:, :, :, 0:D],
                                rsum[:, :, :].unsqueeze(3).to_broadcast([P, QB, 4, D]), ALU.mult).then_inc(o_ready, 1)

            for vu in range(2):
                for s in range(QB):
                    reduce_max(vu, vu, s)
                if vu == 0:
                    split_max(0, 0, 0, True)

            def slot(u, it, k, first, last):
                k1, i1 = ahead(it, k, 1)
                k2, i2 = ahead(it, k, 2)
                for s in range(QB):
                    if s == 0 and not (first and k == 0):
                        evacuate(u - 1)
                    if not (last and k >= NBUF - 2):
                        reduce_max(u + 2, k2, s)
                    if s == 0 and not (last and k == NBUF - 1):
                        split_max(u + 1, i1, k1, False)
                    if s == 2 and not (first and k == 0):
                        finish(u - 1, it - (1 if k == 0 else 0), (k - 1) % NBUF, first and k < 3)
            slots(V, slot)
            evacuate(U - 1)
            finish(U - 1, NI - 1, NBUF - 1, False)

        @block.tensor
        def _(t):
            mm = nc.tensor.matmul

            def max_scores(vu, k, s, static):
                w = (s + 1) * P if causal else S
                for j in range(4):
                    n = vu * 16 + s * 4 + j
                    if not (static and n < 2):
                        t.wait_ge(reduced, n - 1)
                    last = mm(mx[:, j % 2, 0:w], qs[k][0:MROW, j, s * P:(s + 1) * P], ks[k][0:MROW, 0:w], start=True, stop=not causal)
                    if causal:
                        last = mm(mx[:, j % 2, s * P:w], mem.identb[:, :], mem.mask_q[:, :], start=False, stop=True)
                    last.then_inc(mx_done, 1)

            def key_scores(u, k, s, static):
                lo, hi = cols(s)
                g = u * QB + s
                for pair in range(2):
                    if not (static and g < 1):
                        t.wait_ge(exp_done, g * 2 + pair - 1)
                    for j in (2 * pair, 2 * pair + 1):
                        last = mm(st[:, j, lo:hi], ks[k][0:KROWS, s * P:(s + 1) * P], qs[k][0:KROWS, j, lo:hi], start=True, stop=not causal)
                        if causal:
                            last = mm(st[:, j, lo:lo + P], mem.identb[:, :], mem.mask_k[:, :], start=False, stop=True)
                    last.then_inc(st_done, 1)

            def values(u, k, s):
                lo, hi = cols(s)
                t.wait_ge(exp_done, u * 2 * QB + 2 * s + 2)
                for j in range(4):
                    last = mm(pv[32 * j:32 * j + VW, lo:hi], vb[k][:, s, :], pt[:, s % 2, j, lo:hi], start=(s == 0), stop=(s == QB - 1))
                last.then_inc(pv_done, 1)

            def turn_max(u, k):
                t.wait_ge(reduced, u * 16 + 16)
                nc.tensor.transpose(turn[0:16, 0:P], negmax[:, k % 2].rearrange("p j s -> p (j s)"), mem.ident[:, :]).then_inc(m_turned, 1)

            def turn_out(u):
                t.wait_ge(evac, u + 1)
                t.wait_ge(m_ready, u + 3) if not (isinstance(u, int) and u + 3 > U) else t.wait_ge(m_ready, U)
                for i in range(QB):
                    last = nc.tensor.transpose(turn[:, i * P:(i + 1) * P], oT[:, i * P:(i + 1) * P], mem.ident[:, :])
                last.then_inc(o_turned, 1)

            for vu in range(2):
                t.wait_ge(ld[vu], 48)
                for s in range(QB):
                    max_scores(vu, vu, s, True)
                if vu == 0:
                    turn_max(0, 0)
            t.wait_ge(mrow[0], 48)
            key_scores(0, 0, 0, True)

            def slot(u, it, k, first, last):
                k1, i1 = ahead(it, k, 1)
                k2, i2 = ahead(it, k, 2)
                for s in range(QB):
                    if not (last and k >= NBUF - 2):
                        if s == 0:
                            t.wait_ge(ld[k2], i2 * 48 + 48)
                        max_scores(u + 2, k2, s, False)
                    if s < QB - 1:
                        key_scores(u, k, s + 1, False)
                    elif not (last and k == NBUF - 1):
                        t.wait_ge(mrow[k1], i1 * 48 + 48)
                        key_scores(u + 1, k1, 0, False)
                    if s == 0 and not (first and k == 0):
                        t.wait_ge(evac, u)
                    values(u, k, s)
                    if s == 0 and not (last and k == NBUF - 1):
                        if not (first and k == 0):
                            t.wait_ge(o_ready, u - 1) if not (first and k == 1) else None
                        turn_max(u + 1, k1)
                    if s == 2 and not (first and k == 0):
                        turn_out(u - 1)
            slots(nc.tensor, slot)
            turn_out(U - 1)


def after_attention(nc, mem, l, x_src):
    G, D = ATT[l]["g"], ATT[l]["d"]
    E = MOE[l]["e"]
    HC = 4 if l == 0 else 2
    router = mem.named["gwT"] if l == 0 else mem.named["rwT"]
    with ExitStack() as c:
        def sb(n, s, t):
            return c.enter_context(nc.sbuf_tensor(f"{n}_c{l}", s, t))

        def sem(n):
            return mem.sem(f"c{l}_{n}")
        x4 = sb("x4", [P, QB, C], F32)
        att = sb("att", [P, G, QB, 4 * D], F32)
        amem = sb("amem", [P, QB, C], F32)
        gate = sb("gate", [P, C], F32)
        rows = sb("rows", [P, 3, C], F32)
        t4 = sb("t4", [P, QB, C], F32)
        x1 = sb("x1", [P, QB, C], F32)
        base = sb("base", [P, QB, C], F32)
        stats = sb("stats", [P, QB, 6], F32)
        mark = sb("mark", [P, 1], F32)
        mv = sb("mv", [P, QB, 2], F32)
        rstd = sb("rstd", [P, QB], F32)
        half = sb("half", [P, QB], F32)
        xn = sb("xn", [P, QB, C], F32)
        hrows = sb("hrows", [P, QB, C], F32)
        hT = sb("hT", [P, CC, S], F32)
        ex = sb("ex", [P, QB, E], F32)
        hid = sb("hid", [P, HC, S], F32)
        sig = sb("sig", [P, HC, S], F32)
        if l == 0:
            up = sb("up", [P, CC, 512], F32)
            down = sb("down", [P, 4, C], F32)
        else:
            up, down = mem.named["suT"], mem.named["sdT"]
        ps_t = c.enter_context(nc.psum_tensor(f"ps_t_c{l}", [P, CC, 512], F32))
        ps_l = c.enter_context(nc.psum_tensor(f"ps_l_c{l}", [P, 512], F32))
        ps_u = c.enter_context(nc.psum_tensor(f"ps_u_c{l}", [P, 4, 512], F32))
        (x_in, rows_in, w_in, own, x1_ok, var_ok, rstd_ok, xn_ok, turned, h_ok, hrow_ok, logit, ex_ok, score_ok,
         hid_ps, act_ok, hid_ok, down_ps, base_ok, h_st, base_st, init) = (
            sem(n) for n in ("x", "rows", "w", "own", "x1", "var", "rstd", "xn", "turned", "h", "hrow", "logit",
                             "ex", "score", "hidps", "act", "hid", "down", "base", "hst", "basest", "init"))
        NL = 3 + l
        K_OWN = 5 if l == 0 else 10
        prime(nc, [x1_ok, hrow_ok, base_ok, h_st, base_st, score_ok, hid_ok, act_ok, ex_ok])
        block = c.enter_context(nc.Block())

        @block.sync
        def _(sp):
            if l == 0:
                sp.dma_start(up[:, :, :], mem.A["L0_ffn_w_up_shared"].rearrange("(c p) n -> p c n", p=P)).then_inc(w_in, 16)
                sp.dma_start(down[:, :, :], mem.A["L0_ffn_w_down_shared"].rearrange("(c p) n -> p c n", p=P)).then_inc(w_in, 16)
            with nc.sync.Fori(0, B) as b:
                sp.wait_ge(x1_ok, b + 1)
                sp.dma_start(x4[:, :, :], x_src[bass.ds(b, 1)].rearrange("a (i p) c -> (a p) i c", p=P)).then_inc(x_in, 16)
                sp.dma_start(att[:, :, :, :], mem.att_d[l][bass.ds(b, 1)].rearrange("b g p n -> (b p) g n")).then_inc(x_in, 16)
                if l == 1:
                    sp.dma_start(amem[:, :, :], mem.amem_d[bass.ds(b, 1)].rearrange("a (i p) c -> (a p) i c", p=P)).then_inc(x_in, 16)
                sp.dma_start(gate[:, :], mem.mod_d[l, bass.ds(b, 1), 2 * C:3 * C].rearrange("b n -> (b n)").partition_broadcast(P)).then_inc(x_in, 16)
                sp.wait_ge(hrow_ok, b * 2 + 1)
                sp.wait_ge(base_ok, b + 1)
                sp.dma_start(rows[:, :, :].rearrange("p a n -> p (a n)"),
                             mem.mod_d[l, bass.ds(b, 1), 3 * C:6 * C].rearrange("b n -> (b n)").partition_broadcast(P)).then_inc(rows_in, 16)

        @block.gpsimd
        def _(pool):
            g = nc.gpsimd
            g.memset(half[:, :], -0.5).then_inc(init, 1)
            pool.wait_ge(init, 1)
            with g.Fori(0, B) as b:
                pool.wait_ge(var_ok, b + 1)
                g.tensor_tensor(rstd[:, :], mv[:, :, 1], half[:, :], ALU.pow).then_inc(rstd_ok, 1)
                pool.wait_ge(xn_ok, b * QB + QB)
                pool.wait_ge(rows_in, b * 16 + 16)
                pool.wait_ge(h_st, b * 16 + 1)
                g.tensor_tensor(hrows[:, :, :], xn[:, :, :], rows[:, 1, :].unsqueeze(1).to_broadcast([P, QB, C]), ALU.mult).then_inc(hrow_ok, 1)
                pool.wait_ge(hrow_ok, b * 2 + 1 + 1)
                g.tensor_tensor(hrows[:, :, :], hrows[:, :, :], rows[:, 0, :].unsqueeze(1).to_broadcast([P, QB, C]), ALU.add).then_inc(hrow_ok, 1)

        @block.vector
        def _(v):
            V = nc.vector
            with V.Fori(0, B) as b:
                do = Chain(v, own, b * K_OWN)
                v.wait_ge(base_ok, b + 1)
                v.wait_ge(x_in, (b + 1) * 16 * NL)
                if l == 0:
                    for i in range(QB):
                        last = V.tensor_tensor(t4[:, i, :].rearrange("p (g n) -> p g n", g=G), att[:, :, i, :],
                                               gate[:, :].rearrange("p (g n) -> p g n", g=G), ALU.mult)
                    do(last)
                else:
                    do(V.tensor_scalar(att[:, :, :, :], att[:, :, :, :], mem.wmem[:, 1:2], None, ALU.mult))
                    for i in range(QB):
                        last = V.tensor_tensor(t4[:, i, :].rearrange("p (j g d) -> p j g d", j=4, g=G),
                                               att[:, :, i, :].rearrange("p g (j d) -> p j g d", j=4),
                                               amem[:, i, :].rearrange("p (j g d) -> p j g d", j=4, g=G), ALU.add)
                    do(last)
                    do(V.tensor_tensor(t4[:, :, :], t4[:, :, :], gate[:, :].unsqueeze(1).to_broadcast([P, QB, C]), ALU.mult))
                V.tensor_tensor(x1[:, :, :], x4[:, :, :], t4[:, :, :], ALU.add).then_inc(x1_ok, 1)
                v.wait_ge(x1_ok, b + 2)
                for i in range(QB):
                    last = V.bn_stats(stats[:, i, :], x1[:, i, :])
                do(last)
                V.memset(mark[:, :], 0.0)
                for i in range(QB):
                    last = V.bn_aggr(mv[:, i, :], stats[:, i, :])
                do(last)
                V.tensor_scalar(mv[:, :, 1], mv[:, :, 1], EPS, None, ALU.add).then_inc(var_ok, 1)
                v.wait_ge(rstd_ok, b + 1)
                v.wait_ge(hrow_ok, b * 2 + 1)
                for i in range(QB):
                    V.tensor_scalar(xn[:, i, :], x1[:, i, :], mv[:, i, 0:1], rstd[:, i:i + 1],
                                    ALU.subtract, ALU.mult).then_inc(xn_ok, 1)
                for cc in range(CC):
                    v.wait_ge(turned, b * CC + cc + 1)
                    V.tensor_scalar(hT[:, cc, :], ps_t[:, cc, :], mem.modT[:, l, 8 + cc, bass.ds(b, 1)],
                                    mem.modT[:, l, 6 + cc, bass.ds(b, 1)], ALU.mult, ALU.add).then_inc(h_ok, 1)
                v.wait_ge(ex_ok, b + 2)
                do(V.tensor_scalar(ex[:, :, :], ex[:, :, :], 1.0, None, ALU.add))
                V.reciprocal(mem.scores[:, bass.ds(b * QB, QB), 0:E], ex[:, :, :]).then_inc(score_ok, 1)
                if l == 0:
                    for h in range(HC):
                        v.wait_ge(act_ok, b * HC + h + 1 + 1)
                        V.tensor_tensor(hid[:, h, :], sig[:, h, :], sig[:, h, :], ALU.mult).then_inc(hid_ok, 1)
                else:
                    v.wait_ge(act_ok, b + 2)
                    do(V.tensor_scalar(sig[:, :, :], sig[:, :, :], 1.0, None, ALU.add))
                    do(V.reciprocal(sig[:, :, :], sig[:, :, :]))
                    do(V.tensor_tensor(hid[:, :, :], ps_u[:, 0:2, :], sig[:, :, :], ALU.mult))
                    V.tensor_tensor(hid[:, :, :], hid[:, :, :], ps_u[:, 2:4, :], ALU.mult).then_inc(hid_ok, 1)
                v.wait_ge(down_ps, b + 1)
                v.wait_ge(rows_in, b * 16 + 16)
                v.wait_ge(base_st, b * 16 + 1)
                do(V.tensor_tensor(t4[:, :, :], ps_t[:, :, :].rearrange("p a (i c) -> p (a i) c", c=C),
                                   rows[:, 2, :].unsqueeze(1).to_broadcast([P, QB, C]), ALU.mult))
                V.tensor_tensor(base[:, :, :], t4[:, :, :], x1[:, :, :], ALU.add).then_inc(base_ok, 1)
                assert do.n == K_OWN

        @block.scalar
        def _(s):
            A = nc.scalar.activation
            with nc.scalar.Fori(0, B) as b:
                s.wait_ge(logit, b + 1)
                s.wait_ge(score_ok, b + 1)
                A(ex[:, :, :], ps_l[:, 0:QB * E].rearrange("p (i e) -> p i e", e=E), ACT.Exp, scale=-1.0).then_inc(ex_ok, 1)
                if l == 0:
                    s.wait_ge(hid_ok, b * HC + 1)
                    for h in range(HC):
                        s.wait_ge(hid_ps, b * HC + h + 1)
                        A(sig[:, h, :], ps_u[:, h, :], ACT.Relu).then_inc(act_ok, 1)
                else:
                    s.wait_ge(hid_ok, b + 1)
                    s.wait_ge(hid_ps, b * HC + HC)
                    A(sig[:, :, :], ps_u[:, 0:2, :], ACT.Exp, scale=-1.0).then_inc(act_ok, 1)
                s.wait_ge(hrow_ok, b * 2 + 2 + 1)
                s.dma_start(mem.h_d[bass.ds(b, 1)].rearrange("b (i p) c -> (b p) i c", p=P), hrows[:, :, :]).then_inc(h_st, 16)
                s.wait_ge(base_ok, b + 2)
                s.dma_start(mem.base_d[bass.ds(b, 1)].rearrange("b (i p) c -> (b p) i c", p=P), base[:, :, :]).then_inc(base_st, 16)
            s.wait_ge(h_st, 16 * B + 1)
            s.wait_ge(base_st, 16 * B + 1)

        @block.tensor
        def _(t):
            mm = nc.tensor.matmul
            if l == 0:
                t.wait_ge(w_in, 32)
            with nc.tensor.Fori(0, B) as b:
                t.wait_ge(base_ok, b + 1)
                t.wait_ge(xn_ok, b * QB + QB)
                for cc in range(CC):
                    for i in range(QB):
                        last = nc.tensor.transpose(ps_t[:, cc, i * P:(i + 1) * P], xn[:, i, cc * P:(cc + 1) * P], mem.ident[:, :])
                    last.then_inc(turned, 1)
                t.wait_ge(h_ok, b * CC + CC)
                t.wait_ge(ex_ok, b + 1)
                for i in range(QB):
                    for cc in range(CC):
                        last = mm(ps_l[:, i * E:(i + 1) * E], hT[:, cc, i * P:(i + 1) * P], router[:, cc, :], start=(cc == 0), stop=(cc == CC - 1))
                last.then_inc(logit, 1)
                t.wait_ge(act_ok, (b * HC if l == 0 else b) + 1)
                t.wait_ge(hid_ok, (b * HC if l == 0 else b) + 1)
                for h in range(HC):
                    for part, w in ((0, up),) if l == 0 else ((0, mem.named["sgT"]), (2, up)):
                        for cc in range(CC):
                            last = mm(ps_u[:, part + h, :], w[:, cc, h * P:(h + 1) * P], hT[:, cc, :], start=(cc == 0), stop=(cc == CC - 1))
                    last.then_inc(hid_ps, 1)
                t.wait_ge(hid_ok, ((b + 1) * HC if l == 0 else b + 1) + 1)
                for i in range(QB):
                    for h in range(HC):
                        last = mm(ps_t[:, i // 2, (i % 2) * C:(i % 2) * C + C], hid[:, h, i * P:(i + 1) * P], down[:, h, :],
                                  start=(h == 0), stop=(h == HC - 1))
                last.then_inc(down_ps, 1)


def routing(nc, mem, l):
    m = MOE[l]
    E, N, K, GS = m["e"], m["n"], m["k"], m["e"] // m["n"]
    with ExitStack() as c:
        def sb(n, s, t=F32):
            return c.enter_context(nc.sbuf_tensor(f"{n}_d{l}", s, t))

        def sem(n):
            return mem.sem(f"d{l}_{n}")
        biased = sb("biased", [P, NT, E])
        hi = [sb(f"hi{k}", [P, NT * N, GS // 2]) for k in range(2)]
        lo = [sb(f"lo{k}", [P, NT * N, GS // 2]) for k in range(2)]
        gsum = sb("gsum", [P, NT, N])
        cmp = sb("cmp", [P, NT, N, N])
        eqs = sb("eqs", [P, NT, N, N])
        lower = sb("lower", [P, N, N])
        kept = sb("kept", [P, NT, N])
        kth = sb("kth", [P, NT, 8])
        sel = sb("sel", [P, NT, E])
        selb = sb("selb", [P, NT, E], BF16)
        scan = [sb(f"scan{k}", [P, NT, E]) for k in range(2)]
        w = sb("w", [P, NT, E])
        cnt = sb("cnt", [P, NT])
        ebase = sb("ebase", [P, 3, E])
        ebase_i = sb("ebase_i", [P, E], I32)
        tix = sb("tix", [P, 2])
        tcmp = sb("tcmp", [P, 2, E])
        eid = sb("eid", [P, 2])
        eid_i = sb("eid_i", [P, 2], I32)
        idx = sb("idx", [P, NT, 8])
        sidx = sb("sidx", [P, NT, 8], I32)
        skip = sb("skip", [P, NT, 8])
        NH = 4
        hb = sb("hb", [P, NH, C])
        ps_p = c.enter_context(nc.psum_tensor(f"ps_p_d{l}", [P, NT * E], F32))
        ps_n = c.enter_context(nc.psum_tensor(f"ps_n_d{l}", [P, NT * E], F32))
        own, init, picked, counted, listed, eid_ok, eid_st = (sem(n) for n in ("own", "init", "picked", "counted", "listed", "eid", "eidst"))
        h_in = [sem(f"h{k}") for k in range(NH)]
        sent = [sem(f"sent{k}") for k in range(NH)]
        block = c.enter_context(nc.Block())

        @block.gpsimd
        def _(pool):
            g = nc.gpsimd
            g.memset(lower[:, :, :], 1.0).then_inc(init, 1)
            pool.wait_ge(init, 1)
            g.affine_select(out=lower[:, :, :], in_=lower[:, :, :], compare_op=ALU.is_gt, fill=0.0, base=0,
                            pattern=[[1, N], [-1, N]], channel_multiplier=0).then_inc(init, 1)
            g.iota(tix[:, :], pattern=[[P, 2]], base=0, channel_multiplier=1, allow_small_or_imprecise_dtypes=True).then_inc(init, 1)
            g.iota(ebase[:, 0, :], pattern=[[m["cap"] or 0, E]], base=0, channel_multiplier=0, allow_small_or_imprecise_dtypes=True).then_inc(init, 1)
            pool.wait_ge(listed, 1)
            pool.wait_ge(mem.zeroed, mem.zero_count)
            for i in range(NT):
                pool.wait_ge(h_in[i % NH], 16 * (i // NH + 1))
                for k in range(K):
                    g.indirect_dma_start(out=mem.xs_d[0:SLOTS[l] + 1, :],
                                         out_offset=bass.IndirectOffsetOnAxis(ap=sidx[:, i, k:k + 1], axis=0),
                                         in_=hb[:, i % NH, :], in_offset=None,
                                         bounds_check=SLOTS[l], oob_is_err=False).then_inc(sent[i % NH], 16)
            for n in range(NH):
                pool.wait_ge(sent[n], 16 * K * (NT // NH))

        @block.sync
        def _(sp):
            hv = mem.h_d.rearrange("b (i p) c -> (b i) p c", p=P)
            for i in range(NT):
                if i >= NH:
                    sp.wait_ge(sent[i % NH], 16 * K * (i // NH))
                sp.dma_start(hb[:, i % NH, :], hv[i]).then_inc(h_in[i % NH], 16)
            if l == 0:
                sp.wait_ge(eid_ok, 1)
                sp.dma_start(mem.eid_d.rearrange("(h p) -> p h", p=P), eid_i[:, :], allow_slow_non_contiguous=True).then_inc(eid_st, 16)
                sp.wait_ge(eid_st, 16)

        @block.vector
        def _(v):
            V = nc.vector
            TT, TS = V.tensor_tensor, V.tensor_scalar
            do = Chain(v, own)
            sc = mem.scores[:, :, 0:E]
            do(TT(biased[:, :, :], sc, mem.gbias[l][:, :].unsqueeze(1).to_broadcast([P, NT, E]), ALU.add))
            grp = biased[:, :, :].rearrange("p t (n s) -> p (t n) s", n=N)
            h = GS // 2
            do(TT(hi[0][:, :, :], grp[:, :, 0:h], grp[:, :, h:], ALU.max))
            do(TT(lo[0][:, :, :], grp[:, :, 0:h], grp[:, :, h:], ALU.min))
            a = 0
            while h > 1:
                q = h // 2
                H, L = hi[a], lo[a]
                do(TT(hi[1 - a][:, :, 0:q], H[:, :, 0:q], H[:, :, q:h], ALU.max))
                do(TT(lo[1 - a][:, :, 0:q], H[:, :, 0:q], H[:, :, q:h], ALU.min))
                do(TT(L[:, :, 0:q], L[:, :, 0:q], L[:, :, q:h], ALU.max))
                do(TT(lo[1 - a][:, :, 0:q], lo[1 - a][:, :, 0:q], L[:, :, 0:q], ALU.max))
                h, a = q, 1 - a
            gs = gsum[:, :, :]
            do(TT(gs.rearrange("p t n -> p (t n)"), hi[a][:, :, 0], lo[a][:, :, 0], ALU.add))
            v.wait_ge(init, 4)
            other, this = gs.unsqueeze(2).to_broadcast([P, NT, N, N]), gs.unsqueeze(3).to_broadcast([P, NT, N, N])
            do(TT(cmp[:, :, :, :], other, this, ALU.is_gt))
            do(TT(eqs[:, :, :, :], other, this, ALU.is_equal))
            do(TT(eqs[:, :, :, :], eqs[:, :, :, :], lower[:, :, :].unsqueeze(1).to_broadcast([P, NT, N, N]), ALU.mult))
            do(TT(cmp[:, :, :, :], cmp[:, :, :, :], eqs[:, :, :, :], ALU.add))
            do(V.tensor_reduce(kept[:, :, :], cmp[:, :, :, :], axis=AX.X, op=ALU.add))
            do(TS(kept[:, :, :], kept[:, :, :], float(m["kg"]), None, ALU.is_lt))
            kb = kept[:, :, :].rearrange("p t n -> p (t n)").unsqueeze(2).to_broadcast([P, NT * N, GS])
            if l == 0:
                do(TS(kept[:, :, :], kept[:, :, :], -1.0, 1.0e30, ALU.add, ALU.mult))
                do(TT(grp, grp, kb, ALU.add))
            else:
                do(TT(grp, grp, kb, ALU.mult))
                do(TS(grp, grp, 0.0, None, ALU.add))
            for i in range(NT):
                last = V.max(kth[:, i, :], biased[:, i, :])
            do(last)
            kv = kth[:, :, K - 1].unsqueeze(2).to_broadcast([P, NT, E])
            do(TT(sel[:, :, :], biased[:, :, :], kv, ALU.is_gt))
            do(TT(scan[0][:, :, :], biased[:, :, :], kv, ALU.is_equal))
            do(TT(w[:, :, :], biased[:, :, :], kv, ALU.is_equal))
            do(V.tensor_reduce(cnt[:, :], sel[:, :, :], axis=AX.X, op=ALU.add))
            a, sh = 0, 1
            while sh < E:
                do(V.tensor_copy(scan[1 - a][:, :, 0:sh], scan[a][:, :, 0:sh]))
                do(TT(scan[1 - a][:, :, sh:], scan[a][:, :, sh:], scan[a][:, :, 0:E - sh], ALU.add))
                a, sh = 1 - a, 2 * sh
            do(TT(scan[a][:, :, :], scan[a][:, :, :], cnt[:, :].unsqueeze(2).to_broadcast([P, NT, E]), ALU.add))
            do(TS(scan[a][:, :, :], scan[a][:, :, :], float(K), None, ALU.is_le))
            do(TT(w[:, :, :], w[:, :, :], scan[a][:, :, :], ALU.mult))
            do(TT(sel[:, :, :], sel[:, :, :], w[:, :, :], ALU.add))
            V.tensor_copy(selb[:, :, :], sel[:, :, :]).then_inc(picked, 1)
            do(TT(w[:, :, :], sc, sel[:, :, :], ALU.mult))
            do(V.tensor_reduce(cnt[:, :], w[:, :, :], axis=AX.X, op=ALU.add))
            do(TS(cnt[:, :], cnt[:, :], 1e-20, None, ALU.add))
            do(V.reciprocal(cnt[:, :], cnt[:, :]))
            do(TT(w[:, :, :], w[:, :, :], cnt[:, :].unsqueeze(2).to_broadcast([P, NT, E]), ALU.mult))
            do(TS(w[:, :, :], w[:, :, :], m["scale"], None, ALU.mult))
            v.wait_ge(counted, 2)
            tot = ps_n[:, :].rearrange("p (t e) -> p t e", e=E)
            do(V.tensor_copy(scan[0][:, :, :], tot))
            a, sh = 0, 1
            while sh < NT:
                do(V.tensor_copy(scan[1 - a][:, 0:sh, :], scan[a][:, 0:sh, :]))
                do(TT(scan[1 - a][:, sh:, :], scan[a][:, sh:, :], scan[a][:, 0:NT - sh, :], ALU.add))
                a, sh = 1 - a, 2 * sh
            slot, incl = scan[1 - a], scan[a]
            do(TT(slot[:, :, :], incl[:, :, :], tot, ALU.subtract))
            do(TT(slot[:, :, :], slot[:, :, :], ps_p[:, :].rearrange("p (t e) -> p t e", e=E), ALU.add))
            if l == 0:
                do(TS(ebase_i[:, :], incl[:, NT - 1, :], float(P - 1), None, ALU.add))
                do(TS(ebase_i[:, :], ebase_i[:, :], 7, None, ALU.arith_shift_right))
                do(V.tensor_copy(ebase[:, 0, :], ebase_i[:, :]))
                do(V.tensor_copy(ebase[:, 1, :], ebase[:, 0, :]))
                e, sh = 1, 1
                while sh < E:
                    do(V.tensor_copy(ebase[:, 3 - e, 0:sh], ebase[:, e, 0:sh]))
                    do(TT(ebase[:, 3 - e, sh:], ebase[:, e, sh:], ebase[:, e, 0:E - sh], ALU.add))
                    e, sh = 3 - e, 2 * sh
                for n in range(2):
                    last = TT(tcmp[:, n, :], ebase[:, e, :], tix[:, n:n + 1].to_broadcast([P, E]), ALU.is_le)
                do(last)
                do(V.tensor_reduce(eid[:, :], tcmp[:, :, :], axis=AX.X, op=ALU.add))
                do(TS(eid[:, :], eid[:, :], float(E - 1), None, ALU.min))
                V.tensor_copy(eid_i[:, :], eid[:, :]).then_inc(eid_ok, 1)
                do(TT(ebase[:, 0, :], ebase[:, e, :], ebase[:, 0, :], ALU.subtract))
                do(TS(ebase[:, 0, :], ebase[:, 0, :], float(P), None, ALU.mult))
            else:
                do(TS(incl[:, :, :], slot[:, :, :], float(m["cap"]), None, ALU.is_lt))
                do(TT(sel[:, :, :], sel[:, :, :], incl[:, :, :], ALU.mult))
                do(TT(w[:, :, :], w[:, :, :], incl[:, :, :], ALU.mult))
            do(TT(slot[:, :, :], slot[:, :, :], ebase[:, 0, :].unsqueeze(1).to_broadcast([P, NT, E]), ALU.add))
            do(TS(slot[:, :, :], slot[:, :, :], 1.0, None, ALU.add))
            do(TT(slot[:, :, :], slot[:, :, :], sel[:, :, :], ALU.mult))
            for i in range(NT):
                last = V.max(idx[:, i, :], slot[:, i, :])
            do(last)
            do(V.tensor_copy(mem.gidx[:, :, :], idx[:, :, :]))
            do(TS(skip[:, :, :], idx[:, :, :], 0.0, 1.0e6, ALU.is_equal, ALU.mult))
            do(TT(skip[:, :, :], skip[:, :, :], idx[:, :, :], ALU.add))
            V.tensor_copy(sidx[:, :, :], skip[:, :, :]).then_inc(listed, 1)
            for k in range(K):
                do(TT(incl[:, :, :], slot[:, :, :], idx[:, :, k].unsqueeze(2).to_broadcast([P, NT, E]), ALU.is_equal))
                do(TT(incl[:, :, :], incl[:, :, :], w[:, :, :], ALU.mult))
                do(V.tensor_reduce(mem.wk[:, :, k], incl[:, :, :], axis=AX.X, op=ALU.add))

        @block.tensor
        def _(t):
            t.wait_ge(picked, 1)
            flat = selb[:, :, :].rearrange("p t e -> p (t e)")
            for ps, left in ((ps_p, mem.before), (ps_n, mem.onesb)):
                for n in range(0, NT * E, 512):
                    last = nc.tensor.matmul(ps[:, n:n + 512], left[:, :], flat[:, n:n + 512], start=True, stop=True)
                last.then_inc(counted, 1)


def experts_any(nc, mem):
    TL, E = MOE[0]["tiles"], MOE[0]["e"]
    assert TL % 4 == 0
    with ExitStack() as c:
        def sb(n, s, t=F32):
            return c.enter_context(nc.sbuf_tensor(f"{n}_e0", s, t))

        def sem(n):
            return mem.sem(f"e0_{n}")
        w1 = sb("w1", [P, E, CC, P])
        w2 = sb("w2", [P, E, C])
        table = sb("table", [1, TL], I32)
        xin = sb("xin", [P, 4, C])
        xT = sb("xT", [P, 2, C])
        r = sb("r", [P, 2, P])
        aT = sb("aT", [P, 2, P])
        y = sb("y", [P, 4, C])
        ps_x = c.enter_context(nc.psum_tensor("ps_x_e0", [P, 2, 512], F32))
        ps_h = c.enter_context(nc.psum_tensor("ps_h_e0", [P, 2, 512], F32))
        ps_r = c.enter_context(nc.psum_tensor("ps_r_e0", [P, 2, 512], F32))
        ps_y = c.enter_context(nc.psum_tensor("ps_y_e0", [P, 2, 512], F32))
        x_in = [sem(f"x{k}") for k in range(4)]
        y_st = [sem(f"yst{k}") for k in range(4)]
        w_in, t_in, x_turned, xT_ok, h_ps, r_ok, r_turned, aT_ok, y_ps, y_ok = (
            sem(n) for n in ("w", "t", "xturn", "xT", "h", "r", "rturn", "aT", "yps", "y"))
        prime(nc, y_st + [y_ok])
        block = c.enter_context(nc.Block())
        xs = mem.xs_d[1:1 + TL * P, :].rearrange("(t p) c -> t p c", p=P)
        ys = mem.ys_d[1:1 + TL * P, :].rearrange("(t p) c -> t p c", p=P)
        w1_d = mem.A["L0_ffn_w1_experts"].rearrange("e (c p) i -> p e c i", p=P)
        w2_d = mem.A["L0_ffn_w2_experts"].rearrange("e i c -> i e c")

        def slots(engine, slot):
            for k in range(4):
                slot(k, 0, k)
            with engine.Fori(1, TL // 4) as it:
                for k in range(4):
                    slot(it * 4 + k, it, k)
            for k in range(3):
                slot(TL + k, TL // 4, k)

        def stage(s, lag):
            return not isinstance(s, int) or 0 <= s - lag < TL

        @block.sync
        def _(sp):
            sp.dma_start(table[:, :], mem.eid_d.rearrange("(a n) -> a n", a=1)).then_inc(t_in, 16)
            for e in range(0, E, 8):
                for cc in range(CC):
                    sp.dma_start(w1[:, e:e + 8, cc, :], w1_d[:, e:e + 8, cc, :]).then_inc(w_in, 16)
                sp.dma_start(w2[:, e:e + 8, :], w2_d[:, e:e + 8, :]).then_inc(w_in, 16)

            def load(t, k):
                sp.dma_start(xin[:, k, :], xs[bass.ds(t, 1)].rearrange("t p c -> (t p) c")).then_inc(x_in[k], 16)
            for t in range(3):
                load(t, t)

            def slot(s, it, k):
                if stage(s, 0) and (not isinstance(s, int) or s + 3 < TL):
                    if not (isinstance(s, int) and s < 1):
                        sp.wait_ge(x_turned, s)
                    load(s + 3, (k + 3) % 4)
                if stage(s, 3):
                    sp.wait_ge(y_ok, s - 2 + 1)
                    sp.dma_start(ys[bass.ds(s - 3, 1)].rearrange("t p c -> (t p) c"), y[:, (k - 3) % 4, :]).then_inc(y_st[(k - 3) % 4], 16)
            for k in range(4):
                slot(k, 0, k)
            with nc.sync.Fori(1, TL // 4 - 1) as it:
                for k in range(4):
                    slot(it * 4 + k, it, k)
            for k in range(7):
                slot(TL - 4 + k, TL // 4 - 1 + k // 4, k % 4)
            for k in range(4):
                sp.wait_ge(y_st[k], 16 * (TL // 4) + 1)

        @block.tensor
        def _(t):
            mm = nc.tensor.matmul
            t.wait_ge(t_in, 16)
            t.wait_ge(w_in, 16 * 3 * (E // 8))

            def slot(s, it, k):
                if stage(s, 3):
                    n = s - 3
                    e = nc.tensor.value_load(table[0:1, bass.ds(n, 1)], min_val=0, max_val=E - 1)
                    t.wait_ge(aT_ok, s - 2)
                    if not (isinstance(s, int) and n < 2):
                        t.wait_ge(y_ok, s - 4 + 1)
                    q = (k - 3) % 2
                    mm(ps_y[:, q, 0:C], aT[:, q, :], w2[:, bass.ds(e, 1), :].rearrange("p e c -> p (e c)"), start=True, stop=True).then_inc(y_ps, 1)
                if stage(s, 2):
                    q = (k - 2) % 2
                    t.wait_ge(r_ok, s - 1)
                    nc.tensor.transpose(ps_r[:, q, 0:P], r[:, q, :], mem.ident[:, :]).then_inc(r_turned, 1)
                if stage(s, 1):
                    e = nc.tensor.value_load(table[0:1, bass.ds(s - 1, 1)], min_val=0, max_val=E - 1)
                    q = (k - 1) % 2
                    t.wait_ge(xT_ok, s)
                    for cc in range(CC):
                        last = mm(ps_h[:, q, 0:P], xT[:, q, cc * P:(cc + 1) * P], w1[:, bass.ds(e, 1), cc, :].rearrange("p e c -> p (e c)"),
                                  start=(cc == 0), stop=(cc == CC - 1))
                    last.then_inc(h_ps, 1)
                if stage(s, 0):
                    t.wait_ge(x_in[k], it * 16 + 16)
                    for cc in range(CC):
                        last = nc.tensor.transpose(ps_x[:, k % 2, cc * P:(cc + 1) * P], xin[:, k, cc * P:(cc + 1) * P], mem.ident[:, :])
                    last.then_inc(x_turned, 1)
            slots(nc.tensor, slot)

        @block.vector
        def _(v):
            V = nc.vector

            def slot(s, it, k):
                if stage(s, 3):
                    v.wait_ge(y_ps, s - 2)
                    if not (isinstance(s, int) and s - 3 < 4):
                        v.wait_ge(y_st[(k - 3) % 4], (it - (1 if k < 3 else 0)) * 16 + 1)
                    V.tensor_copy(y[:, (k - 3) % 4, :], ps_y[:, (k - 3) % 2, 0:C]).then_inc(y_ok, 1)
                if stage(s, 0):
                    v.wait_ge(x_turned, s + 1)
                    if not (isinstance(s, int) and s < 2):
                        v.wait_ge(h_ps, s - 1)
                    V.tensor_copy(xT[:, k % 2, :], ps_x[:, k % 2, 0:C]).then_inc(xT_ok, 1)
            slots(V, slot)

        @block.scalar
        def _(a):
            def slot(s, it, k):
                if stage(s, 2):
                    q = (k - 2) % 2
                    a.wait_ge(r_turned, s - 1)
                    if not (isinstance(s, int) and s - 2 < 2):
                        a.wait_ge(y_ps, s - 3)
                    nc.scalar.activation(aT[:, q, :], ps_r[:, q, 0:P], ACT.Square).then_inc(aT_ok, 1)
                if stage(s, 1):
                    q = (k - 1) % 2
                    a.wait_ge(h_ps, s)
                    if not (isinstance(s, int) and s - 1 < 2):
                        a.wait_ge(r_turned, s - 2)
                    nc.scalar.activation(r[:, q, :], ps_h[:, q, 0:P], ACT.Relu).then_inc(r_ok, 1)
            slots(nc.scalar, slot)


def experts_capped(nc, mem):
    E, CAP = MOE[1]["e"], MOE[1]["cap"]
    R2 = CAP - P
    with ExitStack() as c:
        def sb(n, s, t=F32):
            return c.enter_context(nc.sbuf_tensor(f"{n}_e1", s, t))

        def sem(n):
            return mem.sem(f"e1_{n}")
        NB = 4
        wgu = sb("wgu", [P, NB, 2, CC, P])
        wd = sb("wd", [P, NB, C])
        xa = sb("xa", [P, NB, C])
        xb = sb("xb", [P, NB, C])
        xT = sb("xT", [P, 2, CC, CAP])
        sig = sb("sig", [P, CAP])
        gu = sb("gu", [P, CAP])
        aT = sb("aT", [P, 2, CAP])
        y = sb("y", [P, 2, 2, C])
        ps_x = c.enter_context(nc.psum_tensor("ps_x_e1", [P, 2, 512], F32))
        ps_g = c.enter_context(nc.psum_tensor("ps_g_e1", [P, 2, 512], F32))
        ps_y = c.enter_context(nc.psum_tensor("ps_y_e1", [P, 2, 512], F32))
        ld = [sem(f"ld{k}") for k in range(NB)]
        y_st = [sem(f"yst{k}") for k in range(2)]
        own, x_turned, xT_ok, g_ps, sig_ok, a_ok, y_ps, y_ok = (sem(n) for n in ("own", "xturn", "xT", "g", "sig", "a", "yps", "y"))
        block = c.enter_context(nc.Block())
        xs = mem.xs_d[1:1 + E * CAP, :].rearrange("(e r) c -> e r c", r=CAP)
        ys = mem.ys_d[1:1 + E * CAP, :].rearrange("(e r) c -> e r c", r=CAP)
        A = mem.A

        def slots(engine, slot, lead=0):
            for k in range(4):
                slot(k, 0, k)
            with engine.Fori(1, E // 4 - 1) as it:
                for k in range(4):
                    slot(it * 4 + k, it, k)
            for k in range(6):
                slot(E - 4 + k, E // 4 - 1 + k // 4, k % 4)

        def stage(s, lag):
            return not isinstance(s, int) or 0 <= s - lag < E

        @block.sync
        def _(sp):
            def load(e, k):
                for n, w in ((0, "gate"), (1, "up")):
                    sp.dma_start(wgu[:, k, n, :, :], A[f"L1_ffn_W_{w}"][bass.ds(e, 1)].rearrange("e (c p) i -> (e p) c i", p=P)).then_inc(ld[k], 16)
                sp.dma_start(wd[:, k, :], A["L1_ffn_W_down"][bass.ds(e, 1)].rearrange("e i c -> (e i) c")).then_inc(ld[k], 16)
                sp.dma_start(xa[:, k, :], xs[bass.ds(e, 1), 0:P].rearrange("e r c -> (e r) c")).then_inc(ld[k], 16)
                sp.dma_start(xb[0:R2, k, :], xs[bass.ds(e, 1), P:CAP].rearrange("e r c -> (e r) c")).then_inc(ld[k], 16)
            for e in range(2):
                load(e, e)

            def slot(s, it, k):
                if not isinstance(s, int) or s + 2 < E:
                    if not (isinstance(s, int) and s < 2):
                        sp.wait_ge(y_ps, s - 1)
                    load(s + 2, (k + 2) % 4)
            slots(nc.sync, slot)

        @block.tensor
        def _(t):
            mm = nc.tensor.matmul

            def slot(s, it, k):
                if stage(s, 2):
                    q, b = k % 2, (k - 2) % 4
                    t.wait_ge(a_ok, s - 1)
                    if not (isinstance(s, int) and s - 2 < 2):
                        t.wait_ge(y_ok, s - 3)
                    mm(ps_y[:, q, 0:C], aT[:, q, 0:P], wd[:, b, :], start=True, stop=True)
                    mm(ps_y[0:R2, q, C:2 * C], aT[:, q, P:CAP], wd[:, b, :], start=True, stop=True, skip_group_check=True).then_inc(y_ps, 1)
                if stage(s, 1):
                    q, b = (k - 1) % 2, (k - 1) % 4
                    t.wait_ge(xT_ok, s)
                    for n in range(2):
                        for cc in range(CC):
                            last = mm(ps_g[:, q, n * CAP:(n + 1) * CAP], wgu[:, b, n, cc, :], xT[:, q, cc, :], start=(cc == 0), stop=(cc == CC - 1))
                    last.then_inc(g_ps, 1)
                if stage(s, 0):
                    q = k % 2
                    t.wait_ge(ld[k], it * 80 + 80)
                    for cc in range(CC):
                        nc.tensor.transpose(ps_x[:, q, cc * CAP:cc * CAP + P], xa[:, k, cc * P:(cc + 1) * P], mem.ident[:, :])
                        last = nc.tensor.transpose(ps_x[:, q, cc * CAP + P:(cc + 1) * CAP], xb[0:R2, k, cc * P:(cc + 1) * P], mem.ident[0:R2, 0:R2])
                    last.then_inc(x_turned, 1)
            slots(nc.tensor, slot)

        @block.vector
        def _(v):
            V = nc.vector

            def slot(s, it, k):
                if stage(s, 0):
                    v.wait_ge(x_turned, s + 1)
                    if not (isinstance(s, int) and s < 2):
                        v.wait_ge(g_ps, s - 1)
                    V.tensor_copy(xT[:, k % 2, :, :], ps_x[:, k % 2, 0:CC * CAP].rearrange("p (c n) -> p c n", n=CAP)).then_inc(xT_ok, 1)
                if stage(s, 1):
                    q = (k - 1) % 2
                    n = s - 1
                    v.wait_ge(sig_ok, s)
                    do = Chain(v, own, n * 3)
                    do(V.tensor_scalar(sig[:, :], sig[:, :], 1.0, None, ALU.add))
                    do(V.reciprocal(sig[:, :], sig[:, :]))
                    do(V.tensor_tensor(gu[:, :], ps_g[:, q, 0:CAP], sig[:, :], ALU.mult))
                    if not (isinstance(s, int) and n < 2):
                        v.wait_ge(y_ps, s - 2)
                    V.tensor_tensor(aT[:, q, :], gu[:, :], ps_g[:, q, CAP:2 * CAP], ALU.mult).then_inc(a_ok, 1)
            slots(V, slot)

        @block.scalar
        def _(a):
            def slot(s, it, k):
                if stage(s, 2):
                    q = k % 2
                    a.wait_ge(y_ps, s - 1)
                    if not (isinstance(s, int) and s - 2 < 2):
                        a.wait_ge(y_st[q], (it * 2 + k // 2 - 1) * 32)
                    nc.scalar.activation(y[:, q, 0, :], ps_y[:, q, 0:C], ACT.Copy)
                    nc.scalar.activation(y[0:R2, q, 1, :], ps_y[0:R2, q, C:2 * C], ACT.Copy).then_inc(y_ok, 1)
                    a.wait_ge(y_ok, s - 1)
                    a.dma_start(ys[bass.ds(s - 2, 1), 0:P].rearrange("e r c -> (e r) c"), y[:, q, 0, :]).then_inc(y_st[q], 16)
                    a.dma_start(ys[bass.ds(s - 2, 1), P:CAP].rearrange("e r c -> (e r) c"), y[0:R2, q, 1, :]).then_inc(y_st[q], 16)
                if stage(s, 1):
                    q = (k - 1) % 2
                    a.wait_ge(g_ps, s)
                    if not (isinstance(s, int) and s - 1 < 1):
                        a.wait_ge(a_ok, s - 1)
                    nc.scalar.activation(sig[:, :], ps_g[:, q, 0:CAP], ACT.Exp, scale=-1.0).then_inc(sig_ok, 1)
            slots(nc.scalar, slot)
            for q in range(2):
                a.wait_ge(y_st[q], 32 * (E // 2))


def combine(nc, mem, l, dst):
    K = MOE[l]["k"]
    with ExitStack() as c:
        def sb(n, s, t=F32):
            return c.enter_context(nc.sbuf_tensor(f"{n}_f{l}", s, t))

        def sem(n):
            return mem.sem(f"f{l}_{n}")
        NB = 4
        yk = sb("yk", [P, NB, K, C])
        base = sb("base", [P, NB, C])
        gate = sb("gate", [P, B, C])
        acc2 = sb("acc", [P, 2, C])
        res = sb("res", [P, NB, C])
        got = [sem(f"got{k}") for k in range(NB)]
        ld = [sem(f"ld{k}") for k in range(NB)]
        st = [sem(f"st{k}") for k in range(NB)]
        own, done, gates = sem("own"), sem("done"), sem("gates")
        block = c.enter_context(nc.Block())
        src = mem.base_d.rearrange("b (i p) c -> (b i) p c", p=P)
        out = dst.rearrange("b (i p) c -> (b i) p c", p=P)

        @block.gpsimd
        def _(pool):
            for i in range(NT):
                if i >= NB:
                    pool.wait_ge(done, i - NB + 1)
                for k in range(K):
                    nc.gpsimd.indirect_dma_start(out=yk[:, i % NB, k, :], out_offset=None, in_=mem.ys_d[0:SLOTS[l] + 1, :],
                                                 in_offset=bass.IndirectOffsetOnAxis(ap=mem.gidx[:, i, k:k + 1], axis=0)).then_inc(got[i % NB], 16)

        @block.sync
        def _(sp):
            for b in range(B):
                sp.dma_start(gate[:, b, :], mem.mod_d[l, b, 5 * C:6 * C].partition_broadcast(P)).then_inc(gates, 16)
            for i in range(NT + 2):
                if i < NT:
                    if i >= NB:
                        sp.wait_ge(done, i - NB + 1)
                    sp.dma_start(base[:, i % NB, :], src[i]).then_inc(ld[i % NB], 16)
                if i >= 2:
                    n = i - 2
                    sp.wait_ge(done, n + 1)
                    sp.dma_start(out[n], res[:, n % NB, :]).then_inc(st[n % NB], 16)
            for k in range(NB):
                sp.wait_ge(st[k], 16 * (NT // NB))

        @block.vector
        def _(v):
            V = nc.vector
            do = Chain(v, own)
            v.wait_ge(gates, 16 * B)
            for i in range(NT):
                k4, acc = i % NB, acc2[:, i % 2]
                v.wait_ge(got[k4], 16 * K * (i // NB + 1))
                do(V.tensor_scalar(acc[:, :], yk[:, k4, 0, :], mem.wk[:, i, 0:1], None, ALU.mult))
                for k in range(1, K):
                    do(V.scalar_tensor_tensor(out=acc[:, :], in0=yk[:, k4, k, :], scalar=mem.wk[:, i, k:k + 1], in1=acc[:, :],
                                              op0=ALU.mult, op1=ALU.add))
                do(V.tensor_tensor(acc[:, :], acc[:, :], gate[:, i // QB, :], ALU.mult))
                v.wait_ge(ld[k4], 16 * (i // NB + 1))
                if i >= NB:
                    v.wait_ge(st[k4], 16 * (i // NB))
                V.tensor_tensor(res[:, k4, :], acc[:, :], base[:, k4, :], ALU.add).then_inc(done, 1)


def clear_slots(nc, mem):
    with ExitStack() as c:
        zero = c.enter_context(nc.sbuf_tensor("zero", [P, 16 * C], F32))
        cleared = mem.sem("z_cleared")
        block = c.enter_context(nc.Block())
        rows = 16 * P

        @block.vector
        def _(v):
            nc.vector.memset(zero[:, :], 0.0).then_inc(cleared, 1)

        @block.sync
        def _(sp):
            sp.wait_ge(cleared, 1)
            for n in range(SLOTS[0] // rows):
                sp.dma_start(mem.xs_d[1 + n * rows:1 + (n + 1) * rows, :].rearrange("(p r) c -> p (r c)", p=P), zero[:, :]).then_inc(mem.zeroed, 16)
            sp.dma_start(mem.xs_d[0:1, :], zero[0:1, 0:C]).then_inc(mem.zeroed, 16)
            sp.dma_start(mem.ys_d[0:1, :], zero[0:1, 0:C]).then_inc(mem.zeroed, 16)
            sp.wait_ge(mem.zeroed, mem.zero_count)


class Memory:
    def __init__(self, nc, ctx):
        self.nc, self.ctx, self.named, self.sems = nc, ctx, {}, []

    def sb(self, name, shape, dt):
        return self.ctx.enter_context(self.nc.sbuf_tensor(name, shape, dt))

    def sem(self, name):
        self.sems.append(self.nc.alloc_semaphore(name))
        return self.sems[-1]

    def clear_semaphores(self):
        self.nc.clear_and_free_semaphores(self.sems)
        self.nc.all_engine_barrier()
        self.sems = []

    def dram(self, name, shape, dt):
        return self.nc.dram_tensor(name, shape, dt, kind="Internal").ap()


def adaln_two_layers(nc, A, out):
    with ExitStack() as ctx:
        mem = Memory(nc, ctx)
        mem.A = A
        mem.q_stack = [mem.dram(f"q_stack{l}", [B, a["g"], len(a["pairs"]) * a["d"], 4, S], BF16) for l, a in enumerate(ATT)]
        mem.k_stack = [mem.dram(f"k_stack{l}", [B, a["g"], len(a["pairs"]) * a["d"], S], BF16) for l, a in enumerate(ATT)]
        mem.v_blocks = [mem.dram(f"v_blocks{l}", [B, a["g"], P, QB, VW], F32) for l, a in enumerate(ATT)]
        mem.att_d = [mem.dram(f"att_d{l}", [B, a["g"], P, QB * 4 * a["d"]], F32) for l, a in enumerate(ATT)]
        mem.amem_d = mem.dram("amem_d", [B, S, C], F32)
        mem.h_d = mem.dram("h_d", [B, S, C], F32)
        mem.base_d = mem.dram("base_d", [B, S, C], F32)
        mem.x2_d = mem.dram("x2_d", [B, S, C], F32)
        mem.xs_d = mem.dram("xs_d", [SLOTS[0] + 1, C], F32)
        mem.ys_d = mem.dram("ys_d", [SLOTS[0] + 1, C], F32)
        mem.eid_d = mem.dram("eid_d", [MOE[0]["tiles"]], I32)
        mem.scores = mem.sb("scores", [P, NT, 64], F32)
        mem.wk = mem.sb("wk", [P, NT, 8], F32)
        mem.gidx = mem.sb("gidx", [P, NT, 8], I32)
        mem.zeroed = ctx.enter_context(nc.semaphore("zeroed"))
        mem.zero_count = 16 * (SLOTS[0] // (16 * P) + 2)
        clear_slots(nc, mem)
        setup(nc, mem, A)
        x = A["L0_attn_x"]
        for l in range(2):
            projections(nc, mem, l, x)
            attention(nc, mem, l)
            after_attention(nc, mem, l, x)
            routing(nc, mem, l)
            if l == 0:
                experts_any(nc, mem)
            else:
                experts_capped(nc, mem)
            combine(nc, mem, l, mem.x2_d if l == 0 else out)
            x = mem.x2_d
            mem.clear_semaphores()


def kernel(**inputs):
    import numpy as _np
    import concourse.bacc as _bacc
    from concourse import mybir as _mybir
    from concourse.bass_utils import run_bass_kernel_spmd as _run

    nc = _bacc.Bacc("TRN2", target_bir_lowering=False, num_devices=1)
    arrays, A = {}, {}
    for name, value in inputs.items():
        a = _np.ascontiguousarray(value)
        arrays[f"in_{name}"] = a
        A[name] = nc.dram_tensor(f"in_{name}", a.shape, _mybir.dt.from_np(a.dtype), kind="ExternalInput").ap()
    out = nc.dram_tensor("out", [B, S, C], F32, kind="ExternalOutput").ap()
    adaln_two_layers(nc, A, out)
    r = _run(nc, [arrays], core_ids=[0])
    return r.results[0]["out"]
```

```python
from contextlib import ExitStack

import numpy as np
import concourse.bass as bass
from concourse import mybir

F32 = mybir.dt.float32
BF16 = mybir.dt.bfloat16
I32 = mybir.dt.int32
ALU = mybir.AluOpType
ACT = mybir.ActivationFunctionType
AX = mybir.AxisListType

P = 128
B, S, C = 8, 512, 256
T = B * S
NT = T // P
QB = S // P
CC = C // P
NEG = -1.0e30
EPS = 1e-5
VW = 32
MROW = 96
KROWS = MROW + 3
NBUF = 4

PAIRS6 = [(0, 0), (0, 1), (0, 2), (1, 0), (1, 1), (2, 0)]
PAIRS9 = [(q, k) for q in range(3) for k in range(3)]
Q_RUNS6, K_RUNS6 = [(0, 0, 1, 3), (1, 3, 1, 2), (2, 5, 1, 1)], [(0, 0, 3, 2), (0, 5, 1, 1), (1, 1, 3, 2), (2, 2, 1, 1)]
Q_RUNS9, K_RUNS9 = [(p, 3 * p, 1, 3) for p in range(3)], [(p, p, 3, 3) for p in range(3)]

ATT = [dict(g=4, d=16, pairs=PAIRS6, q_runs=Q_RUNS6, k_runs=K_RUNS6, causal=True, scale=0.25),
       dict(g=8, d=8, pairs=PAIRS9, q_runs=Q_RUNS9, k_runs=K_RUNS9, causal=False, scale=float(np.float32(1.0 / np.sqrt(np.float32(8)))))]
MOE = [dict(e=64, n=8, kg=4, k=6, scale=2.5, cap=None, tiles=T * 6 // P + 64),
       dict(e=32, n=8, kg=3, k=4, scale=2.5, cap=160, tiles=None)]
SLOTS = [MOE[0]["tiles"] * P, MOE[1]["e"] * MOE[1]["cap"]]


class Chain:

    def __init__(self, engine, sem, base=0):
        self.engine, self.sem, self.base, self.n = engine, sem, base, 0

    def __call__(self, instruction):
        self.n += 1
        instruction.then_inc(self.sem, 1)
        self.engine.wait_ge(self.sem, self.base + self.n)


def setup(nc, mem, A):
    sb, d = mem.sb, mem.dram
    mem.ident = sb("ident", [P, P], F32)
    mem.identb = sb("identb", [P, P], BF16)
    mem.mask_q = sb("mask_q", [P, P], BF16)
    mem.mask_k = sb("mask_k", [P, P], BF16)
    mem.before = sb("before", [P, P], BF16)
    mem.onesb = sb("onesb", [P, P], BF16)
    mem.modT = sb("modT", [P, 2, 6 * CC, B], F32)
    mem.wq0 = sb("wq0", [P, CC, C], F32)
    mem.wk0 = sb("wk0", [P, CC, 64], F32)
    mem.wv0 = sb("wv0", [P, CC, 64], F32)
    mem.bq0 = sb("bq0", [P, CC], F32)
    mem.bk0 = sb("bk0", [64, 1], F32)
    mem.bv0 = sb("bv0", [P, 64], F32)
    mem.gbias = [sb("gbias0", [P, 64], F32), sb("gbias1", [P, 32], F32)]
    mem.wmem = sb("wmem", [P, 2], F32)
    mem.memr = sb("memr", [P, CC, 4, 65], F32)
    turned = [("gwT", A["L0_ffn_gate_w"], 64), ("wqT", A["L1_attn_Wq"], 256), ("wkT", A["L1_attn_Wk"], 64),
              ("wvT", A["L1_attn_Wv"], 64), ("rwT", A["L1_ffn_router_w"], 32),
              ("sgT", A["L1_ffn_shared_gate"], 256), ("suT", A["L1_ffn_shared_up"], 256),
              ("sdT", A["L1_ffn_shared_down"], 256)]
    for name, _, rows in turned:
        mem.named[name] = sb(name, [P, CC, rows], F32)
    blocks = [(name, src, r, min(P, rows - r)) for name, src, rows in turned for r in range(0, rows, P)]
    NBK = len(blocks)
    mem.mod_d = d("mod_d", [2, B, 6 * C], F32)

    with ExitStack() as c:
        rows_in = c.enter_context(nc.sbuf_tensor("rows_in", [P, NBK, C], F32))
        c_in = c.enter_context(nc.sbuf_tensor("c_in", [B, 2, C], F32))
        c_e = c.enter_context(nc.sbuf_tensor("c_e", [B, 2, C], F32))
        cT = c.enter_context(nc.sbuf_tensor("cT", [P, 2 * CC, B], F32))
        wmod = c.enter_context(nc.sbuf_tensor("wmod", [P, 2, CC, 6 * C], F32))
        mod = c.enter_context(nc.sbuf_tensor("mod", [B, 2, 6 * C], F32))
        tmp = c.enter_context(nc.sbuf_tensor("tmp_s", [B, 2, 2 * C], F32))
        ps = c.enter_context(nc.psum_tensor("ps_s", [P, 2, 512], F32))
        psm = c.enter_context(nc.psum_tensor("psm_s", [P, 3, 512], F32))
        pst = c.enter_context(nc.psum_tensor("pst_s", [P, 512], F32))
        loaded = mem.sem("s_loaded")
        small = mem.sem("s_small")
        rows_ld = mem.sem("s_rows")
        wmod_ld = mem.sem("s_wmod")
        consts = mem.sem("s_consts")
        dve = mem.sem("s_dve")
        act = mem.sem("s_act")
        pe = mem.sem("s_pe")
        stored = mem.sem("s_stored")
        ready = mem.sem("s_ready")
        memw = mem.sem("s_memw")
        zero0 = mem.sem("s_zero0")
        block = c.enter_context(nc.Block())

        @block.sync
        def _(sp):
            for l in range(2):
                sp.dma_start(c_in[:, l, :], A[f"L{l}_c"]).then_inc(small, 16)
            for i, (_, src, r, n) in enumerate(blocks):
                sp.dma_start(rows_in[0:n, i, :], src[r:r + n, :]).then_inc(rows_ld, 16)
            for l in range(2):
                sp.dma_start(wmod[:, l, :, :], A[f"L{l}_wmod"].rearrange("(c p) n -> p c n", p=P)).then_inc(wmod_ld, 16)
            sp.wait_ge(ready, 1)
            sp.dma_start(mem.mod_d.rearrange("l b n -> b l n"), mod[:, :, :]).then_inc(stored, 16)
            sp.wait_ge(stored, 16)
            sp.wait_ge(loaded, 16 * (10 + 16 + 16))

        @block.gpsimd
        def _(pool):
            g = nc.gpsimd
            n = 0
            for t, v in ((mem.ident, 0.0), (mem.identb, 0.0), (mem.mask_q, 0.0), (mem.mask_k, 0.0),
                         (mem.before, 1.0), (mem.onesb, 1.0), (mem.memr, 0.0)):
                g.memset(t[:], v).then_inc(consts, 1)
                n += 1
            pool.wait_ge(consts, n)
            for t in (mem.ident, mem.identb):
                g.affine_select(out=t[:, :], in_=t[:, :], compare_op=ALU.not_equal, fill=1.0, base=0,
                                pattern=[[-1, P]], channel_multiplier=1).then_inc(consts, 1)
            g.affine_select(out=mem.mask_q[:, :], in_=mem.mask_q[:, :], compare_op=ALU.is_ge, fill=NEG, base=0,
                            pattern=[[-1, P]], channel_multiplier=1).then_inc(consts, 1)
            g.affine_select(out=mem.mask_k[:, :], in_=mem.mask_k[:, :], compare_op=ALU.is_ge, fill=NEG, base=0,
                            pattern=[[1, P]], channel_multiplier=-1).then_inc(consts, 1)
            g.affine_select(out=mem.before[:, :], in_=mem.before[:, :], compare_op=ALU.is_gt, fill=0.0, base=0,
                            pattern=[[1, P]], channel_multiplier=-1).then_inc(consts, 1)

        @block.scalar
        def _(s):
            q = s.dma_start
            q(mem.wq0[:, :, :].rearrange("p c (h d) -> p c h d", d=16)[:, 0], A["L0_attn_Wq"].rearrange("h (c p) d -> c p h d", p=P)[0]).then_inc(loaded, 16)
            q(mem.wq0[:, :, :].rearrange("p c (h d) -> p c h d", d=16)[:, 1], A["L0_attn_Wq"].rearrange("h (c p) d -> c p h d", p=P)[1]).then_inc(loaded, 16)
            for w, n in ((mem.wk0, "k"), (mem.wv0, "v")):
                for cc in range(CC):
                    q(w[:, :, :].rearrange("p c (h d) -> p c h d", d=16)[:, cc], A[f"L0_attn_W{n}"].rearrange("h (c p) d -> c p h d", p=P)[cc]).then_inc(loaded, 16)
            with nc.allow_non_contiguous_dma(reason="small"):
                for g in range(4):
                    for j in range(4):
                        q(mem.bq0[64 * (g % 2) + j:64 * (g % 2) + j + 61:4, g // 2:g // 2 + 1],
                          A["L0_attn_bq"][4 * g + j, :].rearrange("(d o) -> d o", o=1)).then_inc(loaded, 16)
                q(mem.bk0[:, :], A["L0_attn_bk"].rearrange("h d -> (h d)").rearrange("(p o) -> p o", o=1)).then_inc(loaded, 16)
            q(mem.bv0[:, :], A["L0_attn_bv"].rearrange("h d -> (h d)").partition_broadcast(P)).then_inc(loaded, 16)
            q(mem.gbias[0][:, :], A["L0_ffn_gate_bias"].partition_broadcast(P)).then_inc(loaded, 16)
            q(mem.gbias[1][:, :], A["L1_ffn_e_bias"].partition_broadcast(P)).then_inc(loaded, 16)
            q(mem.wmem[:, 0:1], A["L1_attn_memory_weight"].partition_broadcast(P)).then_inc(memw, 16)
            s.wait_ge(consts, 7)
            for cc in range(CC):
                for j in range(4):
                    q(mem.memr[j:j + 125:4, cc, j, 0:64], A["L1_attn_memory"][32 * cc:32 * cc + 32, :]).then_inc(loaded, 16)
                    q(mem.memr[j:j + 125:4, cc, j, 64:65], A["L1_attn_memory_norm"][32 * cc:32 * cc + 32, :]).then_inc(loaded, 16)
            s.wait_ge(small, 32)
            nc.scalar.activation(c_e[:, :, :], c_in[:, :, :], ACT.Exp, scale=-1.0).then_inc(act, 1)
            s.wait_ge(memw, 16)
            nc.scalar.activation(mem.wmem[:, 1:2], mem.wmem[:, 0:1], ACT.Exp, scale=-1.0).then_inc(act, 1)

        @block.vector
        def _(v):
            do = Chain(v, dve)
            V = nc.vector
            v.wait_ge(act, 2)
            do(V.tensor_scalar(c_e[:, :, :], c_e[:, :, :], 1.0, None, ALU.add))
            do(V.reciprocal(c_e[:, :, :], c_e[:, :, :]))
            do(V.tensor_tensor(c_in[:, :, :], c_in[:, :, :], c_e[:, :, :], ALU.mult))
            do(V.tensor_scalar(mem.wmem[:, 1:2], mem.wmem[:, 1:2], 1.0, None, ALU.add))
            do(V.reciprocal(mem.wmem[:, 0:1], mem.wmem[:, 1:2]))
            do(V.tensor_scalar(mem.wmem[:, 1:2], mem.wmem[:, 0:1], -1.0, 1.0, ALU.mult, ALU.add))
            v.wait_ge(pe, 1)
            do(V.tensor_copy(cT[:, :, :], pst[:, 0:2 * CC * B].rearrange("p (a b) -> p a b", b=B)))
            for l in range(2):
                v.wait_ge(pe, 2 + l)
                do(V.tensor_copy(mod[:, l, :], psm[0:B, :, :].rearrange("p a n -> p (a n)")))
            for l in range(2):
                for j in (2, 5):
                    g = mod[:, l, j * C:(j + 1) * C]
                    do(V.tensor_scalar(tmp[:, 0, 0:C], g, 0.0, 2.0, ALU.is_ge, ALU.mult))
                    do(V.tensor_scalar(tmp[:, 0, 0:C], tmp[:, 0, 0:C], -1.0, None, ALU.add))
                    do(V.tensor_scalar(tmp[:, 1, 0:C], g, -1.0, None, ALU.mult))
                    do(V.tensor_tensor(g, g, tmp[:, 1, 0:C], ALU.max))
                    do(V.tensor_scalar(g, g, 0.25, None, ALU.max))
                    do(V.tensor_tensor(g, g, tmp[:, 0, 0:C], ALU.mult))
                for j in (1, 4):
                    g = mod[:, l, j * C:(j + 1) * C]
                    do(V.tensor_scalar(g, g, 1.0, None, ALU.add))
            V.tensor_copy(tmp[:, 0, 0:1], tmp[:, 0, 1:2]).then_inc(ready, 1)
            v.wait_ge(pe, 4)
            do(V.tensor_copy(mem.modT[:, :, :, :], pst[:, 64:64 + 24 * B].rearrange("p (l a b) -> p l a b", l=2, b=B)))
            for i, (name, _, r, n) in enumerate(blocks):
                v.wait_ge(pe, 5 + i)
                do(V.tensor_copy(mem.named[name][:, :, r:r + n], ps[:, i % 2, 0:2 * P].rearrange("p (c t) -> p c t", t=P)[:, :, 0:n]))

        @block.tensor
        def _(t):
            t.wait_ge(consts, 12)
            t.wait_ge(dve, 6)
            for l in range(2):
                for cc in range(CC):
                    a = 2 * l + cc
                    last = nc.tensor.transpose(pst[:, a * B:(a + 1) * B], c_in[:, l, cc * P:(cc + 1) * P], mem.ident[0:B, 0:B])
            last.then_inc(pe, 1)
            t.wait_ge(dve, 7)
            t.wait_ge(wmod_ld, 32)
            for l in range(2):
                if l:
                    t.wait_ge(dve, 7 + l)
                for n in range(3):
                    for cc in range(CC):
                        last = nc.tensor.matmul(psm[0:B, n, :], cT[:, 2 * l + cc, :], wmod[:, l, cc, n * 512:(n + 1) * 512],
                                                start=(cc == 0), stop=(cc == CC - 1))
                last.then_inc(pe, 1)
            t.wait_ge(ready, 1)
            for l in range(2):
                for a in range(12):
                    o = 64 + (12 * l + a) * B
                    last = nc.tensor.transpose(pst[:, o:o + B], mod[:, l, a * P:(a + 1) * P], mem.ident[0:B, 0:B])
            last.then_inc(pe, 1)
            t.wait_ge(rows_ld, 16 * NBK)
            base = 9 + 2 * (2 * 6 + 2) + 1
            for i, (name, _, r, n) in enumerate(blocks):
                if i >= 2:
                    t.wait_ge(dve, base + i - 1)
                for cc in range(CC):
                    last = nc.tensor.transpose(ps[:, i % 2, cc * P:cc * P + n], rows_in[0:n, i, cc * P:(cc + 1) * P], mem.ident[0:n, 0:n])
                last.then_inc(pe, 1)


def prime(nc, sems):
    with nc.Block() as block:
        @block.gpsimd
        def _(pool):
            for sem in sems:
                nc.gpsimd.sem_inc(sem, 1)


def wait_after(engine, sem, count):
    if not isinstance(count, int) or count > 0:
        engine.wait_ge(sem, count)


def batches(engine, body):
    for k in range(2):
        body(k, 0, k, False)
    with engine.Fori(1, B // 2 - 1) as i:
        for k in range(2):
            body(i * 2 + k, i, k, False)
    for k in range(2):
        body(B - 2 + k, B // 2 - 1, k, k == 1)


def projections(nc, mem, l, x_src):
    a = ATT[l]
    G, D, R = a["g"], a["d"], len(a["pairs"])
    GD = G * D
    q_stack, k_stack, v_blocks = mem.q_stack[l], mem.k_stack[l], mem.v_blocks[l]
    wk = mem.wk0 if l == 0 else mem.named["wkT"]
    wv = mem.wv0 if l == 0 else mem.named["wvT"]
    with ExitStack() as c:
        def sb(n, s, t):
            return c.enter_context(nc.sbuf_tensor(f"{n}_a{l}", s, t))

        def sem(n):
            return mem.sem(f"a{l}_{n}")
        wq = sb("wq", [P, CC, C], F32)
        x4 = sb("x4", [P, 2, QB, C], F32)
        stats = sb("stats", [P, QB, 6], F32)
        mv = sb("mv", [P, QB, 2], F32)
        rstd = sb("rstd", [P, QB], F32)
        mark = sb("mark", [P, 1], F32)
        half = sb("half", [P, QB], F32)
        xn = sb("xn", [P, QB, C], F32)
        hT = sb("hT", [P, CC, S], F32)
        full = sb("full", [P, 3, S], F32)
        rest = sb("rest", [P, 3, S], F32)
        parts = sb("parts", [P, 2, 3, 3, S], BF16)
        vs = sb("vs", [P, 2, QB, G, VW], F32)
        ps_t = c.enter_context(nc.psum_tensor(f"ps_t_a{l}", [P, CC, 512], F32))
        ps_q = c.enter_context(nc.psum_tensor(f"ps_q_a{l}", [P, 3, 512], F32))
        ps_v = c.enter_context(nc.psum_tensor(f"ps_v_a{l}", [P, 512], F32))
        if l == 1:
            elu = sb("elu", [P, CC, S], F32)
            low = sb("low", [P, CC, S], F32)
            rden = sb("rden", [P, QB, 4], F32)
            amem = sb("amem", [P, 2, QB, C], F32)
            ps_m = c.enter_context(nc.psum_tensor(f"ps_m_a{l}", [P, 2, 512], F32))
        x_in = [sem(f"x{k}") for k in range(2)]
        stored = [sem(f"stored{k}") for k in range(2)]
        var_ok, rstd_ok, xn_ok, turned, h_ok = (sem(n) for n in ("var", "rstd", "xn", "turned", "h"))
        proj, q_full, part1, rest1, part2, part3 = (sem(n) for n in ("proj", "full", "p1", "r1", "p2", "p3"))
        wq_ok = sem("wq")
        v_ok, own, low_ok, exp_ok, elu_ok, mem_ps, mem_ok, vset, hset = (
            sem(n) for n in ("v", "own", "low", "exp", "elu", "memps", "mem", "vset", "half"))
        NST = CC * len(a["q_runs"]) + len(a["k_runs"]) + 1 + l
        block = c.enter_context(nc.Block())

        @block.sync
        def _(sp):
            def body(b, i, k, last):
                sp.wait_ge(v_ok, b + 1)
                sp.wait_ge(part3, b * 3 + 3)
                for p, r0, step, n in a["q_runs"]:
                    for m in range(CC):
                        dst = q_stack[r0:r0 + step * (n - 1) + 1:step, bass.ds(b, 1), m * P:(m + 1) * P].rearrange("r b q s -> (b q) r s")
                        sp.dma_start(dst, parts[:, k, m, p, :].unsqueeze(1).to_broadcast([P, n, S])).then_inc(stored[k], 16)
                for p, r0, step, n in a["k_runs"]:
                    dst = k_stack[r0:r0 + step * (n - 1) + 1:step, bass.ds(b, 1)].rearrange("r b q s -> (b q) r s")
                    sp.dma_start(dst, parts[0:GD, k, 2, p, :].unsqueeze(1).to_broadcast([GD, n, S])).then_inc(stored[k], 16)
                sp.dma_start(v_blocks[bass.ds(b, 1)].rearrange("b g p i w -> (b p) i g w"), vs[:, k]).then_inc(stored[k], 16)
                if l == 1:
                    sp.wait_ge(mem_ok, b * 4 + 4)
                    sp.dma_start(mem.amem_d[bass.ds(b, 1)].rearrange("b (i p) c -> (b p) i c", p=P), amem[:, k]).then_inc(stored[k], 16)
            batches(nc.sync, body)
            for k in range(2):
                sp.wait_ge(stored[k], B // 2 * 16 * NST)

        @block.gpsimd
        def _(pool):
            def load(b, k):
                nc.gpsimd.dma_start(x4[:, k], x_src[bass.ds(b, 1), :, :].rearrange("a (i p) c -> (a p) i c", p=P)).then_inc(x_in[k], 16)

            def root(b):
                pool.wait_ge(var_ok, b + 1)
                nc.gpsimd.tensor_tensor(rstd[:, :], mv[:, :, 1], half[:, :], ALU.pow).then_inc(rstd_ok, 1)
            load(0, 0)
            load(1, 1)
            nc.gpsimd.memset(half[:, :], -0.5).then_inc(hset, 1)
            pool.wait_ge(hset, 1)
            root(0)

            def body(b, i, k, last):
                if not (isinstance(b, int) and b + 2 >= B):
                    pool.wait_ge(xn_ok, b * QB + QB)
                    load(b + 2, k)
                if not last:
                    root(b + 1)
            batches(nc.gpsimd, body)

        @block.vector
        def _(v):
            V = nc.vector
            for k in range(2):
                V.memset(vs[:, k], 0.0).then_inc(vset, 1)
            v.wait_ge(vset, 2)
            for k in range(2):
                V.memset(vs[:, k, :, :, D:D + 1], 1.0).then_inc(vset, 1)
            v.wait_ge(vset, 4)

            for cc in range(CC):
                src = mem.wq0[:, cc].rearrange("p (g j d) -> p g j d", j=4, d=D) if l == 0 else \
                    mem.named["wqT"][:, cc].rearrange("p (j g d) -> p g j d", j=4, d=D)
                V.tensor_copy(wq[:, cc].rearrange("p (g d j) -> p g j d", j=4, d=D), src).then_inc(wq_ok, 1)

            def normalise(b, i, k, do):
                v.wait_ge(x_in[k], i * 16 + 16)
                for t in range(QB):
                    last = V.bn_stats(stats[:, t, :], x4[:, k, t, :])
                do(last)
                V.memset(mark[:, :], 0.0)
                for t in range(QB):
                    last = V.bn_aggr(mv[:, t, :], stats[:, t, :])
                do(last)
                V.tensor_scalar(mv[:, :, 1], mv[:, :, 1], EPS, None, ALU.add).then_inc(var_ok, 1)
                v.wait_ge(rstd_ok, b + 1)
                for t in range(QB):
                    V.tensor_scalar(xn[:, t, :], x4[:, k, t, :], mv[:, t, 0:1], rstd[:, t:t + 1],
                                    ALU.subtract, ALU.mult).then_inc(xn_ok, 1)
            normalise(0, 0, 0, Chain(v, own))

            def body(b, i, k, last):
                do = Chain(v, own, 2 + b * (2 + l))
                wait_after(v, proj, b * 4)
                for cc in range(CC):
                    v.wait_ge(turned, b * CC + cc + 1)
                    V.tensor_scalar(hT[:, cc, :], ps_t[:, cc, :], mem.modT[:, l, 2 + cc, bass.ds(b, 1)],
                                    mem.modT[:, l, 0 + cc, bass.ds(b, 1)], ALU.mult, ALU.add).then_inc(h_ok, 1)
                if not last:
                    normalise(b + 1, i + k, 1 - k, do)
                for m in range(3):
                    n = P if m < 2 else GD
                    v.wait_ge(part1, b * 3 + m + 1)
                    V.tensor_tensor(rest[0:n, m, :], full[0:n, m, :], parts[0:n, k, m, 0, :], ALU.subtract).then_inc(rest1, 1)
                v.wait_ge(proj, b * 4 + 4)
                wait_after(v, stored[k], i * 16 * NST)
                o = vs[:, k, :, :, 0:D]
                src = ps_v[:, 0:QB * GD].rearrange("p (i g d) -> p i g d", g=G, d=D)
                if l == 0:
                    for t in range(QB):
                        op = V.tensor_tensor(o[:, t], src[:, t], mem.bv0[:, :].rearrange("p (g d) -> p g d", d=D), ALU.add)
                else:
                    op = V.tensor_copy(o, src)
                op.then_inc(v_ok, 1)
                for m in range(3):
                    n = P if m < 2 else GD
                    v.wait_ge(part2, b * 3 + m + 1)
                    V.tensor_tensor(parts[0:n, k, m, 2, :], rest[0:n, m, :], parts[0:n, k, m, 1, :], ALU.subtract).then_inc(part3, 1)
                if l == 1:
                    V.tensor_scalar(low[:, :, :], full[:, 0:2, :], 0.0, None, ALU.min).then_inc(low_ok, 1)
                    v.wait_ge(exp_ok, b + 1)
                    do(V.scalar_tensor_tensor(out=elu[:, :, :], in0=full[:, 0:2, :], scalar=0.0, in1=low[:, :, :],
                                              op0=ALU.max, op1=ALU.add))
                    V.tensor_scalar(elu[:, :, :], elu[:, :, :], -1.0, None, ALU.add).then_inc(elu_ok, 1)
                    for h in range(2):
                        v.wait_ge(mem_ps, b * 2 + h + 1)
                        jn = ps_m[:, :, 0:4 * 65].rearrange("p t (j n) -> p t j n", n=65)
                        V.reciprocal(rden[:, 2 * h:2 * h + 2, :], jn[:, :, :, 64]).then_inc(mem_ok, 1)
                        v.wait_ge(mem_ok, b * 4 + 2 * h + 1)
                        for t in range(2):
                            op = V.scalar_tensor_tensor(
                                out=amem[:, k, 2 * h + t, :].rearrange("p (j n) -> p j n", n=64), in0=jn[:, t, :, 0:64],
                                scalar=mem.wmem[:, 0:1], in1=rden[:, 2 * h + t, :].unsqueeze(2).to_broadcast([P, 4, 64]),
                                op0=ALU.mult, op1=ALU.mult)
                        op.then_inc(mem_ok, 1)
            batches(V, body)

        @block.scalar
        def _(s):
            def body(b, i, k, last):
                wait_after(s, stored[k], i * 16 * NST)
                wait_after(s, rest1, b * 3)
                if l == 1:
                    wait_after(s, elu_ok, b)
                for m in range(3):
                    n = P if m < 2 else GD
                    s.wait_ge(proj, b * 4 + m + 1)
                    if l == 0:
                        nc.scalar.activation(full[0:n, m, :], ps_q[0:n, m, :], ACT.Identity,
                                             bias=mem.bq0[:, m:m + 1] if m < 2 else mem.bk0[:, :]).then_inc(q_full, 1)
                    else:
                        nc.scalar.activation(full[0:n, m, :], ps_q[0:n, m, :], ACT.Copy).then_inc(q_full, 1)
                    s.wait_ge(q_full, b * 3 + m + 1)
                    nc.scalar.activation(parts[0:n, k, m, 0, :], full[0:n, m, :], ACT.Copy).then_inc(part1, 1)
                for m in range(3):
                    n = P if m < 2 else GD
                    s.wait_ge(rest1, b * 3 + m + 1)
                    nc.scalar.activation(parts[0:n, k, m, 1, :], rest[0:n, m, :], ACT.Copy).then_inc(part2, 1)
                if l == 1:
                    s.wait_ge(low_ok, b + 1)
                    nc.scalar.activation(low[:, :, :], low[:, :, :], ACT.Exp).then_inc(exp_ok, 1)
            batches(nc.scalar, body)

        @block.tensor
        def _(t):
            def turn(b):
                t.wait_ge(xn_ok, b * QB + QB)
                for cc in range(CC):
                    for i in range(QB):
                        op = nc.tensor.transpose(ps_t[:, cc, i * P:(i + 1) * P], xn[:, i, cc * P:(cc + 1) * P], mem.ident[:, :])
                    op.then_inc(turned, 1)
            turn(0)
            t.wait_ge(wq_ok, CC)

            def body(b, i, k, last):
                t.wait_ge(h_ok, b * CC + CC)
                for m in range(3):
                    n = P if m < 2 else GD
                    wait_after(t, q_full, b * 3 - 2 + m)
                    for cc in range(CC):
                        w = wq[:, cc, m * P:(m + 1) * P] if m < 2 else wk[:, cc, :]
                        op = nc.tensor.matmul(ps_q[0:n, m, :], w, hT[:, cc, :], start=(cc == 0), stop=(cc == CC - 1))
                    op.then_inc(proj, 1)
                wait_after(t, v_ok, b)
                for j in range(QB):
                    for cc in range(CC):
                        op = nc.tensor.matmul(ps_v[:, j * GD:(j + 1) * GD], hT[:, cc, j * P:(j + 1) * P], wv[:, cc, :],
                                              start=(cc == 0), stop=(cc == CC - 1))
                op.then_inc(proj, 1)
                if not last:
                    turn(b + 1)
                if l == 1:
                    t.wait_ge(elu_ok, b + 1)
                    for h in range(2):
                        wait_after(t, mem_ok, b * 4 + 2 * h)
                        for j in range(2):
                            for cc in range(CC):
                                op = nc.tensor.matmul(ps_m[:, j, 0:260], elu[:, cc, (2 * h + j) * P:(2 * h + j + 1) * P],
                                                      mem.memr[:, cc].rearrange("p j n -> p (j n)"), start=(cc == 0), stop=(cc == CC - 1))
                        op.then_inc(mem_ps, 1)
            batches(nc.tensor, body)


def attention(nc, mem, l):
    a = ATT[l]
    G, D, R, causal, scale = a["g"], a["d"], len(a["pairs"]), a["causal"], a["scale"]
    RD, U, NI = R * D, B * G, B * G // NBUF
    q_stack = mem.q_stack[l].rearrange("r b (g d j) s -> r (b g) d (j s)", d=D, j=4)
    k_stack = mem.k_stack[l].rearrange("r b (g d) s -> r (b g) d s", d=D)
    v_blocks = mem.v_blocks[l].rearrange("b g p i w -> (b g) p (i w)")
    out_d = mem.att_d[l].rearrange("b g p n -> (b g) p n")
    with ExitStack() as c:
        def sb(n, s, t):
            return c.enter_context(nc.sbuf_tensor(f"{n}_b{l}", s, t))

        def sem(n):
            return mem.sem(f"b{l}_{n}")
        qs = [sb(f"qs{k}", [P, 4, S], BF16) for k in range(NBUF)]
        ks = [sb(f"ks{k}", [P, S], BF16) for k in range(NBUF)]
        vb = [sb(f"vb{k}", [P, QB, VW], F32) for k in range(NBUF)]
        pt = sb("pt", [P, 2, 4, S], F32)
        negmax = sb("negmax", [P, 2, 4, QB], F32)
        mparts = sb("mparts", [16, 3, P], BF16)
        mrest = sb("mrest", [16, P], F32)
        oT = sb("oT", [P, S], F32)
        rsum = sb("rsum", [P, QB, 4], F32)
        o_out = sb("o_out", [P, 2, QB, 4, D], F32)
        if l == 0:
            zero = sb("zero", [P, 16 * C], F32)
        st = c.enter_context(nc.psum_tensor(f"st_b{l}", [P, 4, 512], F32))
        side = c.enter_context(nc.psum_tensor(f"side_b{l}", [P, 3, 512], F32))
        pv = c.enter_context(nc.psum_tensor(f"pv_b{l}", [P, 512], F32))
        ld = [sem(f"loaded{k}") for k in range(NBUF)]
        mrow = [sem(f"mrow{k}") for k in range(NBUF)]
        mx_done, items, st_done, exp_done, pv_done = (sem(n) for n in ("mx", "items", "st", "exp", "pv"))
        m_turned, own, evac, o_turned, quotients, init, cleared = (
            sem(n) for n in ("mT", "own", "evac", "oT", "rsum", "init", "cleared"))
        ITEMS, TURN_MAX, TURN_OUT = 18, 4, 13

        def item(u, pos):
            return (u + 2) * ITEMS + pos

        def score_pos(s, j):
            return s * 4 + j + (1 if s > 0 else 0) + (1 if s > 2 else 0)
        o_stored = [sem(f"ostored{k}") for k in range(2)]
        block = c.enter_context(nc.Block())

        def slots(engine, slot):
            for k in range(NBUF):
                slot(k, 0, k, True, False)
            with engine.Fori(1, NI - 1) as it:
                for k in range(NBUF):
                    slot(it * NBUF + k, it, k, False, False)
            for k in range(NBUF):
                slot(U - NBUF + k, NI - 1, k, False, True)

        def ahead(it, k, n):
            return (k + n) % NBUF, it + (k + n) // NBUF

        def cols(s):
            return (s * P if causal else 0, S)

        @block.sync
        def _(sp):
            def load(u, k):
                sp.dma_start(qs[k][0:RD, :, :].rearrange("r j s -> r (j s)"), q_stack[:, bass.ds(u, 1)].rearrange("r u d n -> r (u d) n")).then_inc(ld[k], 16)
                sp.dma_start(ks[k][0:RD, :], k_stack[:, bass.ds(u, 1)].rearrange("r u d s -> r (u d) s")).then_inc(ld[k], 16)
                sp.dma_start(vb[k][:, :, :].rearrange("p i w -> p (i w)"), v_blocks[bass.ds(u, 1)].rearrange("u r n -> (u r) n")).then_inc(ld[k], 16)

            def max_rows(k):
                for p in range(3):
                    sp.dma_start(qs[k][MROW + p:MROW + p + 1, :, :].rearrange("a j (i q) -> a (j i) q", q=P),
                                 mparts[:, p, :]).then_inc(mrow[k], 16)

            def store(u, k):
                sp.dma_start(out_d[bass.ds(u, 1)].rearrange("u p n -> (u p) n"),
                             o_out[:, k % 2].rearrange("p i j d -> p (i j d)")).then_inc(o_stored[k % 2], 16)

            sp.wait_ge(init, NBUF)
            for k in range(NBUF):
                load(k, k)
            sp.wait_ge(items, item(-1, TURN_MAX) + 1)
            max_rows(0)

            def slot(u, it, k, first, last):
                k1, _ = ahead(it, k, 1)
                if not (last and k == NBUF - 1):
                    sp.wait_ge(items, item(u, TURN_MAX) + 1)
                    max_rows(k1)
                if not (first and k == 0):
                    sp.wait_ge(items, item(u, TURN_OUT) + 1)
                    store(u - 1, (k - 1) % NBUF)
                if not last:
                    sp.wait_ge(pv_done, u * QB + QB)
                    load(u + NBUF, k)
            slots(nc.sync, slot)
            sp.wait_ge(items, item(U, TURN_OUT) + 1)
            store(U - 1, NBUF - 1)
            for k in range(2):
                sp.wait_ge(o_stored[k], 8 * U)

        @block.gpsimd
        def _(pool):
            for k in range(NBUF):
                nc.gpsimd.memset(qs[k][:, :, :], 0.0).then_inc(cleared, 1)
                nc.gpsimd.memset(ks[k][:, :], 0.0).then_inc(cleared, 1)
            pool.wait_ge(cleared, 2 * NBUF)
            for k in range(NBUF):
                nc.gpsimd.memset(ks[k][96:128, :], 1.0).then_inc(init, 1)
            if l == 0:
                pool.wait_ge(init, NBUF)
                nc.gpsimd.memset(zero[:, :], 0.0).then_inc(cleared, 1)
                pool.wait_ge(cleared, 2 * NBUF + 1)
                for dst in (mem.xs_d, mem.ys_d):
                    nc.gpsimd.dma_start(dst[0:1, :], zero[0:1, 0:C]).then_inc(mem.zeroed, 16)
                rows = 16 * P
                for n in range(SLOTS[0] // rows):
                    pool.wait_ge(pv_done, (n + 1) * QB)
                    nc.gpsimd.dma_start(mem.xs_d[1 + n * rows:1 + (n + 1) * rows, :].rearrange("(p r) c -> p (r c)", p=P),
                                        zero[:, :]).then_inc(mem.zeroed, 16)
                pool.wait_ge(mem.zeroed, mem.zero_count)

        @block.scalar
        def _(sc):
            def evacuate(u, fresh):
                sc.wait_ge(pv_done, u * QB + QB)
                if not fresh:
                    sc.wait_ge(o_turned, u)
                nc.scalar.activation(oT[:, :], pv[:, :], ACT.Copy).then_inc(evac, 1)

            def slot(u, it, k, first, last):
                for s in range(QB):
                    g = u * QB + s
                    lo, hi = cols(s)
                    if not (first and k == 0 and s < 2):
                        sc.wait_ge(pv_done, g - 1)
                    for pair in range(2):
                        sc.wait_ge(st_done, g * 2 + pair + 1)
                        nc.scalar.activation(pt[:, s % 2, 2 * pair:2 * pair + 2, lo:hi], st[:, 2 * pair:2 * pair + 2, lo:hi],
                                             ACT.Exp, scale=scale).then_inc(exp_done, 1)
                    if s == 0 and not (first and k == 0):
                        evacuate(u - 1, first and k == 1)
            slots(nc.scalar, slot)
            evacuate(U - 1, False)

        @block.vector
        def _(v):
            V = nc.vector

            def reduce_max(vu, k, s, j):
                w = (s + 1) * P if causal else S
                v.wait_ge(mx_done, vu * 16 + s * 4 + j + 1)
                V.tensor_reduce(negmax[:, k % 2, j, s:s + 1], side[:, score_pos(s, j) % 3, 0:w],
                                axis=AX.X, op=ALU.max, negate=True).then_inc(items, 1)

            def split_max(u, it, k, fresh):
                m = side[0:16, TURN_MAX % 3, 0:P]
                v.wait_ge(m_turned, u + 1)
                if not fresh:
                    kp, ip = (k - 1) % NBUF, it - (1 if k == 0 else 0)
                    v.wait_ge(mrow[kp], ip * 48 + 48)
                do = Chain(v, own, u * 3)
                do(V.tensor_copy(mparts[:, 0, :], m))
                do(V.tensor_tensor(mrest[:, :], m, mparts[:, 0, :], ALU.subtract))
                do(V.tensor_copy(mparts[:, 1, :], mrest[:, :]))
                V.tensor_tensor(mparts[:, 2, :], mrest[:, :], mparts[:, 1, :], ALU.subtract).then_inc(items, 1)

            def finish(u, it, k, early):
                v.wait_ge(o_turned, u + 1)
                if not early:
                    v.wait_ge(o_stored[k % 2], it * 32 + 16 * (k // 2))
                t4 = side[:, TURN_OUT % 3, :].rearrange("p (i j w) -> p i j w", i=QB, w=VW)
                V.reciprocal(rsum[:, :, :], t4[:, :, :, D]).then_inc(quotients, 1)
                v.wait_ge(quotients, u + 1)
                V.tensor_tensor(o_out[:, k % 2], t4[:, :, :, 0:D],
                                rsum[:, :, :].unsqueeze(3).to_broadcast([P, QB, 4, D]), ALU.mult).then_inc(items, 1)

            def none(n, count=1):
                v.wait_ge(items, n)
                V.sem_inc(items, count)

            def slot(u, it, k, first, last, lead=False):
                k1, i1 = ahead(it, k, 1)
                k2, i2 = ahead(it, k, 2)
                for s in range(QB):
                    if not (last and k >= NBUF - 2):
                        for j in range(4):
                            reduce_max(u + 2, k2, s, j)
                    else:
                        none(item(u, score_pos(s, 0)), 4)
                    if s == 0:
                        if (lead and u == -2) or (last and k == NBUF - 1):
                            none(item(u, TURN_MAX))
                        else:
                            split_max(u + 1, 0 if lead else i1, 0 if lead else k1, lead)
                    if s == 2:
                        if lead or (first and k == 0):
                            none(item(u, TURN_OUT))
                        else:
                            finish(u - 1, it - (1 if k == 0 else 0), (k - 1) % NBUF, first and k < 3)
            for u in (-2, -1):
                slot(u, 0, u % NBUF, False, False, True)
            slots(V, slot)
            none(item(U, 0), TURN_OUT)
            finish(U - 1, NI - 1, NBUF - 1, False)

        @block.tensor
        def _(t):
            mm = nc.tensor.matmul

            def max_scores(vu, k, s, j, static):
                w = (s + 1) * P if causal else S
                n = item(vu - 2, score_pos(s, j))
                if not (static and n < 3):
                    t.wait_ge(items, n - 2)
                bank = score_pos(s, j) % 3
                last = mm(side[:, bank, 0:w], qs[k][0:MROW, j, s * P:(s + 1) * P], ks[k][0:MROW, 0:w], start=True, stop=not causal)
                if causal:
                    last = mm(side[:, bank, s * P:w], mem.identb[:, :], mem.mask_q[:, :], start=False, stop=True)
                last.then_inc(mx_done, 1)

            def key_scores(u, k, s, pair, static):
                lo, hi = cols(s)
                g = u * QB + s
                if not (static and g < 1):
                    t.wait_ge(exp_done, g * 2 + pair - 1)
                for j in (2 * pair, 2 * pair + 1):
                    last = mm(st[:, j, lo:hi], ks[k][0:KROWS, s * P:(s + 1) * P], qs[k][0:KROWS, j, lo:hi], start=True, stop=not causal)
                    if causal:
                        last = mm(st[:, j, lo:lo + P], mem.identb[:, :], mem.mask_k[:, :], start=False, stop=True)
                last.then_inc(st_done, 1)

            def values(u, k, s):
                lo, hi = cols(s)
                t.wait_ge(exp_done, u * 2 * QB + 2 * s + 2)
                for j in range(4):
                    last = mm(pv[32 * j:32 * j + VW, lo:hi], vb[k][:, s, :], pt[:, s % 2, j, lo:hi], start=(s == 0), stop=(s == QB - 1))
                last.then_inc(pv_done, 1)

            def turn_max(u, k):
                t.wait_ge(items, item(u - 1, TURN_MAX) - 2)
                nc.tensor.transpose(side[0:16, TURN_MAX % 3, 0:P], negmax[:, k % 2].rearrange("p j s -> p (j s)"),
                                    mem.ident[:, :]).then_inc(m_turned, 1)

            def turn_out(u):
                t.wait_ge(evac, u + 1)
                t.wait_ge(items, item(u + 1, TURN_OUT) - 2)
                for i in range(QB):
                    last = nc.tensor.transpose(side[:, TURN_OUT % 3, i * P:(i + 1) * P], oT[:, i * P:(i + 1) * P], mem.ident[:, :])
                last.then_inc(o_turned, 1)

            for vu in range(2):
                t.wait_ge(ld[vu], 48)
                for s in range(QB):
                    for j in range(4):
                        max_scores(vu, vu, s, j, True)
                    if vu == 1 and s == 0:
                        turn_max(0, 0)
            t.wait_ge(mrow[0], 48)
            for pair in range(2):
                key_scores(0, 0, 0, pair, True)

            def slot(u, it, k, first, last):
                k1, i1 = ahead(it, k, 1)
                k2, i2 = ahead(it, k, 2)
                ahead_max = not (last and k >= NBUF - 2)
                ahead_keys = not (last and k == NBUF - 1)
                for s in range(QB):
                    if ahead_max:
                        if s == 0:
                            t.wait_ge(ld[k2], i2 * 48 + 48)
                        max_scores(u + 2, k2, s, 0, False)
                    if s == QB - 1 and ahead_keys:
                        t.wait_ge(mrow[k1], i1 * 48 + 48)
                    for pair in range(2):
                        if s < QB - 1:
                            key_scores(u, k, s + 1, pair, False)
                        elif ahead_keys:
                            key_scores(u + 1, k1, 0, pair, False)
                        if ahead_max:
                            max_scores(u + 2, k2, s, 1 + pair, False)
                    if s == 0 and not (first and k == 0):
                        t.wait_ge(evac, u)
                    values(u, k, s)
                    if ahead_max:
                        max_scores(u + 2, k2, s, 3, False)
                    if s == 0 and not (last and k == NBUF - 1):
                        turn_max(u + 1, k1)
                    if s == 2 and not (first and k == 0):
                        turn_out(u - 1)
            slots(nc.tensor, slot)
            turn_out(U - 1)


def after_attention(nc, mem, l, x_src):
    G, D = ATT[l]["g"], ATT[l]["d"]
    E = MOE[l]["e"]
    HC = 4 if l == 0 else 2
    router = mem.named["gwT"] if l == 0 else mem.named["rwT"]
    with ExitStack() as c:
        def sb(n, s, t):
            return c.enter_context(nc.sbuf_tensor(f"{n}_c{l}", s, t))

        def sem(n):
            return mem.sem(f"c{l}_{n}")
        x4 = sb("x4", [P, QB, C], F32)
        att = sb("att", [P, G, QB, 4 * D], F32)
        amem = sb("amem", [P, QB, C], F32)
        gate = sb("gate", [P, C], F32)
        rows = sb("rows", [P, 3, C], F32)
        t4 = sb("t4", [P, QB, C], F32)
        x1 = sb("x1", [P, QB, C], F32)
        base = sb("base", [P, QB, C], F32)
        stats = sb("stats", [P, QB, 6], F32)
        mark = sb("mark", [P, 1], F32)
        mv = sb("mv", [P, QB, 2], F32)
        rstd = sb("rstd", [P, QB], F32)
        half = sb("half", [P, QB], F32)
        xn = sb("xn", [P, QB, C], F32)
        hrows = sb("hrows", [P, QB, C], F32)
        hT = sb("hT", [P, CC, S], F32)
        ex = sb("ex", [P, QB, E], F32)
        hid = sb("hid", [P, HC, S], F32)
        sig = sb("sig", [P, HC, S], F32)
        if l == 0:
            up = sb("up", [P, CC, 512], F32)
            down = sb("down", [P, 4, C], F32)
        else:
            up, down = mem.named["suT"], mem.named["sdT"]
        ps_t = c.enter_context(nc.psum_tensor(f"ps_t_c{l}", [P, CC, 512], F32))
        ps_l = c.enter_context(nc.psum_tensor(f"ps_l_c{l}", [P, 512], F32))
        ps_u = c.enter_context(nc.psum_tensor(f"ps_u_c{l}", [P, 4, 512], F32))
        (x_in, rows_in, w_in, own, x1_ok, var_ok, rstd_ok, xn_ok, turned, h_ok, hrow_ok, logit, ex_ok, score_ok,
         hid_ps, act_ok, hid_ok, down_ps, base_ok, h_st, base_st, init) = (
            sem(n) for n in ("x", "rows", "w", "own", "x1", "var", "rstd", "xn", "turned", "h", "hrow", "logit",
                             "ex", "score", "hidps", "act", "hid", "down", "base", "hst", "basest", "init"))
        NL = 3 + l
        K_OWN = 5 if l == 0 else 10
        prime(nc, [x1_ok, hrow_ok, base_ok, h_st, base_st, score_ok, hid_ok, act_ok, ex_ok])
        block = c.enter_context(nc.Block())

        @block.sync
        def _(sp):
            if l == 0:
                sp.dma_start(up[:, :, :], mem.A["L0_ffn_w_up_shared"].rearrange("(c p) n -> p c n", p=P)).then_inc(w_in, 16)
                sp.dma_start(down[:, :, :], mem.A["L0_ffn_w_down_shared"].rearrange("(c p) n -> p c n", p=P)).then_inc(w_in, 16)
            with nc.sync.Fori(0, B) as b:
                sp.wait_ge(x1_ok, b + 1)
                sp.dma_start(x4[:, :, :], x_src[bass.ds(b, 1)].rearrange("a (i p) c -> (a p) i c", p=P)).then_inc(x_in, 16)
                sp.dma_start(att[:, :, :, :], mem.att_d[l][bass.ds(b, 1)].rearrange("b g p n -> (b p) g n")).then_inc(x_in, 16)
                if l == 1:
                    sp.dma_start(amem[:, :, :], mem.amem_d[bass.ds(b, 1)].rearrange("a (i p) c -> (a p) i c", p=P)).then_inc(x_in, 16)
                sp.dma_start(gate[:, :], mem.mod_d[l, bass.ds(b, 1), 2 * C:3 * C].rearrange("b n -> (b n)").partition_broadcast(P)).then_inc(x_in, 16)
                sp.wait_ge(hrow_ok, b * 2 + 1)
                sp.wait_ge(base_ok, b + 1)
                sp.dma_start(rows[:, :, :].rearrange("p a n -> p (a n)"),
                             mem.mod_d[l, bass.ds(b, 1), 3 * C:6 * C].rearrange("b n -> (b n)").partition_broadcast(P)).then_inc(rows_in, 16)

        @block.gpsimd
        def _(pool):
            g = nc.gpsimd
            g.memset(half[:, :], -0.5).then_inc(init, 1)
            pool.wait_ge(init, 1)
            with g.Fori(0, B) as b:
                pool.wait_ge(var_ok, b + 1)
                g.tensor_tensor(rstd[:, :], mv[:, :, 1], half[:, :], ALU.pow).then_inc(rstd_ok, 1)
                pool.wait_ge(xn_ok, b * QB + QB)
                pool.wait_ge(rows_in, b * 16 + 16)
                pool.wait_ge(h_st, b * 16 + 1)
                g.tensor_tensor(hrows[:, :, :], xn[:, :, :], rows[:, 1, :].unsqueeze(1).to_broadcast([P, QB, C]), ALU.mult).then_inc(hrow_ok, 1)
                pool.wait_ge(hrow_ok, b * 2 + 1 + 1)
                g.tensor_tensor(hrows[:, :, :], hrows[:, :, :], rows[:, 0, :].unsqueeze(1).to_broadcast([P, QB, C]), ALU.add).then_inc(hrow_ok, 1)

        @block.vector
        def _(v):
            V = nc.vector
            with V.Fori(0, B) as b:
                do = Chain(v, own, b * K_OWN)
                v.wait_ge(base_ok, b + 1)
                v.wait_ge(x_in, (b + 1) * 16 * NL)
                if l == 0:
                    for i in range(QB):
                        last = V.tensor_tensor(t4[:, i, :].rearrange("p (g n) -> p g n", g=G), att[:, :, i, :],
                                               gate[:, :].rearrange("p (g n) -> p g n", g=G), ALU.mult)
                    do(last)
                else:
                    do(V.tensor_scalar(att[:, :, :, :], att[:, :, :, :], mem.wmem[:, 1:2], None, ALU.mult))
                    for i in range(QB):
                        last = V.tensor_tensor(t4[:, i, :].rearrange("p (j g d) -> p j g d", j=4, g=G),
                                               att[:, :, i, :].rearrange("p g (j d) -> p j g d", j=4),
                                               amem[:, i, :].rearrange("p (j g d) -> p j g d", j=4, g=G), ALU.add)
                    do(last)
                    do(V.tensor_tensor(t4[:, :, :], t4[:, :, :], gate[:, :].unsqueeze(1).to_broadcast([P, QB, C]), ALU.mult))
                V.tensor_tensor(x1[:, :, :], x4[:, :, :], t4[:, :, :], ALU.add).then_inc(x1_ok, 1)
                v.wait_ge(x1_ok, b + 2)
                for i in range(QB):
                    last = V.bn_stats(stats[:, i, :], x1[:, i, :])
                do(last)
                V.memset(mark[:, :], 0.0)
                for i in range(QB):
                    last = V.bn_aggr(mv[:, i, :], stats[:, i, :])
                do(last)
                V.tensor_scalar(mv[:, :, 1], mv[:, :, 1], EPS, None, ALU.add).then_inc(var_ok, 1)
                v.wait_ge(rstd_ok, b + 1)
                v.wait_ge(hrow_ok, b * 2 + 1)
                for i in range(QB):
                    V.tensor_scalar(xn[:, i, :], x1[:, i, :], mv[:, i, 0:1], rstd[:, i:i + 1],
                                    ALU.subtract, ALU.mult).then_inc(xn_ok, 1)
                for cc in range(CC):
                    v.wait_ge(turned, b * CC + cc + 1)
                    V.tensor_scalar(hT[:, cc, :], ps_t[:, cc, :], mem.modT[:, l, 8 + cc, bass.ds(b, 1)],
                                    mem.modT[:, l, 6 + cc, bass.ds(b, 1)], ALU.mult, ALU.add).then_inc(h_ok, 1)
                v.wait_ge(ex_ok, b + 2)
                do(V.tensor_scalar(ex[:, :, :], ex[:, :, :], 1.0, None, ALU.add))
                V.reciprocal(mem.scores[:, bass.ds(b * QB, QB), 0:E], ex[:, :, :]).then_inc(score_ok, 1)
                if l == 0:
                    for h in range(HC):
                        v.wait_ge(act_ok, b * HC + h + 1 + 1)
                        V.tensor_tensor(hid[:, h, :], sig[:, h, :], sig[:, h, :], ALU.mult).then_inc(hid_ok, 1)
                else:
                    v.wait_ge(act_ok, b + 2)
                    do(V.tensor_scalar(sig[:, :, :], sig[:, :, :], 1.0, None, ALU.add))
                    do(V.reciprocal(sig[:, :, :], sig[:, :, :]))
                    do(V.tensor_tensor(hid[:, :, :], ps_u[:, 0:2, :], sig[:, :, :], ALU.mult))
                    V.tensor_tensor(hid[:, :, :], hid[:, :, :], ps_u[:, 2:4, :], ALU.mult).then_inc(hid_ok, 1)
                v.wait_ge(down_ps, b + 1)
                v.wait_ge(rows_in, b * 16 + 16)
                v.wait_ge(base_st, b * 16 + 1)
                do(V.tensor_tensor(t4[:, :, :], ps_t[:, :, :].rearrange("p a (i c) -> p (a i) c", c=C),
                                   rows[:, 2, :].unsqueeze(1).to_broadcast([P, QB, C]), ALU.mult))
                V.tensor_tensor(base[:, :, :], t4[:, :, :], x1[:, :, :], ALU.add).then_inc(base_ok, 1)
                assert do.n == K_OWN

        @block.scalar
        def _(s):
            A = nc.scalar.activation
            with nc.scalar.Fori(0, B) as b:
                s.wait_ge(logit, b + 1)
                s.wait_ge(score_ok, b + 1)
                A(ex[:, :, :], ps_l[:, 0:QB * E].rearrange("p (i e) -> p i e", e=E), ACT.Exp, scale=-1.0).then_inc(ex_ok, 1)
                if l == 0:
                    s.wait_ge(hid_ok, b * HC + 1)
                    for h in range(HC):
                        s.wait_ge(hid_ps, b * HC + h + 1)
                        A(sig[:, h, :], ps_u[:, h, :], ACT.Relu).then_inc(act_ok, 1)
                else:
                    s.wait_ge(hid_ok, b + 1)
                    s.wait_ge(hid_ps, b * HC + HC)
                    A(sig[:, :, :], ps_u[:, 0:2, :], ACT.Exp, scale=-1.0).then_inc(act_ok, 1)
                s.wait_ge(hrow_ok, b * 2 + 2 + 1)
                s.dma_start(mem.h_d[bass.ds(b, 1)].rearrange("b (i p) c -> (b p) i c", p=P), hrows[:, :, :]).then_inc(h_st, 16)
                s.wait_ge(base_ok, b + 2)
                s.dma_start(mem.base_d[bass.ds(b, 1)].rearrange("b (i p) c -> (b p) i c", p=P), base[:, :, :]).then_inc(base_st, 16)
            s.wait_ge(h_st, 16 * B + 1)
            s.wait_ge(base_st, 16 * B + 1)

        @block.tensor
        def _(t):
            mm = nc.tensor.matmul
            if l == 0:
                t.wait_ge(w_in, 32)
            with nc.tensor.Fori(0, B) as b:
                t.wait_ge(base_ok, b + 1)
                t.wait_ge(xn_ok, b * QB + QB)
                for cc in range(CC):
                    for i in range(QB):
                        last = nc.tensor.transpose(ps_t[:, cc, i * P:(i + 1) * P], xn[:, i, cc * P:(cc + 1) * P], mem.ident[:, :])
                    last.then_inc(turned, 1)
                t.wait_ge(h_ok, b * CC + CC)
                t.wait_ge(ex_ok, b + 1)
                for i in range(QB):
                    for cc in range(CC):
                        last = mm(ps_l[:, i * E:(i + 1) * E], hT[:, cc, i * P:(i + 1) * P], router[:, cc, :], start=(cc == 0), stop=(cc == CC - 1))
                last.then_inc(logit, 1)
                t.wait_ge(act_ok, (b * HC if l == 0 else b) + 1)
                t.wait_ge(hid_ok, (b * HC if l == 0 else b) + 1)
                for h in range(HC):
                    for part, w in ((0, up),) if l == 0 else ((0, mem.named["sgT"]), (2, up)):
                        for cc in range(CC):
                            last = mm(ps_u[:, part + h, :], w[:, cc, h * P:(h + 1) * P], hT[:, cc, :], start=(cc == 0), stop=(cc == CC - 1))
                    last.then_inc(hid_ps, 1)
                t.wait_ge(hid_ok, ((b + 1) * HC if l == 0 else b + 1) + 1)
                for i in range(QB):
                    for h in range(HC):
                        last = mm(ps_t[:, i // 2, (i % 2) * C:(i % 2) * C + C], hid[:, h, i * P:(i + 1) * P], down[:, h, :],
                                  start=(h == 0), stop=(h == HC - 1))
                last.then_inc(down_ps, 1)


def routing(nc, mem, l):
    m = MOE[l]
    E, N, K, GS = m["e"], m["n"], m["k"], m["e"] // m["n"]
    with ExitStack() as c:
        def sb(n, s, t=F32):
            return c.enter_context(nc.sbuf_tensor(f"{n}_d{l}", s, t))

        def sem(n):
            return mem.sem(f"d{l}_{n}")
        biased = sb("biased", [P, NT, E])
        hi = [sb(f"hi{k}", [P, NT * N, GS // 2]) for k in range(2)]
        lo = [sb(f"lo{k}", [P, NT * N, GS // 2]) for k in range(2)]
        gsum = sb("gsum", [P, NT, N])
        cmp = sb("cmp", [P, NT, N, N])
        eqs = sb("eqs", [P, NT, N, N])
        lower = sb("lower", [P, N, N])
        kept = sb("kept", [P, NT, N])
        kth = sb("kth", [P, NT, 8])
        sel = sb("sel", [P, NT, E])
        selb = sb("selb", [P, NT, E], BF16)
        scan = [sb(f"scan{k}", [P, NT, E]) for k in range(2)]
        w = sb("w", [P, NT, E])
        cnt = sb("cnt", [P, NT])
        ebase = sb("ebase", [P, 3, E])
        ebase_i = sb("ebase_i", [P, E], I32)
        tix = sb("tix", [P, 2])
        tcmp = sb("tcmp", [P, 2, E])
        eid = sb("eid", [P, 2])
        eid_i = sb("eid_i", [P, 2], I32)
        idx = sb("idx", [P, NT, 8])
        sidx = sb("sidx", [P, NT, 8], I32)
        skip = sb("skip", [P, NT, 8])
        NH = 4
        hb = sb("hb", [P, NH, C])
        ps_p = c.enter_context(nc.psum_tensor(f"ps_p_d{l}", [P, NT * E], F32))
        ps_n = c.enter_context(nc.psum_tensor(f"ps_n_d{l}", [P, NT * E], F32))
        own, init, picked, counted, listed, eid_ok, eid_st = (sem(n) for n in ("own", "init", "picked", "counted", "listed", "eid", "eidst"))
        h_in = [sem(f"h{k}") for k in range(NH)]
        sent = [sem(f"sent{k}") for k in range(NH)]
        block = c.enter_context(nc.Block())

        @block.gpsimd
        def _(pool):
            g = nc.gpsimd
            g.memset(lower[:, :, :], 1.0).then_inc(init, 1)
            pool.wait_ge(init, 1)
            g.affine_select(out=lower[:, :, :], in_=lower[:, :, :], compare_op=ALU.is_gt, fill=0.0, base=0,
                            pattern=[[1, N], [-1, N]], channel_multiplier=0).then_inc(init, 1)
            g.iota(tix[:, :], pattern=[[P, 2]], base=0, channel_multiplier=1, allow_small_or_imprecise_dtypes=True).then_inc(init, 1)
            g.iota(ebase[:, 0, :], pattern=[[m["cap"] or 0, E]], base=0, channel_multiplier=0, allow_small_or_imprecise_dtypes=True).then_inc(init, 1)
            pool.wait_ge(listed, 1)
            for i in range(NT):
                pool.wait_ge(h_in[i % NH], 16 * (i // NH + 1))
                for k in range(K):
                    g.indirect_dma_start(out=mem.xs_d[0:SLOTS[l] + 1, :],
                                         out_offset=bass.IndirectOffsetOnAxis(ap=sidx[:, i, k:k + 1], axis=0),
                                         in_=hb[:, i % NH, :], in_offset=None,
                                         bounds_check=SLOTS[l], oob_is_err=False).then_inc(sent[i % NH], 16)
            for n in range(NH):
                pool.wait_ge(sent[n], 16 * K * (NT // NH))

        @block.sync
        def _(sp):
            hv = mem.h_d.rearrange("b (i p) c -> (b i) p c", p=P)
            for i in range(NT):
                if i >= NH:
                    sp.wait_ge(sent[i % NH], 16 * K * (i // NH))
                sp.dma_start(hb[:, i % NH, :], hv[i]).then_inc(h_in[i % NH], 16)
            if l == 0:
                sp.wait_ge(eid_ok, 1)
                sp.dma_start(mem.eid_d.rearrange("(h p) -> p h", p=P), eid_i[:, :], allow_slow_non_contiguous=True).then_inc(eid_st, 16)
                sp.wait_ge(eid_st, 16)

        @block.vector
        def _(v):
            V = nc.vector
            TT, TS = V.tensor_tensor, V.tensor_scalar
            do = Chain(v, own)
            sc = mem.scores[:, :, 0:E]
            do(TT(biased[:, :, :], sc, mem.gbias[l][:, :].unsqueeze(1).to_broadcast([P, NT, E]), ALU.add))
            grp = biased[:, :, :].rearrange("p t (n s) -> p (t n) s", n=N)
            h = GS // 2
            do(TT(hi[0][:, :, :], grp[:, :, 0:h], grp[:, :, h:], ALU.max))
            do(TT(lo[0][:, :, :], grp[:, :, 0:h], grp[:, :, h:], ALU.min))
            a = 0
            while h > 1:
                q = h // 2
                H, L = hi[a], lo[a]
                do(TT(hi[1 - a][:, :, 0:q], H[:, :, 0:q], H[:, :, q:h], ALU.max))
                do(TT(lo[1 - a][:, :, 0:q], H[:, :, 0:q], H[:, :, q:h], ALU.min))
                do(TT(L[:, :, 0:q], L[:, :, 0:q], L[:, :, q:h], ALU.max))
                do(TT(lo[1 - a][:, :, 0:q], lo[1 - a][:, :, 0:q], L[:, :, 0:q], ALU.max))
                h, a = q, 1 - a
            gs = gsum[:, :, :]
            do(TT(gs.rearrange("p t n -> p (t n)"), hi[a][:, :, 0], lo[a][:, :, 0], ALU.add))
            v.wait_ge(init, 4)
            other, this = gs.unsqueeze(2).to_broadcast([P, NT, N, N]), gs.unsqueeze(3).to_broadcast([P, NT, N, N])
            do(TT(cmp[:, :, :, :], other, this, ALU.is_gt))
            do(TT(eqs[:, :, :, :], other, this, ALU.is_equal))
            do(TT(eqs[:, :, :, :], eqs[:, :, :, :], lower[:, :, :].unsqueeze(1).to_broadcast([P, NT, N, N]), ALU.mult))
            do(TT(cmp[:, :, :, :], cmp[:, :, :, :], eqs[:, :, :, :], ALU.add))
            do(V.tensor_reduce(kept[:, :, :], cmp[:, :, :, :], axis=AX.X, op=ALU.add))
            do(TS(kept[:, :, :], kept[:, :, :], float(m["kg"]), None, ALU.is_lt))
            kb = kept[:, :, :].rearrange("p t n -> p (t n)").unsqueeze(2).to_broadcast([P, NT * N, GS])
            if l == 0:
                do(TS(kept[:, :, :], kept[:, :, :], -1.0, 1.0e30, ALU.add, ALU.mult))
                do(TT(grp, grp, kb, ALU.add))
            else:
                do(TT(grp, grp, kb, ALU.mult))
                do(TS(grp, grp, 0.0, None, ALU.add))
            for i in range(NT):
                last = V.max(kth[:, i, :], biased[:, i, :])
            do(last)
            kv = kth[:, :, K - 1].unsqueeze(2).to_broadcast([P, NT, E])
            do(TT(sel[:, :, :], biased[:, :, :], kv, ALU.is_gt))
            do(TT(scan[0][:, :, :], biased[:, :, :], kv, ALU.is_equal))
            do(TT(w[:, :, :], biased[:, :, :], kv, ALU.is_equal))
            do(V.tensor_reduce(cnt[:, :], sel[:, :, :], axis=AX.X, op=ALU.add))
            a, sh = 0, 1
            while sh < E:
                do(V.tensor_copy(scan[1 - a][:, :, 0:sh], scan[a][:, :, 0:sh]))
                do(TT(scan[1 - a][:, :, sh:], scan[a][:, :, sh:], scan[a][:, :, 0:E - sh], ALU.add))
                a, sh = 1 - a, 2 * sh
            do(TT(scan[a][:, :, :], scan[a][:, :, :], cnt[:, :].unsqueeze(2).to_broadcast([P, NT, E]), ALU.add))
            do(TS(scan[a][:, :, :], scan[a][:, :, :], float(K), None, ALU.is_le))
            do(TT(w[:, :, :], w[:, :, :], scan[a][:, :, :], ALU.mult))
            do(TT(sel[:, :, :], sel[:, :, :], w[:, :, :], ALU.add))
            V.tensor_copy(selb[:, :, :], sel[:, :, :]).then_inc(picked, 1)
            do(TT(w[:, :, :], sc, sel[:, :, :], ALU.mult))
            do(V.tensor_reduce(cnt[:, :], w[:, :, :], axis=AX.X, op=ALU.add))
            do(TS(cnt[:, :], cnt[:, :], 1e-20, None, ALU.add))
            do(V.reciprocal(cnt[:, :], cnt[:, :]))
            do(TT(w[:, :, :], w[:, :, :], cnt[:, :].unsqueeze(2).to_broadcast([P, NT, E]), ALU.mult))
            do(TS(w[:, :, :], w[:, :, :], m["scale"], None, ALU.mult))
            v.wait_ge(counted, 2)
            tot = ps_n[:, :].rearrange("p (t e) -> p t e", e=E)
            do(V.tensor_copy(scan[0][:, :, :], tot))
            a, sh = 0, 1
            while sh < NT:
                do(V.tensor_copy(scan[1 - a][:, 0:sh, :], scan[a][:, 0:sh, :]))
                do(TT(scan[1 - a][:, sh:, :], scan[a][:, sh:, :], scan[a][:, 0:NT - sh, :], ALU.add))
                a, sh = 1 - a, 2 * sh
            slot, incl = scan[1 - a], scan[a]
            do(TT(slot[:, :, :], incl[:, :, :], tot, ALU.subtract))
            do(TT(slot[:, :, :], slot[:, :, :], ps_p[:, :].rearrange("p (t e) -> p t e", e=E), ALU.add))
            if l == 0:
                do(TS(ebase_i[:, :], incl[:, NT - 1, :], float(P - 1), None, ALU.add))
                do(TS(ebase_i[:, :], ebase_i[:, :], 7, None, ALU.arith_shift_right))
                do(V.tensor_copy(ebase[:, 0, :], ebase_i[:, :]))
                do(V.tensor_copy(ebase[:, 1, :], ebase[:, 0, :]))
                e, sh = 1, 1
                while sh < E:
                    do(V.tensor_copy(ebase[:, 3 - e, 0:sh], ebase[:, e, 0:sh]))
                    do(TT(ebase[:, 3 - e, sh:], ebase[:, e, sh:], ebase[:, e, 0:E - sh], ALU.add))
                    e, sh = 3 - e, 2 * sh
                for n in range(2):
                    last = TT(tcmp[:, n, :], ebase[:, e, :], tix[:, n:n + 1].to_broadcast([P, E]), ALU.is_le)
                do(last)
                do(V.tensor_reduce(eid[:, :], tcmp[:, :, :], axis=AX.X, op=ALU.add))
                do(TS(eid[:, :], eid[:, :], float(E - 1), None, ALU.min))
                V.tensor_copy(eid_i[:, :], eid[:, :]).then_inc(eid_ok, 1)
                do(TT(ebase[:, 0, :], ebase[:, e, :], ebase[:, 0, :], ALU.subtract))
                do(TS(ebase[:, 0, :], ebase[:, 0, :], float(P), None, ALU.mult))
            else:
                do(TS(incl[:, :, :], slot[:, :, :], float(m["cap"]), None, ALU.is_lt))
                do(TT(sel[:, :, :], sel[:, :, :], incl[:, :, :], ALU.mult))
                do(TT(w[:, :, :], w[:, :, :], incl[:, :, :], ALU.mult))
            do(TT(slot[:, :, :], slot[:, :, :], ebase[:, 0, :].unsqueeze(1).to_broadcast([P, NT, E]), ALU.add))
            do(TS(slot[:, :, :], slot[:, :, :], 1.0, None, ALU.add))
            do(TT(slot[:, :, :], slot[:, :, :], sel[:, :, :], ALU.mult))
            for i in range(NT):
                last = V.max(idx[:, i, :], slot[:, i, :])
            do(last)
            do(V.tensor_copy(mem.gidx[:, :, :], idx[:, :, :]))
            do(TS(skip[:, :, :], idx[:, :, :], 0.0, 1.0e6, ALU.is_equal, ALU.mult))
            do(TT(skip[:, :, :], skip[:, :, :], idx[:, :, :], ALU.add))
            V.tensor_copy(sidx[:, :, :], skip[:, :, :]).then_inc(listed, 1)
            for k in range(K):
                do(TT(incl[:, :, :], slot[:, :, :], idx[:, :, k].unsqueeze(2).to_broadcast([P, NT, E]), ALU.is_equal))
                do(TT(incl[:, :, :], incl[:, :, :], w[:, :, :], ALU.mult))
                do(V.tensor_reduce(mem.wk[:, :, k], incl[:, :, :], axis=AX.X, op=ALU.add))

        @block.tensor
        def _(t):
            t.wait_ge(picked, 1)
            flat = selb[:, :, :].rearrange("p t e -> p (t e)")
            for ps, left in ((ps_p, mem.before), (ps_n, mem.onesb)):
                for n in range(0, NT * E, 512):
                    last = nc.tensor.matmul(ps[:, n:n + 512], left[:, :], flat[:, n:n + 512], start=True, stop=True)
                last.then_inc(counted, 1)


def experts_any(nc, mem):
    TL, E = MOE[0]["tiles"], MOE[0]["e"]
    assert TL % 4 == 0
    with ExitStack() as c:
        def sb(n, s, t=F32):
            return c.enter_context(nc.sbuf_tensor(f"{n}_e0", s, t))

        def sem(n):
            return mem.sem(f"e0_{n}")
        w1 = sb("w1", [P, E, CC, P])
        w2 = sb("w2", [P, E, C])
        table = sb("table", [1, TL], I32)
        xin = sb("xin", [P, 4, C])
        xT = sb("xT", [P, 2, C])
        r = sb("r", [P, 2, P])
        aT = sb("aT", [P, 2, P])
        y = sb("y", [P, 4, C])
        ps_x = c.enter_context(nc.psum_tensor("ps_x_e0", [P, 2, 512], F32))
        ps_h = c.enter_context(nc.psum_tensor("ps_h_e0", [P, 2, 512], F32))
        ps_r = c.enter_context(nc.psum_tensor("ps_r_e0", [P, 2, 512], F32))
        ps_y = c.enter_context(nc.psum_tensor("ps_y_e0", [P, 2, 512], F32))
        x_in = [sem(f"x{k}") for k in range(4)]
        y_st = [sem(f"yst{k}") for k in range(4)]
        w_in, t_in, x_turned, xT_ok, h_ps, r_ok, r_turned, aT_ok, y_ps, y_ok = (
            sem(n) for n in ("w", "t", "xturn", "xT", "h", "r", "rturn", "aT", "yps", "y"))
        prime(nc, y_st + [y_ok])
        block = c.enter_context(nc.Block())
        xs = mem.xs_d[1:1 + TL * P, :].rearrange("(t p) c -> t p c", p=P)
        ys = mem.ys_d[1:1 + TL * P, :].rearrange("(t p) c -> t p c", p=P)
        w1_d = mem.A["L0_ffn_w1_experts"].rearrange("e (c p) i -> p e c i", p=P)
        w2_d = mem.A["L0_ffn_w2_experts"].rearrange("e i c -> i e c")

        def slots(engine, slot):
            for k in range(4):
                slot(k, 0, k)
            with engine.Fori(1, TL // 4) as it:
                for k in range(4):
                    slot(it * 4 + k, it, k)
            for k in range(3):
                slot(TL + k, TL // 4, k)

        def stage(s, lag):
            return not isinstance(s, int) or 0 <= s - lag < TL

        @block.sync
        def _(sp):
            sp.dma_start(table[:, :], mem.eid_d.rearrange("(a n) -> a n", a=1)).then_inc(t_in, 16)
            for e in range(0, E, 8):
                for cc in range(CC):
                    sp.dma_start(w1[:, e:e + 8, cc, :], w1_d[:, e:e + 8, cc, :]).then_inc(w_in, 16)
                sp.dma_start(w2[:, e:e + 8, :], w2_d[:, e:e + 8, :]).then_inc(w_in, 16)

            def load(t, k):
                sp.dma_start(xin[:, k, :], xs[bass.ds(t, 1)].rearrange("t p c -> (t p) c")).then_inc(x_in[k], 16)
            for t in range(3):
                load(t, t)

            def slot(s, it, k):
                if stage(s, 0) and (not isinstance(s, int) or s + 3 < TL):
                    if not (isinstance(s, int) and s < 1):
                        sp.wait_ge(x_turned, s)
                    load(s + 3, (k + 3) % 4)
                if stage(s, 3):
                    sp.wait_ge(y_ok, s - 2 + 1)
                    sp.dma_start(ys[bass.ds(s - 3, 1)].rearrange("t p c -> (t p) c"), y[:, (k - 3) % 4, :]).then_inc(y_st[(k - 3) % 4], 16)
            for k in range(4):
                slot(k, 0, k)
            with nc.sync.Fori(1, TL // 4 - 1) as it:
                for k in range(4):
                    slot(it * 4 + k, it, k)
            for k in range(7):
                slot(TL - 4 + k, TL // 4 - 1 + k // 4, k % 4)
            for k in range(4):
                sp.wait_ge(y_st[k], 16 * (TL // 4) + 1)

        @block.tensor
        def _(t):
            mm = nc.tensor.matmul
            t.wait_ge(t_in, 16)
            t.wait_ge(w_in, 16 * 3 * (E // 8))

            def slot(s, it, k):
                if stage(s, 3):
                    n = s - 3
                    e = nc.tensor.value_load(table[0:1, bass.ds(n, 1)], min_val=0, max_val=E - 1)
                    t.wait_ge(aT_ok, s - 2)
                    if not (isinstance(s, int) and n < 2):
                        t.wait_ge(y_ok, s - 4 + 1)
                    q = (k - 3) % 2
                    mm(ps_y[:, q, 0:C], aT[:, q, :], w2[:, bass.ds(e, 1), :].rearrange("p e c -> p (e c)"), start=True, stop=True).then_inc(y_ps, 1)
                if stage(s, 2):
                    q = (k - 2) % 2
                    t.wait_ge(r_ok, s - 1)
                    nc.tensor.transpose(ps_r[:, q, 0:P], r[:, q, :], mem.ident[:, :]).then_inc(r_turned, 1)
                if stage(s, 1):
                    e = nc.tensor.value_load(table[0:1, bass.ds(s - 1, 1)], min_val=0, max_val=E - 1)
                    q = (k - 1) % 2
                    t.wait_ge(xT_ok, s)
                    for cc in range(CC):
                        last = mm(ps_h[:, q, 0:P], xT[:, q, cc * P:(cc + 1) * P], w1[:, bass.ds(e, 1), cc, :].rearrange("p e c -> p (e c)"),
                                  start=(cc == 0), stop=(cc == CC - 1))
                    last.then_inc(h_ps, 1)
                if stage(s, 0):
                    t.wait_ge(x_in[k], it * 16 + 16)
                    for cc in range(CC):
                        last = nc.tensor.transpose(ps_x[:, k % 2, cc * P:(cc + 1) * P], xin[:, k, cc * P:(cc + 1) * P], mem.ident[:, :])
                    last.then_inc(x_turned, 1)
            slots(nc.tensor, slot)

        @block.vector
        def _(v):
            V = nc.vector

            def slot(s, it, k):
                if stage(s, 3):
                    v.wait_ge(y_ps, s - 2)
                    if not (isinstance(s, int) and s - 3 < 4):
                        v.wait_ge(y_st[(k - 3) % 4], (it - (1 if k < 3 else 0)) * 16 + 1)
                    V.tensor_copy(y[:, (k - 3) % 4, :], ps_y[:, (k - 3) % 2, 0:C]).then_inc(y_ok, 1)
                if stage(s, 0):
                    v.wait_ge(x_turned, s + 1)
                    if not (isinstance(s, int) and s < 2):
                        v.wait_ge(h_ps, s - 1)
                    V.tensor_copy(xT[:, k % 2, :], ps_x[:, k % 2, 0:C]).then_inc(xT_ok, 1)
            slots(V, slot)

        @block.scalar
        def _(a):
            def slot(s, it, k):
                if stage(s, 2):
                    q = (k - 2) % 2
                    a.wait_ge(r_turned, s - 1)
                    if not (isinstance(s, int) and s - 2 < 2):
                        a.wait_ge(y_ps, s - 3)
                    nc.scalar.activation(aT[:, q, :], ps_r[:, q, 0:P], ACT.Square).then_inc(aT_ok, 1)
                if stage(s, 1):
                    q = (k - 1) % 2
                    a.wait_ge(h_ps, s)
                    if not (isinstance(s, int) and s - 1 < 2):
                        a.wait_ge(r_turned, s - 2)
                    nc.scalar.activation(r[:, q, :], ps_h[:, q, 0:P], ACT.Relu).then_inc(r_ok, 1)
            slots(nc.scalar, slot)


def experts_capped(nc, mem):
    E, CAP = MOE[1]["e"], MOE[1]["cap"]
    R2 = CAP - P
    with ExitStack() as c:
        def sb(n, s, t=F32):
            return c.enter_context(nc.sbuf_tensor(f"{n}_e1", s, t))

        def sem(n):
            return mem.sem(f"e1_{n}")
        NB = 4
        wgu = sb("wgu", [P, NB, 2, CC, P])
        wd = sb("wd", [P, NB, C])
        xa = sb("xa", [P, NB, C])
        xb = sb("xb", [P, NB, C])
        xT = sb("xT", [P, 2, CC, CAP])
        sig = sb("sig", [P, CAP])
        gu = sb("gu", [P, CAP])
        aT = sb("aT", [P, 2, CAP])
        y = sb("y", [P, 2, 2, C])
        ps_x = c.enter_context(nc.psum_tensor("ps_x_e1", [P, 2, 512], F32))
        ps_g = c.enter_context(nc.psum_tensor("ps_g_e1", [P, 2, 512], F32))
        ps_y = c.enter_context(nc.psum_tensor("ps_y_e1", [P, 2, 512], F32))
        ld = [sem(f"ld{k}") for k in range(NB)]
        y_st = [sem(f"yst{k}") for k in range(2)]
        own, x_turned, xT_ok, g_ps, sig_ok, a_ok, y_ps, y_ok = (sem(n) for n in ("own", "xturn", "xT", "g", "sig", "a", "yps", "y"))
        block = c.enter_context(nc.Block())
        xs = mem.xs_d[1:1 + E * CAP, :].rearrange("(e r) c -> e r c", r=CAP)
        ys = mem.ys_d[1:1 + E * CAP, :].rearrange("(e r) c -> e r c", r=CAP)
        A = mem.A

        def slots(engine, slot, lead=0):
            for k in range(4):
                slot(k, 0, k)
            with engine.Fori(1, E // 4 - 1) as it:
                for k in range(4):
                    slot(it * 4 + k, it, k)
            for k in range(6):
                slot(E - 4 + k, E // 4 - 1 + k // 4, k % 4)

        def stage(s, lag):
            return not isinstance(s, int) or 0 <= s - lag < E

        @block.sync
        def _(sp):
            def load(e, k):
                for n, w in ((0, "gate"), (1, "up")):
                    sp.dma_start(wgu[:, k, n, :, :], A[f"L1_ffn_W_{w}"][bass.ds(e, 1)].rearrange("e (c p) i -> (e p) c i", p=P)).then_inc(ld[k], 16)
                sp.dma_start(wd[:, k, :], A["L1_ffn_W_down"][bass.ds(e, 1)].rearrange("e i c -> (e i) c")).then_inc(ld[k], 16)
                sp.dma_start(xa[:, k, :], xs[bass.ds(e, 1), 0:P].rearrange("e r c -> (e r) c")).then_inc(ld[k], 16)
                sp.dma_start(xb[0:R2, k, :], xs[bass.ds(e, 1), P:CAP].rearrange("e r c -> (e r) c")).then_inc(ld[k], 16)
            for e in range(2):
                load(e, e)

            def slot(s, it, k):
                if not isinstance(s, int) or s + 2 < E:
                    if not (isinstance(s, int) and s < 2):
                        sp.wait_ge(y_ps, s - 1)
                    load(s + 2, (k + 2) % 4)
            slots(nc.sync, slot)

        @block.tensor
        def _(t):
            mm = nc.tensor.matmul

            def slot(s, it, k):
                if stage(s, 2):
                    q, b = k % 2, (k - 2) % 4
                    t.wait_ge(a_ok, s - 1)
                    if not (isinstance(s, int) and s - 2 < 2):
                        t.wait_ge(y_ok, s - 3)
                    mm(ps_y[:, q, 0:C], aT[:, q, 0:P], wd[:, b, :], start=True, stop=True)
                    mm(ps_y[0:R2, q, C:2 * C], aT[:, q, P:CAP], wd[:, b, :], start=True, stop=True, skip_group_check=True).then_inc(y_ps, 1)
                if stage(s, 1):
                    q, b = (k - 1) % 2, (k - 1) % 4
                    t.wait_ge(xT_ok, s)
                    for n in range(2):
                        for cc in range(CC):
                            last = mm(ps_g[:, q, n * CAP:(n + 1) * CAP], wgu[:, b, n, cc, :], xT[:, q, cc, :], start=(cc == 0), stop=(cc == CC - 1))
                    last.then_inc(g_ps, 1)
                if stage(s, 0):
                    q = k % 2
                    t.wait_ge(ld[k], it * 80 + 80)
                    for cc in range(CC):
                        nc.tensor.transpose(ps_x[:, q, cc * CAP:cc * CAP + P], xa[:, k, cc * P:(cc + 1) * P], mem.ident[:, :])
                        last = nc.tensor.transpose(ps_x[:, q, cc * CAP + P:(cc + 1) * CAP], xb[0:R2, k, cc * P:(cc + 1) * P], mem.ident[0:R2, 0:R2])
                    last.then_inc(x_turned, 1)
            slots(nc.tensor, slot)

        @block.vector
        def _(v):
            V = nc.vector

            def slot(s, it, k):
                if stage(s, 0):
                    v.wait_ge(x_turned, s + 1)
                    if not (isinstance(s, int) and s < 2):
                        v.wait_ge(g_ps, s - 1)
                    V.tensor_copy(xT[:, k % 2, :, :], ps_x[:, k % 2, 0:CC * CAP].rearrange("p (c n) -> p c n", n=CAP)).then_inc(xT_ok, 1)
                if stage(s, 1):
                    q = (k - 1) % 2
                    n = s - 1
                    v.wait_ge(sig_ok, s)
                    do = Chain(v, own, n * 3)
                    do(V.tensor_scalar(sig[:, :], sig[:, :], 1.0, None, ALU.add))
                    do(V.reciprocal(sig[:, :], sig[:, :]))
                    do(V.tensor_tensor(gu[:, :], ps_g[:, q, 0:CAP], sig[:, :], ALU.mult))
                    if not (isinstance(s, int) and n < 2):
                        v.wait_ge(y_ps, s - 2)
                    V.tensor_tensor(aT[:, q, :], gu[:, :], ps_g[:, q, CAP:2 * CAP], ALU.mult).then_inc(a_ok, 1)
            slots(V, slot)

        @block.scalar
        def _(a):
            def slot(s, it, k):
                if stage(s, 2):
                    q = k % 2
                    a.wait_ge(y_ps, s - 1)
                    if not (isinstance(s, int) and s - 2 < 2):
                        a.wait_ge(y_st[q], (it * 2 + k // 2 - 1) * 32)
                    nc.scalar.activation(y[:, q, 0, :], ps_y[:, q, 0:C], ACT.Copy)
                    nc.scalar.activation(y[0:R2, q, 1, :], ps_y[0:R2, q, C:2 * C], ACT.Copy).then_inc(y_ok, 1)
                    a.wait_ge(y_ok, s - 1)
                    a.dma_start(ys[bass.ds(s - 2, 1), 0:P].rearrange("e r c -> (e r) c"), y[:, q, 0, :]).then_inc(y_st[q], 16)
                    a.dma_start(ys[bass.ds(s - 2, 1), P:CAP].rearrange("e r c -> (e r) c"), y[0:R2, q, 1, :]).then_inc(y_st[q], 16)
                if stage(s, 1):
                    q = (k - 1) % 2
                    a.wait_ge(g_ps, s)
                    if not (isinstance(s, int) and s - 1 < 1):
                        a.wait_ge(a_ok, s - 1)
                    nc.scalar.activation(sig[:, :], ps_g[:, q, 0:CAP], ACT.Exp, scale=-1.0).then_inc(sig_ok, 1)
            slots(nc.scalar, slot)
            for q in range(2):
                a.wait_ge(y_st[q], 32 * (E // 2))


def combine(nc, mem, l, dst):
    K = MOE[l]["k"]
    with ExitStack() as c:
        def sb(n, s, t=F32):
            return c.enter_context(nc.sbuf_tensor(f"{n}_f{l}", s, t))

        def sem(n):
            return mem.sem(f"f{l}_{n}")
        NB = 4
        yk = sb("yk", [P, NB, K, C])
        base = sb("base", [P, NB, C])
        gate = sb("gate", [P, B, C])
        acc2 = sb("acc", [P, 2, C])
        res = sb("res", [P, NB, C])
        got = [sem(f"got{k}") for k in range(NB)]
        ld = [sem(f"ld{k}") for k in range(NB)]
        st = [sem(f"st{k}") for k in range(NB)]
        own, done, gates = sem("own"), sem("done"), sem("gates")
        block = c.enter_context(nc.Block())
        src = mem.base_d.rearrange("b (i p) c -> (b i) p c", p=P)
        out = dst.rearrange("b (i p) c -> (b i) p c", p=P)

        @block.gpsimd
        def _(pool):
            for i in range(NT):
                if i >= NB:
                    pool.wait_ge(done, i - NB + 1)
                for k in range(K):
                    nc.gpsimd.indirect_dma_start(out=yk[:, i % NB, k, :], out_offset=None, in_=mem.ys_d[0:SLOTS[l] + 1, :],
                                                 in_offset=bass.IndirectOffsetOnAxis(ap=mem.gidx[:, i, k:k + 1], axis=0)).then_inc(got[i % NB], 16)

        @block.sync
        def _(sp):
            for b in range(B):
                sp.dma_start(gate[:, b, :], mem.mod_d[l, b, 5 * C:6 * C].partition_broadcast(P)).then_inc(gates, 16)
            for i in range(NT + 2):
                if i < NT:
                    if i >= NB:
                        sp.wait_ge(done, i - NB + 1)
                    sp.dma_start(base[:, i % NB, :], src[i]).then_inc(ld[i % NB], 16)
                if i >= 2:
                    n = i - 2
                    sp.wait_ge(done, n + 1)
                    sp.dma_start(out[n], res[:, n % NB, :]).then_inc(st[n % NB], 16)
            for k in range(NB):
                sp.wait_ge(st[k], 16 * (NT // NB))

        @block.vector
        def _(v):
            V = nc.vector
            do = Chain(v, own)
            v.wait_ge(gates, 16 * B)
            for i in range(NT):
                k4, acc = i % NB, acc2[:, i % 2]
                v.wait_ge(got[k4], 16 * K * (i // NB + 1))
                do(V.tensor_scalar(acc[:, :], yk[:, k4, 0, :], mem.wk[:, i, 0:1], None, ALU.mult))
                for k in range(1, K):
                    do(V.scalar_tensor_tensor(out=acc[:, :], in0=yk[:, k4, k, :], scalar=mem.wk[:, i, k:k + 1], in1=acc[:, :],
                                              op0=ALU.mult, op1=ALU.add))
                do(V.tensor_tensor(acc[:, :], acc[:, :], gate[:, i // QB, :], ALU.mult))
                v.wait_ge(ld[k4], 16 * (i // NB + 1))
                if i >= NB:
                    v.wait_ge(st[k4], 16 * (i // NB))
                V.tensor_tensor(res[:, k4, :], acc[:, :], base[:, k4, :], ALU.add).then_inc(done, 1)


class Memory:
    def __init__(self, nc, ctx):
        self.nc, self.ctx, self.named, self.sems = nc, ctx, {}, []

    def sb(self, name, shape, dt):
        return self.ctx.enter_context(self.nc.sbuf_tensor(name, shape, dt))

    def sem(self, name):
        self.sems.append(self.nc.alloc_semaphore(name))
        return self.sems[-1]

    def clear_semaphores(self):
        self.nc.clear_and_free_semaphores(self.sems)
        self.nc.all_engine_barrier()
        self.sems = []

    def dram(self, name, shape, dt):
        return self.nc.dram_tensor(name, shape, dt, kind="Internal").ap()


def adaln_two_layers(nc, A, out):
    with ExitStack() as ctx:
        mem = Memory(nc, ctx)
        mem.A = A
        mem.q_stack = [mem.dram(f"q_stack{l}", [len(a["pairs"]), B, a["g"] * a["d"] * 4, S], BF16) for l, a in enumerate(ATT)]
        mem.k_stack = [mem.dram(f"k_stack{l}", [len(a["pairs"]), B, a["g"] * a["d"], S], BF16) for l, a in enumerate(ATT)]
        mem.v_blocks = [mem.dram(f"v_blocks{l}", [B, a["g"], P, QB, VW], F32) for l, a in enumerate(ATT)]
        mem.att_d = [mem.dram(f"att_d{l}", [B, a["g"], P, QB * 4 * a["d"]], F32) for l, a in enumerate(ATT)]
        mem.amem_d = mem.dram("amem_d", [B, S, C], F32)
        mem.h_d = mem.dram("h_d", [B, S, C], F32)
        mem.base_d = mem.dram("base_d", [B, S, C], F32)
        mem.x2_d = mem.dram("x2_d", [B, S, C], F32)
        mem.xs_d = mem.dram("xs_d", [SLOTS[0] + 1, C], F32)
        mem.ys_d = mem.dram("ys_d", [SLOTS[0] + 1, C], F32)
        mem.eid_d = mem.dram("eid_d", [MOE[0]["tiles"]], I32)
        mem.scores = mem.sb("scores", [P, NT, 64], F32)
        mem.wk = mem.sb("wk", [P, NT, 8], F32)
        mem.gidx = mem.sb("gidx", [P, NT, 8], I32)
        mem.zeroed = ctx.enter_context(nc.semaphore("zeroed"))
        mem.zero_count = 16 * (SLOTS[0] // (16 * P) + 2)
        setup(nc, mem, A)
        x = A["L0_attn_x"]
        for l in range(2):
            projections(nc, mem, l, x)
            attention(nc, mem, l)
            after_attention(nc, mem, l, x)
            routing(nc, mem, l)
            if l == 0:
                experts_any(nc, mem)
            else:
                experts_capped(nc, mem)
            combine(nc, mem, l, mem.x2_d if l == 0 else out)
            x = mem.x2_d
            mem.clear_semaphores()


def kernel(**inputs):
    import numpy as _np
    import concourse.bacc as _bacc
    from concourse import mybir as _mybir
    from concourse.bass_utils import run_bass_kernel_spmd as _run

    nc = _bacc.Bacc("TRN2", target_bir_lowering=False, num_devices=1)
    arrays, A = {}, {}
    for name, value in inputs.items():
        a = _np.ascontiguousarray(value)
        arrays[f"in_{name}"] = a
        A[name] = nc.dram_tensor(f"in_{name}", a.shape, _mybir.dt.from_np(a.dtype), kind="ExternalInput").ap()
    out = nc.dram_tensor("out", [B, S, C], F32, kind="ExternalOutput").ap()
    adaln_two_layers(nc, A, out)
    r = _run(nc, [arrays], core_ids=[0])
    return r.results[0]["out"]
```

```python
from contextlib import ExitStack

import numpy as np
import concourse.bass as bass
from concourse import mybir

F32 = mybir.dt.float32
BF16 = mybir.dt.bfloat16
I32 = mybir.dt.int32
ALU = mybir.AluOpType
ACT = mybir.ActivationFunctionType
AX = mybir.AxisListType

P = 128
B, S, C = 8, 512, 256
T = B * S
NT = T // P
QB = S // P
CC = C // P
NEG = -1.0e30
EPS = 1e-5
VW = 32
MROW = 96
KROWS = MROW + 3
NBUF = 4

PAIRS6 = [(0, 0), (0, 1), (0, 2), (1, 0), (1, 1), (2, 0)]
PAIRS9 = [(q, k) for q in range(3) for k in range(3)]
Q_RUNS6, K_RUNS6 = [(0, 0, 1, 3), (1, 3, 1, 2), (2, 5, 1, 1)], [(0, 0, 3, 2), (0, 5, 1, 1), (1, 1, 3, 2), (2, 2, 1, 1)]
Q_RUNS9, K_RUNS9 = [(p, 3 * p, 1, 3) for p in range(3)], [(p, p, 3, 3) for p in range(3)]

ATT = [dict(g=4, d=16, pairs=PAIRS6, q_runs=Q_RUNS6, k_runs=K_RUNS6, causal=True, scale=0.25),
       dict(g=8, d=8, pairs=PAIRS9, q_runs=Q_RUNS9, k_runs=K_RUNS9, causal=False, scale=float(np.float32(1.0 / np.sqrt(np.float32(8)))))]
MOE = [dict(e=64, n=8, kg=4, k=6, scale=2.5, cap=None, tiles=T * 6 // P + 64),
       dict(e=32, n=8, kg=3, k=4, scale=2.5, cap=160, tiles=None)]
SLOTS = [MOE[0]["tiles"] * P, MOE[1]["e"] * MOE[1]["cap"]]


class Chain:

    def __init__(self, engine, sem, base=0):
        self.engine, self.sem, self.base, self.n = engine, sem, base, 0

    def __call__(self, instruction):
        self.n += 1
        instruction.then_inc(self.sem, 1)
        self.engine.wait_ge(self.sem, self.base + self.n)


def setup(nc, mem, A):
    sb, d = mem.sb, mem.dram
    mem.ident = sb("ident", [P, P], F32)
    mem.identb = sb("identb", [P, P], BF16)
    mem.mask_q = sb("mask_q", [P, P], BF16)
    mem.mask_k = sb("mask_k", [P, P], BF16)
    mem.before = sb("before", [P, P], BF16)
    mem.onesb = sb("onesb", [P, P], BF16)
    mem.modT = sb("modT", [P, 2, 6 * CC, B], F32)
    mem.wq0 = sb("wq0", [P, CC, C], F32)
    mem.wk0 = sb("wk0", [P, CC, 64], F32)
    mem.wv0 = sb("wv0", [P, CC, 64], F32)
    mem.bq0 = sb("bq0", [P, CC], F32)
    mem.bk0 = sb("bk0", [64, 1], F32)
    mem.bv0 = sb("bv0", [P, 64], F32)
    mem.gbias = [sb("gbias0", [P, 64], F32), sb("gbias1", [P, 32], F32)]
    mem.wmem = sb("wmem", [P, 2], F32)
    mem.memr = sb("memr", [P, CC, 4, 65], F32)
    turned = [("gwT", A["L0_ffn_gate_w"], 64), ("wqT", A["L1_attn_Wq"], 256), ("wkT", A["L1_attn_Wk"], 64),
              ("wvT", A["L1_attn_Wv"], 64), ("rwT", A["L1_ffn_router_w"], 32),
              ("sgT", A["L1_ffn_shared_gate"], 256), ("suT", A["L1_ffn_shared_up"], 256),
              ("sdT", A["L1_ffn_shared_down"], 256)]
    for name, _, rows in turned:
        mem.named[name] = sb(name, [P, CC, rows], F32)
    blocks = [(name, src, r, min(P, rows - r)) for name, src, rows in turned for r in range(0, rows, P)]
    NBK = len(blocks)
    mem.mod_d = d("mod_d", [2, B, 6 * C], F32)

    with ExitStack() as c:
        rows_in = c.enter_context(nc.sbuf_tensor("rows_in", [P, NBK, C], F32))
        c_in = c.enter_context(nc.sbuf_tensor("c_in", [B, 2, C], F32))
        c_e = c.enter_context(nc.sbuf_tensor("c_e", [B, 2, C], F32))
        cT = c.enter_context(nc.sbuf_tensor("cT", [P, 2 * CC, B], F32))
        wmod = c.enter_context(nc.sbuf_tensor("wmod", [P, 2, CC, 6 * C], F32))
        mod = c.enter_context(nc.sbuf_tensor("mod", [B, 2, 6 * C], F32))
        tmp = c.enter_context(nc.sbuf_tensor("tmp_s", [B, 2, 4, C], F32))
        ps = c.enter_context(nc.psum_tensor("ps_s", [P, 2, 512], F32))
        psm = c.enter_context(nc.psum_tensor("psm_s", [P, 3, 512], F32))
        pst = c.enter_context(nc.psum_tensor("pst_s", [P, 512], F32))
        loaded = mem.sem("s_loaded")
        small = mem.sem("s_small")
        rows_ld = mem.sem("s_rows")
        wmod_ld = mem.sem("s_wmod")
        consts = mem.sem("s_consts")
        dve = mem.sem("s_dve")
        act = mem.sem("s_act")
        pe = mem.sem("s_pe")
        stored = mem.sem("s_stored")
        ready = mem.sem("s_ready")
        memw = mem.sem("s_memw")
        block = c.enter_context(nc.Block())

        @block.sync
        def _(sp):
            for l in range(2):
                sp.dma_start(c_in[:, l, :], A[f"L{l}_c"]).then_inc(small, 16)
            for l in range(2):
                sp.dma_start(wmod[:, l, :, :], A[f"L{l}_wmod"].rearrange("(c p) n -> p c n", p=P)).then_inc(wmod_ld, 16)
            for i, (_, src, r, n) in enumerate(blocks):
                sp.dma_start(rows_in[0:n, i, :], src[r:r + n, :]).then_inc(rows_ld, 16)
            sp.wait_ge(ready, 1)
            sp.dma_start(mem.mod_d.rearrange("l b n -> b l n"), mod[:, :, :]).then_inc(stored, 16)
            sp.wait_ge(stored, 16)
            sp.wait_ge(loaded, 16 * (10 + 16 + 16))

        @block.gpsimd
        def _(pool):
            g = nc.gpsimd
            n = 0
            for t, v in ((mem.ident, 0.0), (mem.identb, 0.0), (mem.mask_q, 0.0), (mem.mask_k, 0.0),
                         (mem.before, 1.0), (mem.onesb, 1.0), (mem.memr, 0.0)):
                g.memset(t[:], v).then_inc(consts, 1)
                n += 1
            pool.wait_ge(consts, n)
            for t in (mem.ident, mem.identb):
                g.affine_select(out=t[:, :], in_=t[:, :], compare_op=ALU.not_equal, fill=1.0, base=0,
                                pattern=[[-1, P]], channel_multiplier=1).then_inc(consts, 1)
            g.affine_select(out=mem.mask_q[:, :], in_=mem.mask_q[:, :], compare_op=ALU.is_ge, fill=NEG, base=0,
                            pattern=[[-1, P]], channel_multiplier=1).then_inc(consts, 1)
            g.affine_select(out=mem.mask_k[:, :], in_=mem.mask_k[:, :], compare_op=ALU.is_ge, fill=NEG, base=0,
                            pattern=[[1, P]], channel_multiplier=-1).then_inc(consts, 1)
            g.affine_select(out=mem.before[:, :], in_=mem.before[:, :], compare_op=ALU.is_gt, fill=0.0, base=0,
                            pattern=[[1, P]], channel_multiplier=-1).then_inc(consts, 1)

        @block.scalar
        def _(s):
            s.wait_ge(small, 32)
            nc.scalar.activation(c_e[:, :, :], c_in[:, :, :], ACT.Exp, scale=-1.0).then_inc(act, 1)
            q = s.dma_start
            q(mem.wq0[:, :, :].rearrange("p c (h d) -> p c h d", d=16)[:, 0], A["L0_attn_Wq"].rearrange("h (c p) d -> c p h d", p=P)[0]).then_inc(loaded, 16)
            q(mem.wq0[:, :, :].rearrange("p c (h d) -> p c h d", d=16)[:, 1], A["L0_attn_Wq"].rearrange("h (c p) d -> c p h d", p=P)[1]).then_inc(loaded, 16)
            for w, n in ((mem.wk0, "k"), (mem.wv0, "v")):
                for cc in range(CC):
                    q(w[:, :, :].rearrange("p c (h d) -> p c h d", d=16)[:, cc], A[f"L0_attn_W{n}"].rearrange("h (c p) d -> c p h d", p=P)[cc]).then_inc(loaded, 16)
            with nc.allow_non_contiguous_dma(reason="small"):
                for g in range(4):
                    for j in range(4):
                        q(mem.bq0[64 * (g % 2) + j:64 * (g % 2) + j + 61:4, g // 2:g // 2 + 1],
                          A["L0_attn_bq"][4 * g + j, :].rearrange("(d o) -> d o", o=1)).then_inc(loaded, 16)
                q(mem.bk0[:, :], A["L0_attn_bk"].rearrange("h d -> (h d)").rearrange("(p o) -> p o", o=1)).then_inc(loaded, 16)
            q(mem.bv0[:, :], A["L0_attn_bv"].rearrange("h d -> (h d)").partition_broadcast(P)).then_inc(loaded, 16)
            q(mem.gbias[0][:, :], A["L0_ffn_gate_bias"].partition_broadcast(P)).then_inc(loaded, 16)
            q(mem.gbias[1][:, :], A["L1_ffn_e_bias"].partition_broadcast(P)).then_inc(loaded, 16)
            q(mem.wmem[:, 0:1], A["L1_attn_memory_weight"].partition_broadcast(P)).then_inc(memw, 16)
            s.wait_ge(consts, 7)
            for cc in range(CC):
                for j in range(4):
                    q(mem.memr[j:j + 125:4, cc, j, 0:64], A["L1_attn_memory"][32 * cc:32 * cc + 32, :]).then_inc(loaded, 16)
                    q(mem.memr[j:j + 125:4, cc, j, 64:65], A["L1_attn_memory_norm"][32 * cc:32 * cc + 32, :]).then_inc(loaded, 16)
            s.wait_ge(memw, 16)
            nc.scalar.activation(mem.wmem[:, 1:2], mem.wmem[:, 0:1], ACT.Exp, scale=-1.0).then_inc(act, 1)

        @block.vector
        def _(v):
            do = Chain(v, dve)
            V = nc.vector
            v.wait_ge(act, 1)
            do(V.tensor_scalar(c_e[:, :, :], c_e[:, :, :], 1.0, None, ALU.add))
            do(V.reciprocal(c_e[:, :, :], c_e[:, :, :]))
            do(V.tensor_tensor(c_in[:, :, :], c_in[:, :, :], c_e[:, :, :], ALU.mult))
            v.wait_ge(pe, 1)
            do(V.tensor_copy(cT[:, :, :], pst[:, 0:2 * CC * B].rearrange("p (a b) -> p a b", b=B)))
            for l in range(2):
                v.wait_ge(pe, 2 + l)
                do(V.tensor_copy(mod[:, l, :], psm[0:B, :, :].rearrange("p a n -> p (a n)")))
            parts = mod[:, :, :].rearrange("b l (h x) -> b (l h) x", h=2)
            g, sign, low = parts[:, :, 2 * C:3 * C], tmp[:, 0], tmp[:, 1]
            do(V.tensor_scalar(sign, g, 0.0, 2.0, ALU.is_ge, ALU.mult))
            do(V.tensor_scalar(sign, sign, -1.0, None, ALU.add))
            do(V.tensor_scalar(low, g, -1.0, None, ALU.mult))
            do(V.tensor_tensor(g, g, low, ALU.max))
            do(V.tensor_scalar(g, g, 0.25, None, ALU.max))
            do(V.tensor_tensor(g, g, sign, ALU.mult))
            do(V.tensor_scalar(parts[:, :, C:2 * C], parts[:, :, C:2 * C], 1.0, None, ALU.add))
            V.tensor_copy(tmp[:, 0, 0, 0:1], tmp[:, 0, 0, 1:2]).then_inc(ready, 1)
            v.wait_ge(pe, 4)
            v.wait_ge(act, 2)
            do(V.tensor_scalar(mem.wmem[:, 1:2], mem.wmem[:, 1:2], 1.0, None, ALU.add))
            do(V.reciprocal(mem.wmem[:, 0:1], mem.wmem[:, 1:2]))
            do(V.tensor_scalar(mem.wmem[:, 1:2], mem.wmem[:, 0:1], -1.0, 1.0, ALU.mult, ALU.add))
            do(V.tensor_copy(mem.modT[:, :, :, :], pst[:, 64:64 + 24 * B].rearrange("p (l a b) -> p l a b", l=2, b=B)))
            for i, (name, _, r, n) in enumerate(blocks):
                v.wait_ge(pe, 5 + i)
                do(V.tensor_copy(mem.named[name][:, :, r:r + n], ps[:, i % 2, 0:2 * P].rearrange("p (c t) -> p c t", t=P)[:, :, 0:n]))

        @block.tensor
        def _(t):
            t.wait_ge(consts, 12)
            t.wait_ge(dve, 3)
            for l in range(2):
                for cc in range(CC):
                    a = 2 * l + cc
                    last = nc.tensor.transpose(pst[:, a * B:(a + 1) * B], c_in[:, l, cc * P:(cc + 1) * P], mem.ident[0:B, 0:B])
            last.then_inc(pe, 1)
            t.wait_ge(dve, 4)
            t.wait_ge(wmod_ld, 32)
            for l in range(2):
                if l:
                    t.wait_ge(dve, 4 + l)
                for n in range(3):
                    for cc in range(CC):
                        last = nc.tensor.matmul(psm[0:B, n, :], cT[:, 2 * l + cc, :], wmod[:, l, cc, n * 512:(n + 1) * 512],
                                                start=(cc == 0), stop=(cc == CC - 1))
                last.then_inc(pe, 1)
            t.wait_ge(ready, 1)
            for l in range(2):
                for a in range(12):
                    o = 64 + (12 * l + a) * B
                    last = nc.tensor.transpose(pst[:, o:o + B], mod[:, l, a * P:(a + 1) * P], mem.ident[0:B, 0:B])
            last.then_inc(pe, 1)
            t.wait_ge(rows_ld, 16 * NBK)
            base = 3 + 1 + 2 + 7 + 3 + 1
            for i, (name, _, r, n) in enumerate(blocks):
                if i >= 2:
                    t.wait_ge(dve, base + i - 1)
                for cc in range(CC):
                    last = nc.tensor.transpose(ps[:, i % 2, cc * P:cc * P + n], rows_in[0:n, i, cc * P:(cc + 1) * P], mem.ident[0:n, 0:n])
                last.then_inc(pe, 1)


def wait_after(engine, sem, count):
    if not isinstance(count, int) or count > 0:
        engine.wait_ge(sem, count)


def batches(engine, body, n=B):
    for k in range(2):
        body(k, 0, k, False)
    with engine.Fori(1, n // 2 - 1) as i:
        for k in range(2):
            body(i * 2 + k, i, k, False)
    for k in range(2):
        body(n - 2 + k, n // 2 - 1, k, k == 1)


def projections(nc, mem, l, x_src):
    a = ATT[l]
    G, D = a["g"], a["d"]
    GD = G * D
    q_stack, k_stack, v_blocks = mem.q_stack[l], mem.k_stack[l], mem.v_blocks[l]
    wk = mem.wk0 if l == 0 else mem.named["wkT"]
    wv = mem.wv0 if l == 0 else mem.named["wvT"]
    with ExitStack() as c:
        def sb(n, s, t):
            return c.enter_context(nc.sbuf_tensor(f"{n}_a{l}", s, t))

        def sem(n):
            return mem.sem(f"a{l}_{n}")
        wq = sb("wq", [P, CC, C], F32)
        x4 = sb("x4", [P, 2, QB, C], F32)
        stats = sb("stats", [P, QB, 6], F32)
        mv = sb("mv", [P, QB, 2], F32)
        rstd = sb("rstd", [P, QB], F32)
        mark = sb("mark", [P, 1], F32)
        half = sb("half", [P, QB], F32)
        xn = sb("xn", [P, QB, C], F32)
        hT = sb("hT", [P, CC, S], F32)
        full = sb("full", [P, 3, S], F32)
        rest = sb("rest", [P, 3, S], F32)
        parts = sb("parts", [P, 2, 3, 3, S], BF16)
        vs = sb("vs", [P, 2, QB, G, VW], F32)
        ps_t = c.enter_context(nc.psum_tensor(f"ps_t_a{l}", [P, CC, 512], F32))
        ps_q = c.enter_context(nc.psum_tensor(f"ps_q_a{l}", [P, 3, 512], F32))
        ps_v = c.enter_context(nc.psum_tensor(f"ps_v_a{l}", [P, 512], F32))
        if l == 1:
            elu = sb("elu", [P, CC, S], F32)
            low = sb("low", [P, CC, S], F32)
            rden = sb("rden", [P, QB, 4], F32)
            amem = sb("amem", [P, 2, QB, C], F32)
            ps_m = c.enter_context(nc.psum_tensor(f"ps_m_a{l}", [P, 2, 512], F32))
            K = MOE[0]["k"]
            yk = sb("yk", [P, 2, QB, K, C], F32)
            index = sb("index", [P, 2, QB, K], I32)
            indexed = sem("indexed")
            base = sb("base", [P, 2, QB, C], F32)
            gate = sb("gate", [P, 2, C], F32)
            acc = sb("acc", [P, 2, C], F32)
            got = [[sem(f"got{k}{t}") for t in range(QB)] for k in range(2)]
            x_st = [sem(f"xst{k}") for k in range(2)]
            summed, sums, passed = sem("summed"), sem("sums"), sem("passed")
        x_in = [sem(f"x{k}") for k in range(2)]
        stored = [sem(f"stored{k}") for k in range(2)]
        var_ok, rstd_ok, xn_ok, turned, h_ok = (sem(n) for n in ("var", "rstd", "xn", "turned", "h"))
        proj, q_full, part1, rest1, part2, part3 = (sem(n) for n in ("proj", "full", "p1", "r1", "p2", "p3"))
        wq_ok = sem("wq")
        v_ok, own, low_ok, exp_ok, elu_ok, mem_ps, mem_ok, vset, hset = (
            sem(n) for n in ("v", "own", "low", "exp", "elu", "memps", "mem", "vset", "half"))
        NST = CC * len(a["q_runs"]) + len(a["k_runs"]) + 1 + l
        block = c.enter_context(nc.Block())

        @block.sync
        def _(sp):
            def body(b, i, k, last):
                sp.wait_ge(v_ok, b + 1)
                sp.wait_ge(part3, b * 3 + 3)
                if l == 1:
                    nc.sync.sem_inc(passed, 1)
                for p, r0, step, n in a["q_runs"]:
                    for m in range(CC):
                        dst = q_stack[r0:r0 + step * (n - 1) + 1:step, bass.ds(b, 1), m * P:(m + 1) * P].rearrange("r b q s -> (b q) r s")
                        sp.dma_start(dst, parts[:, k, m, p, :].unsqueeze(1).to_broadcast([P, n, S])).then_inc(stored[k], 16)
                for p, r0, step, n in a["k_runs"]:
                    dst = k_stack[r0:r0 + step * (n - 1) + 1:step, bass.ds(b, 1)].rearrange("r b q s -> (b q) r s")
                    sp.dma_start(dst, parts[0:GD, k, 2, p, :].unsqueeze(1).to_broadcast([GD, n, S])).then_inc(stored[k], 16)
                sp.dma_start(v_blocks[bass.ds(b, 1)].rearrange("b g p i w -> (b p) i g w"), vs[:, k]).then_inc(stored[k], 16)
                if l == 1:
                    if not (isinstance(b, int) and b == 0):
                        store_memory(b - 1, 1 - k)
                    if not last:
                        sp.wait_ge(summed, b * QB + 2 * QB)
                    if not (isinstance(b, int) and b + 2 >= B):
                        load(b + 2, k)
                    if not last:
                        store(b + 1, 1 - k)

            def store_memory(b, k):
                sp.wait_ge(mem_ok, b * 4 + 4)
                sp.dma_start(mem.amem_d[bass.ds(b, 1)].rearrange("b (i p) c -> (b p) i c", p=P), amem[:, k]).then_inc(stored[k], 16)

            def load(b, k):
                sp.dma_start(base[:, k], mem.base_d[bass.ds(b, 1)].rearrange("b (i p) c -> (b p) i c", p=P)).then_inc(x_in[k], 16)
                sp.dma_start(gate[:, k], mem.mod_d[0, bass.ds(b, 1), 5 * C:6 * C].rearrange("b n -> (b n)").partition_broadcast(P)).then_inc(x_in[k], 16)

            def store(b, k):
                sp.dma_start(x_src[bass.ds(b, 1)].rearrange("b (i p) c -> (b p) i c", p=P), x4[:, k]).then_inc(x_st[k], 16)
            if l == 1:
                load(0, 0)
                load(1, 1)
                sp.wait_ge(summed, QB)
                store(0, 0)
            batches(nc.sync, body)
            if l == 1:
                store_memory(B - 1, 1)
            for k in range(2):
                sp.wait_ge(stored[k], B // 2 * 16 * NST)
                if l == 1:
                    sp.wait_ge(x_st[k], B // 2 * 16)

        @block.gpsimd
        def _(pool):
            def load(b, k):
                nc.gpsimd.dma_start(x4[:, k], x_src[bass.ds(b, 1), :, :].rearrange("a (i p) c -> (a p) i c", p=P)).then_inc(x_in[k], 16)

            def root(b):
                pool.wait_ge(var_ok, b + 1)
                nc.gpsimd.tensor_tensor(rstd[:, :], mv[:, :, 1], half[:, :], ALU.pow).then_inc(rstd_ok, 1)

            def gather(b, k, tiles):
                if tiles[0] == 0:
                    nc.gpsimd.tensor_copy(index[:, k], mem.gidx[:, bass.ds(b * QB, QB), 0:K]).then_inc(indexed, 1)
                    pool.wait_ge(indexed, b + 1)
                    nc.gpsimd.sem_inc(hset, 1)
                for t in tiles:
                    for n in range(K):
                        nc.gpsimd.indirect_dma_start(
                            out=yk[:, k, t, n, :], out_offset=None, in_=mem.ys_d[0:SLOTS[0] + 1, :],
                            in_offset=bass.IndirectOffsetOnAxis(ap=index[:, k, t, n:n + 1], axis=0)).then_inc(got[k][t], 16)
            nc.gpsimd.memset(half[:, :], -0.5).then_inc(hset, 1)
            pool.wait_ge(hset, 1)
            if l == 0:
                load(0, 0)
                load(1, 1)
                root(0)
            else:
                gather(0, 0, range(QB))
                gather(1, 1, range(1))
                root(0)
                gather(1, 1, range(1, QB))

            def body(b, i, k, last):
                more = not (isinstance(b, int) and b + 2 >= B)
                if more:
                    pool.wait_ge(xn_ok, b * QB + QB)
                if l == 0:
                    if more:
                        load(b + 2, k)
                    if not last:
                        root(b + 1)
                else:
                    if more:
                        gather(b + 2, k, range(1))
                    if not last:
                        root(b + 1)
                    if more:
                        gather(b + 2, k, range(1, QB))
            batches(nc.gpsimd, body)

        @block.vector
        def _(v):
            V = nc.vector
            for k in range(2):
                V.memset(vs[:, k], 0.0).then_inc(vset, 1)
            v.wait_ge(vset, 2)
            for k in range(2):
                V.memset(vs[:, k, :, :, D:D + 1], 1.0).then_inc(vset, 1)
            v.wait_ge(vset, 4)

            for cc in range(CC):
                src = mem.wq0[:, cc].rearrange("p (g j d) -> p g j d", j=4, d=D) if l == 0 else \
                    mem.named["wqT"][:, cc].rearrange("p (j g d) -> p g j d", j=4, d=D)
                V.tensor_copy(wq[:, cc].rearrange("p (g d j) -> p g j d", j=4, d=D), src).then_inc(wq_ok, 1)

            def add_experts(b, i, k, t0):
                first = (b * QB + t0) * (K + 1)
                if t0 == 0:
                    v.wait_ge(x_in[k], i * 32 + 32)
                    wait_after(v, x_st[k], i * 16)
                wait_after(v, summed, b * QB + t0)
                for step in range(K + 2):
                    for t in (t0, t0 + 1):
                        a = acc[:, t % 2, :]
                        weight = mem.wk[:, bass.ds(b * QB + t, 1), :].rearrange("p a n -> p (a n)")
                        if step == 0:
                            v.wait_ge(got[k][t], i * 16 * K + 16 * K)
                        else:
                            v.wait_ge(sums, first + 2 * step - 1 + t % 2)
                        if step == 0:
                            V.tensor_scalar(a, yk[:, k, t, 0, :], weight[:, 0:1], None, ALU.mult).then_inc(sums, 1)
                        elif step < K:
                            V.scalar_tensor_tensor(out=a, in0=yk[:, k, t, step, :], scalar=weight[:, step:step + 1], in1=a,
                                                   op0=ALU.mult, op1=ALU.add).then_inc(sums, 1)
                        elif step == K:
                            V.tensor_tensor(a, a, gate[:, k, :], ALU.mult).then_inc(sums, 1)
                        else:
                            V.tensor_tensor(x4[:, k, t, :], a, base[:, k, t, :], ALU.add).then_inc(summed, 1)

            def normalise(b, i, k, do):
                if l == 0:
                    v.wait_ge(x_in[k], i * 16 + 16)
                else:
                    v.wait_ge(summed, b * QB + QB)
                for t in range(QB):
                    last = V.bn_stats(stats[:, t, :], x4[:, k, t, :])
                do(last)
                V.memset(mark[:, :], 0.0)
                for t in range(QB):
                    last = V.bn_aggr(mv[:, t, :], stats[:, t, :])
                do(last)
                V.tensor_scalar(mv[:, :, 1], mv[:, :, 1], EPS, None, ALU.add).then_inc(var_ok, 1)
                v.wait_ge(rstd_ok, b + 1)
                for t in range(QB):
                    V.tensor_scalar(xn[:, t, :], x4[:, k, t, :], mv[:, t, 0:1], rstd[:, t:t + 1],
                                    ALU.subtract, ALU.mult).then_inc(xn_ok, 1)
            if l == 1:
                for t in (0, 2):
                    add_experts(0, 0, 0, t)
            normalise(0, 0, 0, Chain(v, own))

            def read_memory(b, k):
                for h in range(2):
                    v.wait_ge(mem_ps, b * 2 + h + 1)
                    jn = ps_m[:, :, 0:4 * 65].rearrange("p t (j n) -> p t j n", n=65)
                    V.reciprocal(rden[:, 2 * h:2 * h + 2, :], jn[:, :, :, 64]).then_inc(mem_ok, 1)
                    v.wait_ge(mem_ok, b * 4 + 2 * h + 1)
                    for t in range(2):
                        op = V.scalar_tensor_tensor(
                            out=amem[:, k, 2 * h + t, :].rearrange("p (j n) -> p j n", n=64), in0=jn[:, t, :, 0:64],
                            scalar=mem.wmem[:, 0:1], in1=rden[:, 2 * h + t, :].unsqueeze(2).to_broadcast([P, 4, 64]),
                            op0=ALU.mult, op1=ALU.mult)
                    op.then_inc(mem_ok, 1)

            def body(b, i, k, last):
                do = Chain(v, own, 2 + b * (2 + l))

                def ahead(t):
                    if l == 1 and not last:
                        add_experts(b + 1, i + k, 1 - k, t)
                wait_after(v, proj, b * 4)
                for cc in range(CC):
                    v.wait_ge(turned, b * CC + cc + 1)
                    V.tensor_scalar(hT[:, cc, :], ps_t[:, cc, :], mem.modT[:, l, 2 + cc, bass.ds(b, 1)],
                                    mem.modT[:, l, 0 + cc, bass.ds(b, 1)], ALU.mult, ALU.add).then_inc(h_ok, 1)
                if l == 0:
                    normalise(b + 1, i + k, 1 - k, do) if not last else None
                ahead(0)
                for m in range(3):
                    n = P if m < 2 else GD
                    v.wait_ge(part1, b * 3 + m + 1)
                    V.tensor_tensor(rest[0:n, m, :], full[0:n, m, :], parts[0:n, k, m, 0, :], ALU.subtract).then_inc(rest1, 1)
                if l == 1 and not (isinstance(b, int) and b == 0):
                    read_memory(b - 1, 1 - k)
                v.wait_ge(proj, b * 4 + 4)
                wait_after(v, stored[k], i * 16 * NST)
                o = vs[:, k, :, :, 0:D]
                src = ps_v[:, 0:QB * GD].rearrange("p (i g d) -> p i g d", g=G, d=D)
                if l == 0:
                    for t in range(QB):
                        op = V.tensor_tensor(o[:, t], src[:, t], mem.bv0[:, :].rearrange("p (g d) -> p g d", d=D), ALU.add)
                else:
                    op = V.tensor_copy(o, src)
                op.then_inc(v_ok, 1)
                for m in range(3):
                    n = P if m < 2 else GD
                    v.wait_ge(part2, b * 3 + m + 1)
                    V.tensor_tensor(parts[0:n, k, m, 2, :], rest[0:n, m, :], parts[0:n, k, m, 1, :], ALU.subtract).then_inc(part3, 1)
                if l == 1:
                    ahead(2)
                    if not last:
                        normalise(b + 1, i + k, 1 - k, do)
                    V.tensor_scalar(low[:, :, :], full[:, 0:2, :], 0.0, None, ALU.min).then_inc(low_ok, 1)
                    v.wait_ge(exp_ok, b + 1)
                    do(V.scalar_tensor_tensor(out=elu[:, :, :], in0=full[:, 0:2, :], scalar=0.0, in1=low[:, :, :],
                                              op0=ALU.max, op1=ALU.add))
                    V.tensor_scalar(elu[:, :, :], elu[:, :, :], -1.0, None, ALU.add).then_inc(elu_ok, 1)
            batches(V, body)
            if l == 1:
                read_memory(B - 1, 1)

        @block.scalar
        def _(s):
            def body(b, i, k, last):
                wait_after(s, stored[k], i * 16 * NST)
                wait_after(s, rest1, b * 3)
                if l == 1:
                    wait_after(s, elu_ok, b)
                for m in range(3):
                    n = P if m < 2 else GD
                    s.wait_ge(proj, b * 4 + m + 1)
                    if l == 0:
                        nc.scalar.activation(full[0:n, m, :], ps_q[0:n, m, :], ACT.Identity,
                                             bias=mem.bq0[:, m:m + 1] if m < 2 else mem.bk0[:, :]).then_inc(q_full, 1)
                    else:
                        nc.scalar.activation(full[0:n, m, :], ps_q[0:n, m, :], ACT.Copy).then_inc(q_full, 1)
                    s.wait_ge(q_full, b * 3 + m + 1)
                    nc.scalar.activation(parts[0:n, k, m, 0, :], full[0:n, m, :], ACT.Copy).then_inc(part1, 1)
                for m in range(3):
                    n = P if m < 2 else GD
                    s.wait_ge(rest1, b * 3 + m + 1)
                    nc.scalar.activation(parts[0:n, k, m, 1, :], rest[0:n, m, :], ACT.Copy).then_inc(part2, 1)
                if l == 1:
                    s.wait_ge(low_ok, b + 1)
                    nc.scalar.activation(low[:, :, :], low[:, :, :], ACT.Exp).then_inc(exp_ok, 1)
            batches(nc.scalar, body)

        @block.tensor
        def _(t):
            def turn(b):
                t.wait_ge(xn_ok, b * QB + QB)
                for cc in range(CC):
                    for i in range(QB):
                        op = nc.tensor.transpose(ps_t[:, cc, i * P:(i + 1) * P], xn[:, i, cc * P:(cc + 1) * P], mem.ident[:, :])
                    op.then_inc(turned, 1)
            def memory(b):
                t.wait_ge(elu_ok, b + 1)
                for h in range(2):
                    wait_after(t, mem_ok, b * 4 + 2 * h)
                    for j in range(2):
                        for cc in range(CC):
                            op = nc.tensor.matmul(ps_m[:, j, 0:260], elu[:, cc, (2 * h + j) * P:(2 * h + j + 1) * P],
                                                  mem.memr[:, cc].rearrange("p j n -> p (j n)"), start=(cc == 0), stop=(cc == CC - 1))
                    op.then_inc(mem_ps, 1)
            turn(0)
            t.wait_ge(wq_ok, CC)

            def body(b, i, k, last):
                t.wait_ge(h_ok, b * CC + CC)
                for m in range(3):
                    n = P if m < 2 else GD
                    wait_after(t, q_full, b * 3 - 2 + m)
                    for cc in range(CC):
                        w = wq[:, cc, m * P:(m + 1) * P] if m < 2 else wk[:, cc, :]
                        op = nc.tensor.matmul(ps_q[0:n, m, :], w, hT[:, cc, :], start=(cc == 0), stop=(cc == CC - 1))
                    op.then_inc(proj, 1)
                wait_after(t, v_ok, b)
                for j in range(QB):
                    for cc in range(CC):
                        op = nc.tensor.matmul(ps_v[:, j * GD:(j + 1) * GD], hT[:, cc, j * P:(j + 1) * P], wv[:, cc, :],
                                              start=(cc == 0), stop=(cc == CC - 1))
                op.then_inc(proj, 1)
                if l == 0 and not last:
                    turn(b + 1)
                if l == 1:
                    if not (isinstance(b, int) and b == 0):
                        memory(b - 1)
                    if not last:
                        turn(b + 1)
            batches(nc.tensor, body)
            if l == 1:
                memory(B - 1)


def attention(nc, mem, l):
    a = ATT[l]
    G, D, R, causal, scale = a["g"], a["d"], len(a["pairs"]), a["causal"], a["scale"]
    RD, U, NI = R * D, B * G, B * G // NBUF
    q_stack = mem.q_stack[l].rearrange("r b (g d j) s -> r (b g) d (j s)", d=D, j=4)
    k_stack = mem.k_stack[l].rearrange("r b (g d) s -> r (b g) d s", d=D)
    v_blocks = mem.v_blocks[l].rearrange("b g p i w -> (b g) p (i w)")
    out_d = mem.att_d[l].rearrange("b g p n -> (b g) p n")
    with ExitStack() as c:
        def sb(n, s, t):
            return c.enter_context(nc.sbuf_tensor(f"{n}_b{l}", s, t))

        def sem(n):
            return mem.sem(f"b{l}_{n}")
        qs = [sb(f"qs{k}", [P, 4, S], BF16) for k in range(NBUF)]
        ks = [sb(f"ks{k}", [P, S], BF16) for k in range(NBUF)]
        vb = [sb(f"vb{k}", [P, QB, VW], F32) for k in range(NBUF)]
        pt = sb("pt", [P, 2, 4, S], F32)
        negmax = sb("negmax", [P, 2, 4, QB], F32)
        mparts = sb("mparts", [16, 3, P], BF16)
        mrest = sb("mrest", [16, P], F32)
        oT = sb("oT", [P, S], F32)
        rsum = sb("rsum", [P, QB, 4], F32)
        o_out = sb("o_out", [P, 2, QB, 4, D], F32)
        if l == 0:
            zero = sb("zero", [P, SLOTS[0] // U // QB // P * C], F32)
        st = c.enter_context(nc.psum_tensor(f"st_b{l}", [P, 4, 512], F32))
        side = c.enter_context(nc.psum_tensor(f"side_b{l}", [P, 3, 512], F32))
        pv = c.enter_context(nc.psum_tensor(f"pv_b{l}", [P, 512], F32))
        ld = [sem(f"loaded{k}") for k in range(NBUF)]
        mrow = [sem(f"mrow{k}") for k in range(NBUF)]
        mx_done, items, st_done, exp_done, pv_done = (sem(n) for n in ("mx", "items", "st", "exp", "pv"))
        m_turned, own, evac, o_turned, quotients, init, cleared = (
            sem(n) for n in ("mT", "own", "evac", "oT", "rsum", "init", "cleared"))
        ITEMS, TURN_MAX, TURN_OUT = 18, 4, 13

        def item(u, pos):
            return (u + 2) * ITEMS + pos

        def score_pos(s, j):
            return s * 4 + j + (1 if s > 0 else 0) + (1 if s > 2 else 0)
        o_stored = [sem(f"ostored{k}") for k in range(2)]
        block = c.enter_context(nc.Block())

        def slots(engine, slot):
            for k in range(NBUF):
                slot(k, 0, k, True, False)
            with engine.Fori(1, NI - 1) as it:
                for k in range(NBUF):
                    slot(it * NBUF + k, it, k, False, False)
            for k in range(NBUF):
                slot(U - NBUF + k, NI - 1, k, False, True)

        def ahead(it, k, n):
            return (k + n) % NBUF, it + (k + n) // NBUF

        def cols(s):
            return (s * P if causal else 0, S)

        @block.sync
        def _(sp):
            def load(u, k):
                sp.dma_start(qs[k][0:RD, :, :].rearrange("r j s -> r (j s)"), q_stack[:, bass.ds(u, 1)].rearrange("r u d n -> r (u d) n")).then_inc(ld[k], 16)
                sp.dma_start(ks[k][0:RD, :], k_stack[:, bass.ds(u, 1)].rearrange("r u d s -> r (u d) s")).then_inc(ld[k], 16)
                sp.dma_start(vb[k][:, :, :].rearrange("p i w -> p (i w)"), v_blocks[bass.ds(u, 1)].rearrange("u r n -> (u r) n")).then_inc(ld[k], 16)

            def max_rows(k):
                for p in range(3):
                    sp.dma_start(qs[k][MROW + p:MROW + p + 1, :, :].rearrange("a j (i q) -> a (j i) q", q=P),
                                 mparts[:, p, :]).then_inc(mrow[k], 16)

            def store(u, k):
                sp.dma_start(out_d[bass.ds(u, 1)].rearrange("u p n -> (u p) n"),
                             o_out[:, k % 2].rearrange("p i j d -> p (i j d)")).then_inc(o_stored[k % 2], 16)

            sp.wait_ge(init, NBUF)
            for k in range(NBUF):
                load(k, k)
            sp.wait_ge(items, item(-1, TURN_MAX) + 1)
            max_rows(0)

            def slot(u, it, k, first, last):
                k1, _ = ahead(it, k, 1)
                if not (last and k == NBUF - 1):
                    sp.wait_ge(items, item(u, TURN_MAX) + 1)
                    max_rows(k1)
                if not (first and k == 0):
                    sp.wait_ge(items, item(u, TURN_OUT) + 1)
                    store(u - 1, (k - 1) % NBUF)
                if not last:
                    sp.wait_ge(pv_done, u * QB + QB)
                    load(u + NBUF, k)
            slots(nc.sync, slot)
            sp.wait_ge(items, item(U, TURN_OUT) + 1)
            store(U - 1, NBUF - 1)
            for k in range(2):
                sp.wait_ge(o_stored[k], 8 * U)

        @block.gpsimd
        def _(pool):
            for k in range(NBUF):
                nc.gpsimd.memset(qs[k][:, :, :], 0.0).then_inc(cleared, 1)
                nc.gpsimd.memset(ks[k][:, :], 0.0).then_inc(cleared, 1)
            pool.wait_ge(cleared, 2 * NBUF)
            for k in range(NBUF):
                nc.gpsimd.memset(ks[k][96:128, :], 1.0).then_inc(init, 1)
            if l == 0:
                pool.wait_ge(init, NBUF)
                nc.gpsimd.memset(zero[:, :], 0.0).then_inc(cleared, 1)
                pool.wait_ge(cleared, 2 * NBUF + 1)
                for dst in (mem.xs_d, mem.ys_d):
                    nc.gpsimd.dma_start(dst[0:1, :], zero[0:1, 0:C]).then_inc(mem.zeroed, 16)
                slots_d = mem.xs_d[1:1 + SLOTS[0], :].rearrange("(n p r) c -> n p (r c)", n=U * QB, p=P)
                with nc.gpsimd.Fori(0, U * QB) as n:
                    pool.wait_ge(pv_done, n + 1)
                    nc.gpsimd.dma_start(slots_d[bass.ds(n, 1)].rearrange("n p x -> (n p) x"), zero[:, :]).then_inc(mem.zeroed, 16)
                pool.wait_ge(mem.zeroed, mem.zero_count)

        @block.scalar
        def _(sc):
            def evacuate(u, fresh):
                sc.wait_ge(pv_done, u * QB + QB)
                if not fresh:
                    sc.wait_ge(o_turned, u)
                nc.scalar.activation(oT[:, :], pv[:, :], ACT.Copy).then_inc(evac, 1)

            def slot(u, it, k, first, last):
                for s in range(QB):
                    g = u * QB + s
                    lo, hi = cols(s)
                    if not (first and k == 0 and s < 2):
                        sc.wait_ge(pv_done, g - 1)
                    for pair in range(2):
                        sc.wait_ge(st_done, g * 2 + pair + 1)
                        nc.scalar.activation(pt[:, s % 2, 2 * pair:2 * pair + 2, lo:hi], st[:, 2 * pair:2 * pair + 2, lo:hi],
                                             ACT.Exp, scale=scale).then_inc(exp_done, 1)
                    if s == 0 and not (first and k == 0):
                        evacuate(u - 1, first and k == 1)
            slots(nc.scalar, slot)
            evacuate(U - 1, False)

        @block.vector
        def _(v):
            V = nc.vector

            def reduce_max(vu, k, s, j):
                w = (s + 1) * P if causal else S
                v.wait_ge(mx_done, vu * 16 + s * 4 + j + 1)
                V.tensor_reduce(negmax[:, k % 2, j, s:s + 1], side[:, score_pos(s, j) % 3, 0:w],
                                axis=AX.X, op=ALU.max, negate=True).then_inc(items, 1)

            def split_max(u, it, k, fresh):
                m = side[0:16, TURN_MAX % 3, 0:P]
                v.wait_ge(m_turned, u + 1)
                if not fresh:
                    kp, ip = (k - 1) % NBUF, it - (1 if k == 0 else 0)
                    v.wait_ge(mrow[kp], ip * 48 + 48)
                do = Chain(v, own, u * 3)
                do(V.tensor_copy(mparts[:, 0, :], m))
                do(V.tensor_tensor(mrest[:, :], m, mparts[:, 0, :], ALU.subtract))
                do(V.tensor_copy(mparts[:, 1, :], mrest[:, :]))
                V.tensor_tensor(mparts[:, 2, :], mrest[:, :], mparts[:, 1, :], ALU.subtract).then_inc(items, 1)

            def finish(u, it, k, early):
                v.wait_ge(o_turned, u + 1)
                if not early:
                    v.wait_ge(o_stored[k % 2], it * 32 + 16 * (k // 2))
                t4 = side[:, TURN_OUT % 3, :].rearrange("p (i j w) -> p i j w", i=QB, w=VW)
                V.reciprocal(rsum[:, :, :], t4[:, :, :, D]).then_inc(quotients, 1)
                v.wait_ge(quotients, u + 1)
                V.tensor_tensor(o_out[:, k % 2], t4[:, :, :, 0:D],
                                rsum[:, :, :].unsqueeze(3).to_broadcast([P, QB, 4, D]), ALU.mult).then_inc(items, 1)

            def none(n, count=1):
                v.wait_ge(items, n)
                V.sem_inc(items, count)

            def slot(u, it, k, first, last, lead=False):
                k1, i1 = ahead(it, k, 1)
                k2, i2 = ahead(it, k, 2)
                for s in range(QB):
                    if not (last and k >= NBUF - 2):
                        for j in range(4):
                            reduce_max(u + 2, k2, s, j)
                    else:
                        none(item(u, score_pos(s, 0)), 4)
                    if s == 0:
                        if (lead and u == -2) or (last and k == NBUF - 1):
                            none(item(u, TURN_MAX))
                        else:
                            split_max(u + 1, 0 if lead else i1, 0 if lead else k1, lead)
                    if s == 2:
                        if lead or (first and k == 0):
                            none(item(u, TURN_OUT))
                        else:
                            finish(u - 1, it - (1 if k == 0 else 0), (k - 1) % NBUF, first and k < 3)
            for u in (-2, -1):
                slot(u, 0, u % NBUF, False, False, True)
            slots(V, slot)
            none(item(U, 0), TURN_OUT)
            finish(U - 1, NI - 1, NBUF - 1, False)

        @block.tensor
        def _(t):
            mm = nc.tensor.matmul

            def max_scores(vu, k, s, j, static):
                w = (s + 1) * P if causal else S
                n = item(vu - 2, score_pos(s, j))
                if not (static and n < 3):
                    t.wait_ge(items, n - 2)
                bank = score_pos(s, j) % 3
                last = mm(side[:, bank, 0:w], qs[k][0:MROW, j, s * P:(s + 1) * P], ks[k][0:MROW, 0:w], start=True, stop=not causal)
                if causal:
                    last = mm(side[:, bank, s * P:w], mem.identb[:, :], mem.mask_q[:, :], start=False, stop=True)
                last.then_inc(mx_done, 1)

            def key_scores(u, k, s, pair, static):
                lo, hi = cols(s)
                g = u * QB + s
                if not (static and g < 1):
                    t.wait_ge(exp_done, g * 2 + pair - 1)
                for j in (2 * pair, 2 * pair + 1):
                    last = mm(st[:, j, lo:hi], ks[k][0:KROWS, s * P:(s + 1) * P], qs[k][0:KROWS, j, lo:hi], start=True, stop=not causal)
                    if causal:
                        last = mm(st[:, j, lo:lo + P], mem.identb[:, :], mem.mask_k[:, :], start=False, stop=True)
                last.then_inc(st_done, 1)

            def values(u, k, s):
                lo, hi = cols(s)
                t.wait_ge(exp_done, u * 2 * QB + 2 * s + 2)
                for j in range(4):
                    last = mm(pv[32 * j:32 * j + VW, lo:hi], vb[k][:, s, :], pt[:, s % 2, j, lo:hi], start=(s == 0), stop=(s == QB - 1))
                last.then_inc(pv_done, 1)

            def turn_max(u, k):
                t.wait_ge(items, item(u - 1, TURN_MAX) - 2)
                nc.tensor.transpose(side[0:16, TURN_MAX % 3, 0:P], negmax[:, k % 2].rearrange("p j s -> p (j s)"),
                                    mem.ident[:, :]).then_inc(m_turned, 1)

            def turn_out(u):
                t.wait_ge(evac, u + 1)
                t.wait_ge(items, item(u + 1, TURN_OUT) - 2)
                for i in range(QB):
                    last = nc.tensor.transpose(side[:, TURN_OUT % 3, i * P:(i + 1) * P], oT[:, i * P:(i + 1) * P], mem.ident[:, :])
                last.then_inc(o_turned, 1)

            for vu in range(2):
                t.wait_ge(ld[vu], 48)
                for s in range(QB):
                    for j in range(4):
                        max_scores(vu, vu, s, j, True)
                    if vu == 1 and s == 0:
                        turn_max(0, 0)
            t.wait_ge(mrow[0], 48)
            for pair in range(2):
                key_scores(0, 0, 0, pair, True)

            def slot(u, it, k, first, last):
                k1, i1 = ahead(it, k, 1)
                k2, i2 = ahead(it, k, 2)
                ahead_max = not (last and k >= NBUF - 2)
                ahead_keys = not (last and k == NBUF - 1)
                for s in range(QB):
                    if ahead_max:
                        if s == 0:
                            t.wait_ge(ld[k2], i2 * 48 + 48)
                        max_scores(u + 2, k2, s, 0, False)
                    if s == QB - 1 and ahead_keys:
                        t.wait_ge(mrow[k1], i1 * 48 + 48)
                    for pair in range(2):
                        if s < QB - 1:
                            key_scores(u, k, s + 1, pair, False)
                        elif ahead_keys:
                            key_scores(u + 1, k1, 0, pair, False)
                        if ahead_max:
                            max_scores(u + 2, k2, s, 1 + pair, False)
                    if s == 0 and not (first and k == 0):
                        t.wait_ge(evac, u)
                    values(u, k, s)
                    if ahead_max:
                        max_scores(u + 2, k2, s, 3, False)
                    if s == 0 and not (last and k == NBUF - 1):
                        turn_max(u + 1, k1)
                    if s == 2 and not (first and k == 0):
                        turn_out(u - 1)
            slots(nc.tensor, slot)
            turn_out(U - 1)


def after_attention(nc, mem, l, x_src):
    G, D = ATT[l]["g"], ATT[l]["d"]
    E = MOE[l]["e"]
    router = mem.named["gwT"] if l == 0 else mem.named["rwT"]
    with ExitStack() as c:
        def sb(n, s, t):
            return c.enter_context(nc.sbuf_tensor(f"{n}_c{l}", s, t))

        def sem(n):
            return mem.sem(f"c{l}_{n}")
        x4 = sb("x4", [P, 2, QB, C], F32)
        att = sb("att", [P, 2, G, QB, 4 * D], F32)
        amem = sb("amem", [P, 2, QB, C], F32) if l == 1 else None
        gate = sb("gate", [P, 2, C], F32)
        rows = sb("rows", [P, 2, 2, C], F32)
        t4 = sb("t4", [P, QB, C], F32)
        x1 = sb("x1", [P, 2, QB, C], F32)
        stats = sb("stats", [P, QB, 6], F32)
        mark = sb("mark", [P, 1], F32)
        mv = sb("mv", [P, QB, 2], F32)
        rstd = sb("rstd", [P, QB], F32)
        half = sb("half", [P, QB], F32)
        xn = sb("xn", [P, 2, QB, C], F32)
        hrows = sb("hrows", [P, 2, QB, C], F32)
        hT = sb("hT", [P, 2, CC, S], F32)
        ex = sb("ex", [P, QB, E], F32)
        ps_t = c.enter_context(nc.psum_tensor(f"ps_t_c{l}", [P, CC, 512], F32))
        ps_l = c.enter_context(nc.psum_tensor(f"ps_l_c{l}", [P, 512], F32))
        own, added, x1_ok, var_ok, rstd_ok, xn_ok, turned, h_ok, hrow_ok, logit, ex_ok, score_ok, init = (
            sem(n) for n in ("own", "added", "x1", "var", "rstd", "xn", "turned", "h", "hrow", "logit", "ex", "score", "init"))
        x_in, x1_st, h_st, hT_st = ([sem(f"{n}{k}") for k in range(2)] for n in ("xin", "x1st", "hst", "hTst"))
        NL = 4 + l
        OWN = 3 if l == 0 else 5
        block = c.enter_context(nc.Block())

        @block.sync
        def _(sp):
            def load(b, k):
                sp.dma_start(x4[:, k], x_src[bass.ds(b, 1)].rearrange("a (i p) c -> (a p) i c", p=P)).then_inc(x_in[k], 16)
                sp.dma_start(att[:, k], mem.att_d[l][bass.ds(b, 1)].rearrange("b g p n -> (b p) g n")).then_inc(x_in[k], 16)
                if l == 1:
                    sp.dma_start(amem[:, k], mem.amem_d[bass.ds(b, 1)].rearrange("a (i p) c -> (a p) i c", p=P)).then_inc(x_in[k], 16)
                sp.dma_start(gate[:, k, :], mem.mod_d[l, bass.ds(b, 1), 2 * C:3 * C].rearrange("b n -> (b n)").partition_broadcast(P)).then_inc(x_in[k], 16)
                sp.dma_start(rows[:, k].rearrange("p a n -> p (a n)"),
                             mem.mod_d[l, bass.ds(b, 1), 3 * C:5 * C].rearrange("b n -> (b n)").partition_broadcast(P)).then_inc(x_in[k], 16)
            for k in range(2):
                load(k, k)

            def body(b, i, k, last):
                sp.wait_ge(x1_ok, b + 1)
                sp.dma_start(mem.base_d[bass.ds(b, 1)].rearrange("b (i p) c -> (b p) i c", p=P), x1[:, k]).then_inc(x1_st[k], 16)
                sp.wait_ge(hrow_ok, b * 2 + 2)
                sp.dma_start(mem.h_d[bass.ds(b, 1)].rearrange("b (i p) c -> (b p) i c", p=P), hrows[:, k]).then_inc(h_st[k], 16)
                if not (isinstance(b, int) and b + 2 >= B):
                    load(b + 2, k)
                sp.wait_ge(h_ok, b * CC + CC)
                sp.dma_start(mem.hT_d[bass.ds(b, 1)].rearrange("b p n -> (b p) n"), hT[:, k].rearrange("p c s -> p (c s)")).then_inc(hT_st[k], 16)
            batches(nc.sync, body)
            for k in range(2):
                for st in (x1_st, h_st, hT_st):
                    sp.wait_ge(st[k], B // 2 * 16)

        @block.gpsimd
        def _(pool):
            g = nc.gpsimd
            g.memset(half[:, :], -0.5).then_inc(init, 1)
            pool.wait_ge(init, 1)

            def root(b):
                pool.wait_ge(var_ok, b + 1)
                g.tensor_tensor(rstd[:, :], mv[:, :, 1], half[:, :], ALU.pow).then_inc(rstd_ok, 1)
            root(0)

            def body(b, i, k, last):
                pool.wait_ge(rstd_ok, b + 1)
                pool.wait_ge(xn_ok, b * QB + QB)
                pool.wait_ge(x_in[k], (i + 1) * 16 * NL)
                wait_after(pool, h_st[k], i * 16)
                g.tensor_tensor(hrows[:, k], xn[:, k], rows[:, k, 1, :].unsqueeze(1).to_broadcast([P, QB, C]), ALU.mult).then_inc(hrow_ok, 1)
                pool.wait_ge(hrow_ok, b * 2 + 1)
                g.tensor_tensor(hrows[:, k], hrows[:, k], rows[:, k, 0, :].unsqueeze(1).to_broadcast([P, QB, C]), ALU.add).then_inc(hrow_ok, 1)
                if not last:
                    pool.wait_ge(hrow_ok, b * 2 + 2)
                    root(b + 1)
            batches(g, body)

        @block.vector
        def _(v):
            V = nc.vector

            def add_normalise(b, i, k):
                do = Chain(v, own, b * OWN)
                v.wait_ge(x_in[k], (i + 1) * 16 * NL)
                wait_after(v, x1_st[k], i * 16)
                if l == 0:
                    for t in range(QB):
                        last = V.tensor_tensor(t4[:, t, :].rearrange("p (g n) -> p g n", g=G), att[:, k, :, t, :],
                                               gate[:, k, :].rearrange("p (g n) -> p g n", g=G), ALU.mult)
                    do(last)
                else:
                    do(V.tensor_scalar(att[:, k], att[:, k], mem.wmem[:, 1:2], None, ALU.mult))
                    for t in range(QB):
                        last = V.tensor_tensor(t4[:, t, :].rearrange("p (j g d) -> p j g d", j=4, g=G),
                                               att[:, k, :, t, :].rearrange("p g (j d) -> p j g d", j=4),
                                               amem[:, k, t, :].rearrange("p (j g d) -> p j g d", j=4, g=G), ALU.add)
                    do(last)
                    do(V.tensor_tensor(t4[:, :, :], t4[:, :, :], gate[:, k, :].unsqueeze(1).to_broadcast([P, QB, C]), ALU.mult))
                V.tensor_tensor(x1[:, k], x4[:, k], t4[:, :, :], ALU.add).then_inc(x1_ok, 1)
                v.wait_ge(x1_ok, b + 1)
                for t in range(QB):
                    last = V.bn_stats(stats[:, t, :], x1[:, k, t, :])
                do(last)
                V.memset(mark[:, :], 0.0)
                for t in range(QB):
                    last = V.bn_aggr(mv[:, t, :], stats[:, t, :])
                do(last)
                V.tensor_scalar(mv[:, :, 1], mv[:, :, 1], EPS, None, ALU.add).then_inc(var_ok, 1)
                v.wait_ge(rstd_ok, b + 1)
                wait_after(v, hrow_ok, b * 2 - 3)
                for t in range(QB):
                    V.tensor_scalar(xn[:, k, t, :], x1[:, k, t, :], mv[:, t, 0:1], rstd[:, t:t + 1],
                                    ALU.subtract, ALU.mult).then_inc(xn_ok, 1)

            def modulate(b, i, k):
                wait_after(v, logit, b - 1)
                wait_after(v, hT_st[k], i * 16)
                for cc in range(CC):
                    v.wait_ge(turned, b * CC + cc + 1)
                    V.tensor_scalar(hT[:, k, cc, :], ps_t[:, cc, :], mem.modT[:, l, 8 + cc, bass.ds(b, 1)],
                                    mem.modT[:, l, 6 + cc, bass.ds(b, 1)], ALU.mult, ALU.add).then_inc(h_ok, 1)

            def score(b):
                do = Chain(v, added, b)
                v.wait_ge(ex_ok, b + 1)
                do(V.tensor_scalar(ex[:, :, :], ex[:, :, :], 1.0, None, ALU.add))
                V.reciprocal(mem.scores[:, bass.ds(b * QB, QB), 0:E], ex[:, :, :]).then_inc(score_ok, 1)
            add_normalise(0, 0, 0)

            def body(b, i, k, last):
                if not last:
                    add_normalise(b + 1, i + k, 1 - k)
                modulate(b, i, k)
                if not (isinstance(b, int) and b == 0):
                    score(b - 1)
            batches(V, body)
            score(B - 1)

        @block.scalar
        def _(s):
            def body(b, i, k, last):
                s.wait_ge(logit, b + 1)
                wait_after(s, score_ok, b)
                nc.scalar.activation(ex[:, :, :], ps_l[:, 0:QB * E].rearrange("p (i e) -> p i e", e=E), ACT.Exp, scale=-1.0).then_inc(ex_ok, 1)
            batches(nc.scalar, body)

        @block.tensor
        def _(t):
            def turn(b, k):
                t.wait_ge(xn_ok, b * QB + QB)
                for cc in range(CC):
                    for i in range(QB):
                        last = nc.tensor.transpose(ps_t[:, cc, i * P:(i + 1) * P], xn[:, k, i, cc * P:(cc + 1) * P], mem.ident[:, :])
                    last.then_inc(turned, 1)
            turn(0, 0)

            def body(b, i, k, final):
                t.wait_ge(h_ok, b * CC + CC)
                if not final:
                    turn(b + 1, 1 - k)
                wait_after(t, ex_ok, b)
                for i in range(QB):
                    for cc in range(CC):
                        last = nc.tensor.matmul(ps_l[:, i * E:(i + 1) * E], hT[:, k, cc, i * P:(i + 1) * P], router[:, cc, :],
                                                start=(cc == 0), stop=(cc == CC - 1))
                last.then_inc(logit, 1)
            batches(nc.tensor, body)


def spread_first(l):
    return NT * MOE[l]["e"] // (QB * C)


def spread_tile(nc, mem, l, i, rows, sent):
    for k in range(MOE[l]["k"]):
        nc.gpsimd.indirect_dma_start(out=mem.xs_d[0:SLOTS[l] + 1, :],
                                     out_offset=bass.IndirectOffsetOnAxis(ap=mem.sidx[:, i, k:k + 1], axis=0),
                                     in_=rows, in_offset=None,
                                     bounds_check=SLOTS[l], oob_is_err=False).then_inc(sent, 16)


def routing(nc, mem, l):
    m = MOE[l]
    E, N, K, GS = m["e"], m["n"], m["k"], m["e"] // m["n"]
    with ExitStack() as c:
        def sb(n, s, t=F32):
            return c.enter_context(nc.sbuf_tensor(f"{n}_d{l}", s, t))

        def sem(n):
            return mem.sem(f"d{l}_{n}")
        area = [sb(f"area{k}", [P, NT * max(E, N * N)]) for k in range(4)]

        def by_expert(k):
            return area[k][:, 0:NT * E].rearrange("p (t e) -> p t e", e=E)

        def by_pairs(k):
            return area[k][:, 0:NT * N * N].rearrange("p (t n m) -> p t n m", n=N, m=N)
        biased = sb("biased", [P, NT, E])
        hi, lo = ([area[k][:, a:a + NT * E // 2].rearrange("p (n s) -> p n s", s=GS // 2) for k in range(2)]
                  for a in (0, NT * E // 2))
        gsum = sb("gsum", [P, NT, N])
        cmp, eqs = by_pairs(2), by_pairs(3)
        lower = sb("lower", [P, N, N])
        kept = sb("kept", [P, NT, N])
        kth = sb("kth", [P, NT, 8])
        scan = [by_expert(0), by_expert(1)]
        sel, w = by_expert(2), by_expert(3)
        selb = sb("selb", [P, NT, E], BF16)
        cnt = sb("cnt", [P, NT])
        ebase = sb("ebase", [P, 3, E])
        ebase_i = sb("ebase_i", [P, E], I32)
        tix = sb("tix", [P, 2])
        tcmp = sb("tcmp", [P, 2, E])
        eid = sb("eid", [P, 2])
        word = sb("word", [P, 2])
        eid_i = sb("eid_i", [P, 2], I32)
        idx = sb("idx", [P, NT, 8])
        skip = area[2][:, 0:NT * 8].rearrange("p (t k) -> p t k", k=8)
        ps_p = c.enter_context(nc.psum_tensor(f"ps_p_d{l}", [P, NT * E], F32))
        ps_n = c.enter_context(nc.psum_tensor(f"ps_n_d{l}", [P, NT * E], F32))
        FIRST = spread_first(l)
        hb = biased[:, :, :].rearrange("p t e -> p (t e)")[:, 0:FIRST * QB * C].rearrange("p (n c) -> p n c", c=C)
        own, init, picked, counted, listed, eid_ok, eid_st, h_in, sent = (
            sem(n) for n in ("own", "init", "picked", "counted", "listed", "eid", "eidst", "h", "sent"))
        block = c.enter_context(nc.Block())

        @block.scalar
        def _(s):
            if l == 0:
                w1_d = mem.A["L0_ffn_w1_experts"].rearrange("e (c p) i -> p e c i", p=P)
                w2_d = mem.A["L0_ffn_w2_experts"].rearrange("e i c -> i e c")
                for e in range(0, E, 8):
                    for cc in range(CC):
                        s.dma_start(mem.w1[:, e:e + 8, cc, :], w1_d[:, e:e + 8, cc, :]).then_inc(mem.w_in, 16)
                    s.dma_start(mem.w2[:, e:e + 8, :], w2_d[:, e:e + 8, :]).then_inc(mem.w_in, 16)

        @block.gpsimd
        def _(pool):
            g = nc.gpsimd
            g.memset(lower[:, :, :], 1.0).then_inc(init, 1)
            pool.wait_ge(init, 1)
            g.affine_select(out=lower[:, :, :], in_=lower[:, :, :], compare_op=ALU.is_gt, fill=0.0, base=0,
                            pattern=[[1, N], [-1, N]], channel_multiplier=0).then_inc(init, 1)
            g.iota(tix[:, :], pattern=[[P, 2]], base=0, channel_multiplier=1, allow_small_or_imprecise_dtypes=True).then_inc(init, 1)
            g.iota(ebase[:, 0, :], pattern=[[m["cap"] or 0, E]], base=0, channel_multiplier=0, allow_small_or_imprecise_dtypes=True).then_inc(init, 1)
            pool.wait_ge(listed, 1)
            pool.wait_ge(h_in, 16 * FIRST)
            for i in range(FIRST * QB):
                spread_tile(nc, mem, l, i, hb[:, i, :], sent)
            pool.wait_ge(sent, 16 * K * FIRST * QB)

        @block.sync
        def _(sp):
            sp.wait_ge(picked, 1)
            for b in range(FIRST):
                sp.dma_start(hb[:, b * QB:(b + 1) * QB, :], mem.h_d[b].rearrange("(i p) c -> p i c", p=P)).then_inc(h_in, 16)
            if l == 0:
                sp.wait_ge(eid_ok, 1)
                sp.dma_start(mem.eid_d.rearrange("(h p) -> p h", p=P), eid_i[:, :], allow_slow_non_contiguous=True).then_inc(eid_st, 16)
                sp.wait_ge(eid_st, 16)

        @block.vector
        def _(v):
            V = nc.vector
            TT, TS = V.tensor_tensor, V.tensor_scalar
            do = Chain(v, own)
            sc = mem.scores[:, :, 0:E]
            do(TT(biased[:, :, :], sc, mem.gbias[l][:, :].unsqueeze(1).to_broadcast([P, NT, E]), ALU.add))
            grp = biased[:, :, :].rearrange("p t (n s) -> p (t n) s", n=N)
            h = GS // 2
            do(TT(hi[0][:, :, :], grp[:, :, 0:h], grp[:, :, h:], ALU.max))
            do(TT(lo[0][:, :, :], grp[:, :, 0:h], grp[:, :, h:], ALU.min))
            a = 0
            while h > 1:
                q = h // 2
                H, L = hi[a], lo[a]
                do(TT(hi[1 - a][:, :, 0:q], H[:, :, 0:q], H[:, :, q:h], ALU.max))
                do(TT(lo[1 - a][:, :, 0:q], H[:, :, 0:q], H[:, :, q:h], ALU.min))
                do(TT(L[:, :, 0:q], L[:, :, 0:q], L[:, :, q:h], ALU.max))
                do(TT(lo[1 - a][:, :, 0:q], lo[1 - a][:, :, 0:q], L[:, :, 0:q], ALU.max))
                h, a = q, 1 - a
            gs = gsum[:, :, :]
            do(TT(gs.rearrange("p t n -> p (t n)"), hi[a][:, :, 0], lo[a][:, :, 0], ALU.add))
            v.wait_ge(init, 4)
            other, this = gs.unsqueeze(2).to_broadcast([P, NT, N, N]), gs.unsqueeze(3).to_broadcast([P, NT, N, N])
            do(TT(cmp[:, :, :, :], other, this, ALU.is_gt))
            do(TT(eqs[:, :, :, :], other, this, ALU.is_equal))
            do(TT(eqs[:, :, :, :], eqs[:, :, :, :], lower[:, :, :].unsqueeze(1).to_broadcast([P, NT, N, N]), ALU.mult))
            do(TT(cmp[:, :, :, :], cmp[:, :, :, :], eqs[:, :, :, :], ALU.add))
            do(V.tensor_reduce(kept[:, :, :], cmp[:, :, :, :], axis=AX.X, op=ALU.add))
            do(TS(kept[:, :, :], kept[:, :, :], float(m["kg"]), None, ALU.is_lt))
            kb = kept[:, :, :].rearrange("p t n -> p (t n)").unsqueeze(2).to_broadcast([P, NT * N, GS])
            if l == 0:
                do(TS(kept[:, :, :], kept[:, :, :], -1.0, 1.0e30, ALU.add, ALU.mult))
                do(TT(grp, grp, kb, ALU.add))
            else:
                do(TT(grp, grp, kb, ALU.mult))
                do(TS(grp, grp, 0.0, None, ALU.add))
            for i in range(NT):
                last = V.max(kth[:, i, :], biased[:, i, :])
            do(last)
            kv = kth[:, :, K - 1].unsqueeze(2).to_broadcast([P, NT, E])
            do(TT(sel[:, :, :], biased[:, :, :], kv, ALU.is_gt))
            do(TT(scan[0][:, :, :], biased[:, :, :], kv, ALU.is_equal))
            do(TT(w[:, :, :], biased[:, :, :], kv, ALU.is_equal))
            do(V.tensor_reduce(cnt[:, :], sel[:, :, :], axis=AX.X, op=ALU.add))
            a, sh = 0, 1
            while sh < E:
                do(V.tensor_copy(scan[1 - a][:, :, 0:sh], scan[a][:, :, 0:sh]))
                do(TT(scan[1 - a][:, :, sh:], scan[a][:, :, sh:], scan[a][:, :, 0:E - sh], ALU.add))
                a, sh = 1 - a, 2 * sh
            do(TT(scan[a][:, :, :], scan[a][:, :, :], cnt[:, :].unsqueeze(2).to_broadcast([P, NT, E]), ALU.add))
            do(TS(scan[a][:, :, :], scan[a][:, :, :], float(K), None, ALU.is_le))
            do(TT(w[:, :, :], w[:, :, :], scan[a][:, :, :], ALU.mult))
            do(TT(sel[:, :, :], sel[:, :, :], w[:, :, :], ALU.add))
            V.tensor_copy(selb[:, :, :], sel[:, :, :]).then_inc(picked, 1)
            do(TT(w[:, :, :], sc, sel[:, :, :], ALU.mult))
            do(V.tensor_reduce(cnt[:, :], w[:, :, :], axis=AX.X, op=ALU.add))
            do(TS(cnt[:, :], cnt[:, :], 1e-20, None, ALU.add))
            do(V.reciprocal(cnt[:, :], cnt[:, :]))
            do(TT(w[:, :, :], w[:, :, :], cnt[:, :].unsqueeze(2).to_broadcast([P, NT, E]), ALU.mult))
            do(TS(w[:, :, :], w[:, :, :], m["scale"], None, ALU.mult))
            v.wait_ge(counted, 2)
            tot = ps_n[:, :].rearrange("p (t e) -> p t e", e=E)
            do(V.tensor_copy(scan[0][:, :, :], tot))
            a, sh = 0, 1
            while sh < NT:
                do(V.tensor_copy(scan[1 - a][:, 0:sh, :], scan[a][:, 0:sh, :]))
                do(TT(scan[1 - a][:, sh:, :], scan[a][:, sh:, :], scan[a][:, 0:NT - sh, :], ALU.add))
                a, sh = 1 - a, 2 * sh
            slot, incl = scan[1 - a], scan[a]
            do(TT(slot[:, :, :], incl[:, :, :], tot, ALU.subtract))
            do(TT(slot[:, :, :], slot[:, :, :], ps_p[:, :].rearrange("p (t e) -> p t e", e=E), ALU.add))
            if l == 0:
                do(TS(ebase_i[:, :], incl[:, NT - 1, :], float(P - 1), None, ALU.add))
                do(TS(ebase_i[:, :], ebase_i[:, :], 7, None, ALU.arith_shift_right))
                do(V.tensor_copy(ebase[:, 0, :], ebase_i[:, :]))
                do(V.tensor_copy(ebase[:, 1, :], ebase[:, 0, :]))
                e, sh = 1, 1
                while sh < E:
                    do(V.tensor_copy(ebase[:, 3 - e, 0:sh], ebase[:, e, 0:sh]))
                    do(TT(ebase[:, 3 - e, sh:], ebase[:, e, sh:], ebase[:, e, 0:E - sh], ALU.add))
                    e, sh = 3 - e, 2 * sh
                do(TT(ebase[:, 0, :], ebase[:, e, :], ebase[:, 0, :], ALU.subtract))
                do(TS(ebase[:, 0, :], ebase[:, 0, :], float(P), None, ALU.mult))
            else:
                do(TS(incl[:, :, :], slot[:, :, :], float(m["cap"]), None, ALU.is_lt))
                do(TT(sel[:, :, :], sel[:, :, :], incl[:, :, :], ALU.mult))
                do(TT(w[:, :, :], w[:, :, :], incl[:, :, :], ALU.mult))
            do(TT(slot[:, :, :], slot[:, :, :], ebase[:, 0, :].unsqueeze(1).to_broadcast([P, NT, E]), ALU.add))
            do(TS(slot[:, :, :], slot[:, :, :], 1.0, None, ALU.add))
            do(TT(slot[:, :, :], slot[:, :, :], sel[:, :, :], ALU.mult))
            for i in range(NT):
                last = V.max(idx[:, i, :], slot[:, i, :])
            do(last)
            do(V.tensor_copy(mem.gidx[:, :, :], idx[:, :, :]))
            do(TS(skip[:, :, :], idx[:, :, :], 0.0, 1.0e6, ALU.is_equal, ALU.mult))
            do(TT(skip[:, :, :], skip[:, :, :], idx[:, :, :], ALU.add))
            V.tensor_copy(mem.sidx[:, :, :], skip[:, :, :]).then_inc(listed, 1)
            if l == 0:
                for j in range(4):
                    for n in range(2):
                        last = TT(tcmp[:, n, :], ebase[:, e, :], tix[:, n:n + 1].to_broadcast([P, E]), ALU.is_le)
                    do(last)
                    do(V.tensor_reduce(eid[:, :], tcmp[:, :, :], axis=AX.X, op=ALU.add))
                    do(TS(eid[:, :], eid[:, :], float(E - 1), float(E ** j), ALU.min, ALU.mult))
                    do(V.tensor_copy(word[:, :], eid[:, :]) if j == 0 else TT(word[:, :], word[:, :], eid[:, :], ALU.add))
                    do(TS(tix[:, :], tix[:, :], 1.0, None, ALU.add))
                V.tensor_copy(eid_i[:, :], word[:, :]).then_inc(eid_ok, 1)
            for k in range(K):
                do(TT(incl[:, :, :], slot[:, :, :], idx[:, :, k].unsqueeze(2).to_broadcast([P, NT, E]), ALU.is_equal))
                do(TT(incl[:, :, :], incl[:, :, :], w[:, :, :], ALU.mult))
                do(V.tensor_reduce(mem.wk[:, :, k], incl[:, :, :], axis=AX.X, op=ALU.add))

        @block.tensor
        def _(t):
            t.wait_ge(picked, 1)
            flat = selb[:, :, :].rearrange("p t e -> p (t e)")
            for ps, left in ((ps_p, mem.before), (ps_n, mem.onesb)):
                for n in range(0, NT * E, 512):
                    last = nc.tensor.matmul(ps[:, n:n + 512], left[:, :], flat[:, n:n + 512], start=True, stop=True)
                last.then_inc(counted, 1)


def spread_and_share(nc, mem, l):
    K = MOE[l]["k"]
    HC = 4 if l == 0 else 2
    NP = HC if l == 0 else 2
    FIRST = spread_first(l)
    done = [sum(b % 2 == k for b in range(FIRST)) for k in range(2)]
    with ExitStack() as c:
        def sb(n, s, t=F32):
            return c.enter_context(nc.sbuf_tensor(f"{n}_g{l}", s, t))

        def sem(n):
            return mem.sem(f"g{l}_{n}")
        hb = sb("hb", [P, 2, QB, C])
        hT = sb("hT", [P, 2, CC, S])
        base = sb("base", [P, 2, QB, C])
        gate = sb("gate", [P, 2, C])
        gated = sb("gated", [P, QB, C])
        hid = sb("hid", [P, HC, S])
        sig = sb("sig", [P, 2, S])
        if l == 0:
            up = sb("up", [P, CC, 512])
            down = sb("down", [P, 4, C])
        else:
            up, down = mem.named["suT"], mem.named["sdT"]
            gu = sb("gu", [P, 4, S])
            taken = sem("taken")
        ps_u = c.enter_context(nc.psum_tensor(f"ps_u_g{l}", [P, 4, 512], F32))
        ps_d = c.enter_context(nc.psum_tensor(f"ps_d_g{l}", [P, 2, 512], F32))
        w_in, own, hid_ps, act_ok, exp_ok, hid_ok, down_ps, base_ok = (
            sem(n) for n in ("w", "own", "hidps", "act", "exp", "hid", "down", "base"))
        h_in, sent, hT_in, x_in, base_st = ([sem(f"{n}{k}") for k in range(2)] for n in ("h", "sent", "hT", "x", "basest"))
        block = c.enter_context(nc.Block())

        def rows_of(tensor, b):
            return tensor[bass.ds(b, 1)].rearrange("b (i p) c -> (b p) i c", p=P)

        @block.sync
        def _(sp):
            def load_h(b, k):
                sp.dma_start(hb[:, k], rows_of(mem.h_d, b)).then_inc(h_in[k], 16)

            def load_hT(b, k):
                sp.dma_start(hT[:, k].rearrange("p c s -> p (c s)"), mem.hT_d[bass.ds(b, 1)].rearrange("b p n -> (b p) n")).then_inc(hT_in[k], 16)

            def load_x(b, k):
                sp.dma_start(base[:, k], rows_of(mem.base_d, b)).then_inc(x_in[k], 16)
                sp.dma_start(gate[:, k], mem.mod_d[l, bass.ds(b, 1), 5 * C:6 * C].rearrange("b n -> (b n)").partition_broadcast(P)).then_inc(x_in[k], 16)
            for b in (FIRST, FIRST + 1):
                load_h(b, b % 2)
            if l == 0:
                sp.dma_start(up[:, :, :], mem.A["L0_ffn_w_up_shared"].rearrange("(c p) n -> p c n", p=P)).then_inc(w_in, 16)
                sp.dma_start(down[:, :, :], mem.A["L0_ffn_w_down_shared"].rearrange("(c p) n -> p c n", p=P)).then_inc(w_in, 16)
            for k in range(2):
                load_hT(k, k)
                load_x(k, k)

            def body(b, i, k, last):
                more = not (isinstance(b, int) and b + 2 >= B)
                if more and not (isinstance(b, int) and b < FIRST):
                    sp.wait_ge(sent[k], (i + 1 - done[k]) * 16 * K * QB)
                    load_h(b + 2, k)
                if more:
                    sp.wait_ge(hid_ps, b * NP + NP)
                    load_hT(b + 2, k)
                sp.wait_ge(base_ok, b + 1)
                sp.dma_start(rows_of(mem.base_d, b), base[:, k]).then_inc(base_st[k], 16)
                if more:
                    sp.wait_ge(base_st[k], i * 16 + 16)
                    load_x(b + 2, k)
            batches(nc.sync, body)
            for k in range(2):
                sp.wait_ge(base_st[k], B // 2 * 16)

        @block.gpsimd
        def _(pool):
            for b in range(FIRST, B):
                pool.wait_ge(h_in[b % 2], 16 * (b // 2 + 1 - done[b % 2]))
                for t in range(QB):
                    spread_tile(nc, mem, l, b * QB + t, hb[:, b % 2, t, :], sent[b % 2])
            for k in range(2):
                pool.wait_ge(sent[k], 16 * K * QB * (B // 2 - done[k]))

        @block.vector
        def _(v):
            V = nc.vector
            OWN = 1 if l == 0 else 3

            def body(b, i, k, last):
                do = Chain(v, own, b * OWN)
                if l == 0:
                    for h in range(HC):
                        v.wait_ge(act_ok, b * HC + h + 1)
                        V.tensor_tensor(hid[:, h, :], sig[:, h % 2, :], sig[:, h % 2, :], ALU.mult).then_inc(hid_ok, 1)
                else:
                    v.wait_ge(act_ok, b + 1)
                    do(V.reciprocal(sig[:, :, :], sig[:, :, :]))
                    do(V.tensor_tensor(hid[:, :, :], gu[:, 0:2, :], sig[:, :, :], ALU.mult))
                    V.tensor_tensor(hid[:, :, :], hid[:, :, :], gu[:, 2:4, :], ALU.mult).then_inc(hid_ok, 1)
                v.wait_ge(down_ps, b + 1)
                v.wait_ge(x_in[k], i * 32 + 32)
                do(V.tensor_tensor(gated[:, :, :], ps_d[:, :, :].rearrange("p a (i c) -> p (a i) c", c=C),
                                   gate[:, k, :].unsqueeze(1).to_broadcast([P, QB, C]), ALU.mult))
                V.tensor_tensor(base[:, k], gated[:, :, :], base[:, k], ALU.add).then_inc(base_ok, 1)
            batches(V, body)

        @block.scalar
        def _(s):
            A = nc.scalar.activation

            def body(b, i, k, last):
                if l == 0:
                    for h in range(HC):
                        s.wait_ge(hid_ps, b * HC + h + 1)
                        wait_after(s, hid_ok, b * HC + h - 1)
                        A(sig[:, h % 2, :], ps_u[:, h, :], ACT.Relu).then_inc(act_ok, 1)
                else:
                    s.wait_ge(hid_ps, b * 2 + 2)
                    wait_after(s, hid_ok, b)
                    A(sig[:, :, :], ps_u[:, 0:2, :], ACT.Exp, scale=-1.0).then_inc(exp_ok, 1)
                    A(gu[:, :, :], ps_u[:, :, :], ACT.Copy).then_inc(taken, 1)
                    s.wait_ge(exp_ok, b + 1)
                    s.wait_ge(taken, b + 1)
                    A(sig[:, :, :], sig[:, :, :], ACT.Copy, bias=1.0).then_inc(act_ok, 1)
            batches(nc.scalar, body)

        @block.tensor
        def _(t):
            mm = nc.tensor.matmul
            if l == 0:
                t.wait_ge(w_in, 32)
                parts = [[(h, up, h)] for h in range(HC)]
            else:
                sg = mem.named["sgT"]
                parts = [[(2, up, 0), (3, up, 1)], [(0, sg, 0), (1, sg, 1)]]

            def rise(b, i, k):
                t.wait_ge(hT_in[k], i * 16 + 16)
                wait_after(t, act_ok if l == 0 else taken, b * HC if l == 0 else b)
                for part in parts:
                    for bank, w, h in part:
                        for cc in range(CC):
                            op = mm(ps_u[:, bank, :], w[:, cc, h * P:(h + 1) * P], hT[:, k, cc, :], start=(cc == 0), stop=(cc == CC - 1))
                    op.then_inc(hid_ps, 1)
            rise(0, 0, 0)

            def body(b, i, k, last):
                if not last:
                    rise(b + 1, i + k, 1 - k)
                t.wait_ge(hid_ok, b * HC + HC if l == 0 else b + 1)
                wait_after(t, base_ok, b)
                for n in range(QB):
                    for h in range(HC):
                        op = mm(ps_d[:, n // 2, (n % 2) * C:(n % 2) * C + C], hid[:, h, n * P:(n + 1) * P], down[:, h, :],
                                start=(h == 0), stop=(h == HC - 1))
                op.then_inc(down_ps, 1)
            batches(nc.tensor, body)


def experts_any(nc, mem):
    TL, E = MOE[0]["tiles"], MOE[0]["e"]
    GT = 4
    NG, EBITS = TL // GT, E.bit_length() - 1
    assert TL % (2 * GT) == 0 and E == 1 << EBITS
    with ExitStack() as c:
        def sb(n, s, t=F32):
            return c.enter_context(nc.sbuf_tensor(f"{n}_e0", s, t))

        def sem(n):
            return mem.sem(f"e0_{n}")
        w1, w2 = mem.w1, mem.w2
        table = sb("table", [1, TL], I32)
        xin = sb("xin", [P, 2, GT, C])
        xT = sb("xT", [P, GT, C])
        r = sb("r", [P, GT, P])
        aT = sb("aT", [P, GT, P])
        y = sb("y", [P, 2, GT, C])
        ps_x = c.enter_context(nc.psum_tensor("ps_x_e0", [P, 2, 2, 256], F32))
        ps_h = c.enter_context(nc.psum_tensor("ps_h_e0", [P, 2, 4, P], F32))
        ps_r = c.enter_context(nc.psum_tensor("ps_r_e0", [P, 2, 4, P], F32))
        ps_y = c.enter_context(nc.psum_tensor("ps_y_e0", [P, 2, 2, 256], F32))
        x_in = [sem(f"x{k}") for k in range(2)]
        y_st = [sem(f"yst{k}") for k in range(2)]
        t_in, x_turned, xT_ok, h_ps, r_ok, r_turned, aT_ok, y_ps, y_ok = (
            sem(n) for n in ("t", "xturn", "xT", "h", "r", "rturn", "aT", "yps", "y"))
        block = c.enter_context(nc.Block())
        xs = mem.xs_d[1:1 + TL * P, :].rearrange("(g t p) c -> g p t c", t=GT, p=P)
        ys = mem.ys_d[1:1 + TL * P, :].rearrange("(g t p) c -> g p t c", t=GT, p=P)

        @block.sync
        def _(sp):
            sp.dma_start(table[:, :], mem.eid_d.rearrange("(a n) -> a n", a=1)).then_inc(t_in, 16)

            def load(g, k):
                sp.dma_start(xin[:, k], xs[bass.ds(g, 1)].rearrange("g p t c -> (g p) t c")).then_inc(x_in[k], 16)
            load(0, 0)
            load(1, 1)

            def body(g, i, k, last):
                if not (isinstance(g, int) and g + 2 >= NG):
                    sp.wait_ge(x_turned, g * 2 + 2)
                    load(g + 2, k)
                sp.wait_ge(y_ok, g * 2 + 2)
                sp.dma_start(ys[bass.ds(g, 1)].rearrange("g p t c -> (g p) t c"), y[:, k]).then_inc(y_st[k], 16)
            batches(nc.sync, body, NG)
            for k in range(2):
                sp.wait_ge(y_st[k], 16 * (NG // 2))

        @block.tensor
        def _(t):
            mm = nc.tensor.matmul

            def turn_x(k, h):
                for q in range(2):
                    for cc in range(CC):
                        op = nc.tensor.transpose(ps_x[:, h, q, cc * P:(cc + 1) * P], xin[:, k, 2 * h + q, cc * P:(cc + 1) * P], mem.ident[:, :])
                op.then_inc(x_turned, 1)

            def turn_r(h):
                for q in range(2):
                    op = nc.tensor.transpose(ps_r[:, h, q, :], r[:, 2 * h + q, :], mem.ident[:, :])
                op.then_inc(r_turned, 1)
            t.wait_ge(x_in[0], 16)
            for h in range(2):
                turn_x(0, h)
            t.wait_ge(t_in, 16)
            t.wait_ge(mem.w_in, 16 * 3 * (E // 8))

            def body(g, i, k, last):
                word = nc.tensor.value_load(table[0:1, bass.ds(g * GT, 1)], min_val=0, max_val=E ** GT - 1)

                def expert(n):
                    return (word >> (EBITS * n)) & (E - 1)
                for h in range(2):
                    t.wait_ge(xT_ok, g * 2 + h + 1)
                    for q in range(2):
                        e = expert(2 * h + q)
                        for cc in range(CC):
                            op = mm(ps_h[:, h, q, :], xT[:, 2 * h + q, cc * P:(cc + 1) * P], w1[:, bass.ds(e, 1), cc, :].rearrange("p e c -> p (e c)"),
                                    start=(cc == 0), stop=(cc == CC - 1))
                    op.then_inc(h_ps, 1)
                if not last:
                    t.wait_ge(x_in[1 - k], (i + k) * 16 + 16)
                for h in range(2):
                    if not last:
                        turn_x(1 - k, h)
                    t.wait_ge(r_ok, g * 2 + h + 1)
                    turn_r(h)
                for h in range(2):
                    t.wait_ge(aT_ok, g * 2 + h + 1)
                    wait_after(t, y_ok, g * 2 + h - 1)
                    for q in range(2):
                        e = expert(2 * h + q)
                        op = mm(ps_y[:, h, q, :], aT[:, 2 * h + q, :], w2[:, bass.ds(e, 1), :].rearrange("p e c -> p (e c)"), start=True, stop=True)
                    op.then_inc(y_ps, 1)
            batches(nc.tensor, body, NG)

        @block.vector
        def _(v):
            V = nc.vector

            def copy_x(g, h):
                v.wait_ge(x_turned, g * 2 + h + 1)
                wait_after(v, h_ps, g * 2 + h - 1)
                V.tensor_copy(xT[:, 2 * h:2 * h + 2, :], ps_x[:, h]).then_inc(xT_ok, 1)
            for h in range(2):
                copy_x(0, h)

            def body(g, i, k, last):
                if not last:
                    for h in range(2):
                        copy_x(g + 1, h)
                for h in range(2):
                    v.wait_ge(y_ps, g * 2 + h + 1)
                    if h == 0:
                        wait_after(v, y_st[k], i * 16)
                    V.tensor_copy(y[:, k, 2 * h:2 * h + 2, :], ps_y[:, h]).then_inc(y_ok, 1)
            batches(V, body, NG)

        @block.scalar
        def _(a):
            def body(g, i, k, last):
                for h in range(2):
                    a.wait_ge(h_ps, g * 2 + h + 1)
                    wait_after(a, r_turned, g * 2 + h - 1)
                    nc.scalar.activation(r[:, 2 * h:2 * h + 2, :], ps_h[:, h, 0:2, :], ACT.Relu).then_inc(r_ok, 1)
                for h in range(2):
                    a.wait_ge(r_turned, g * 2 + h + 1)
                    wait_after(a, y_ps, g * 2 + h - 1)
                    nc.scalar.activation(aT[:, 2 * h:2 * h + 2, :], ps_r[:, h, 0:2, :], ACT.Square).then_inc(aT_ok, 1)
            batches(nc.scalar, body, NG)


def experts_capped(nc, mem):
    E, CAP = MOE[1]["e"], MOE[1]["cap"]
    R2 = CAP - P
    with ExitStack() as c:
        def sb(n, s, t=F32):
            return c.enter_context(nc.sbuf_tensor(f"{n}_e1", s, t))

        def sem(n):
            return mem.sem(f"e1_{n}")
        NB = 4
        wgu = sb("wgu", [P, NB, 2, CC, P])
        wd = sb("wd", [P, NB, C])
        xa = sb("xa", [P, NB, C])
        xb = sb("xb", [P, NB, C])
        xT = sb("xT", [P, 2, CC, CAP])
        sig = sb("sig", [P, CAP])
        gu = sb("gu", [P, CAP])
        aT = sb("aT", [P, 2, CAP])
        y = sb("y", [P, 2, 2, C])
        ps_x = c.enter_context(nc.psum_tensor("ps_x_e1", [P, 2, 512], F32))
        ps_g = c.enter_context(nc.psum_tensor("ps_g_e1", [P, 2, 512], F32))
        ps_y = c.enter_context(nc.psum_tensor("ps_y_e1", [P, 2, 512], F32))
        ld = [sem(f"ld{k}") for k in range(NB)]
        y_st = [sem(f"yst{k}") for k in range(2)]
        own, x_turned, xT_ok, g_ps, sig_ok, a_ok, y_ps, y_ok = (sem(n) for n in ("own", "xturn", "xT", "g", "sig", "a", "yps", "y"))
        block = c.enter_context(nc.Block())
        xs = mem.xs_d[1:1 + E * CAP, :].rearrange("(e r) c -> e r c", r=CAP)
        ys = mem.ys_d[1:1 + E * CAP, :].rearrange("(e r) c -> e r c", r=CAP)
        A = mem.A

        def slots(engine, slot, lead=0):
            for k in range(4):
                slot(k, 0, k)
            with engine.Fori(1, E // 4 - 1) as it:
                for k in range(4):
                    slot(it * 4 + k, it, k)
            for k in range(6):
                slot(E - 4 + k, E // 4 - 1 + k // 4, k % 4)

        def stage(s, lag):
            return not isinstance(s, int) or 0 <= s - lag < E

        @block.sync
        def _(sp):
            def load(e, k):
                for n, w in ((0, "gate"), (1, "up")):
                    sp.dma_start(wgu[:, k, n, :, :], A[f"L1_ffn_W_{w}"][bass.ds(e, 1)].rearrange("e (c p) i -> (e p) c i", p=P)).then_inc(ld[k], 16)
                sp.dma_start(wd[:, k, :], A["L1_ffn_W_down"][bass.ds(e, 1)].rearrange("e i c -> (e i) c")).then_inc(ld[k], 16)
                sp.dma_start(xa[:, k, :], xs[bass.ds(e, 1), 0:P].rearrange("e r c -> (e r) c")).then_inc(ld[k], 16)
                sp.dma_start(xb[0:R2, k, :], xs[bass.ds(e, 1), P:CAP].rearrange("e r c -> (e r) c")).then_inc(ld[k], 16)
            for e in range(2):
                load(e, e)

            def slot(s, it, k):
                if not isinstance(s, int) or s + 2 < E:
                    if not (isinstance(s, int) and s < 2):
                        sp.wait_ge(y_ps, s - 1)
                    load(s + 2, (k + 2) % 4)
            slots(nc.sync, slot)

        @block.tensor
        def _(t):
            mm = nc.tensor.matmul

            def slot(s, it, k):
                if stage(s, 1):
                    q, b = (k - 1) % 2, (k - 1) % 4
                    t.wait_ge(xT_ok, s)
                    for n in range(2):
                        for cc in range(CC):
                            last = mm(ps_g[:, q, n * CAP:(n + 1) * CAP], wgu[:, b, n, cc, :], xT[:, q, cc, :], start=(cc == 0), stop=(cc == CC - 1))
                    last.then_inc(g_ps, 1)
                if stage(s, 0):
                    q = k % 2
                    t.wait_ge(ld[k], it * 80 + 80)
                    for cc in range(CC):
                        nc.tensor.transpose(ps_x[:, q, cc * CAP:cc * CAP + P], xa[:, k, cc * P:(cc + 1) * P], mem.ident[:, :])
                        last = nc.tensor.transpose(ps_x[:, q, cc * CAP + P:(cc + 1) * CAP], xb[0:R2, k, cc * P:(cc + 1) * P], mem.ident[0:R2, 0:R2])
                    last.then_inc(x_turned, 1)
                if stage(s, 2):
                    q, b = k % 2, (k - 2) % 4
                    t.wait_ge(a_ok, s - 1)
                    if not (isinstance(s, int) and s - 2 < 2):
                        t.wait_ge(y_ok, s - 3)
                    mm(ps_y[:, q, 0:C], aT[:, q, 0:P], wd[:, b, :], start=True, stop=True)
                    mm(ps_y[0:R2, q, C:2 * C], aT[:, q, P:CAP], wd[:, b, :], start=True, stop=True, skip_group_check=True).then_inc(y_ps, 1)
            slots(nc.tensor, slot)

        @block.vector
        def _(v):
            V = nc.vector

            def slot(s, it, k):
                if stage(s, 0):
                    v.wait_ge(x_turned, s + 1)
                    if not (isinstance(s, int) and s < 2):
                        v.wait_ge(g_ps, s - 1)
                    V.tensor_copy(xT[:, k % 2, :, :], ps_x[:, k % 2, 0:CC * CAP].rearrange("p (c n) -> p c n", n=CAP)).then_inc(xT_ok, 1)
                if stage(s, 1):
                    q = (k - 1) % 2
                    n = s - 1
                    v.wait_ge(sig_ok, s)
                    do = Chain(v, own, n * 3)
                    do(V.tensor_scalar(sig[:, :], sig[:, :], 1.0, None, ALU.add))
                    do(V.reciprocal(sig[:, :], sig[:, :]))
                    do(V.tensor_tensor(gu[:, :], ps_g[:, q, 0:CAP], sig[:, :], ALU.mult))
                    if not (isinstance(s, int) and n < 2):
                        v.wait_ge(y_ps, s - 2)
                    V.tensor_tensor(aT[:, q, :], gu[:, :], ps_g[:, q, CAP:2 * CAP], ALU.mult).then_inc(a_ok, 1)
            slots(V, slot)

        @block.scalar
        def _(a):
            def slot(s, it, k):
                if stage(s, 1):
                    q = (k - 1) % 2
                    a.wait_ge(g_ps, s)
                    if not (isinstance(s, int) and s - 1 < 1):
                        a.wait_ge(a_ok, s - 1)
                    nc.scalar.activation(sig[:, :], ps_g[:, q, 0:CAP], ACT.Exp, scale=-1.0).then_inc(sig_ok, 1)
                if stage(s, 2):
                    q = k % 2
                    a.wait_ge(y_ps, s - 1)
                    if not (isinstance(s, int) and s - 2 < 2):
                        a.wait_ge(y_st[q], (it * 2 + k // 2 - 1) * 32)
                    nc.scalar.activation(y[:, q, 0, :], ps_y[:, q, 0:C], ACT.Copy)
                    nc.scalar.activation(y[0:R2, q, 1, :], ps_y[0:R2, q, C:2 * C], ACT.Copy).then_inc(y_ok, 1)
                    a.wait_ge(y_ok, s - 1)
                    a.dma_start(ys[bass.ds(s - 2, 1), 0:P].rearrange("e r c -> (e r) c"), y[:, q, 0, :]).then_inc(y_st[q], 16)
                    a.dma_start(ys[bass.ds(s - 2, 1), P:CAP].rearrange("e r c -> (e r) c"), y[0:R2, q, 1, :]).then_inc(y_st[q], 16)
            slots(nc.scalar, slot)
            for q in range(2):
                a.wait_ge(y_st[q], 32 * (E // 2))


def combine(nc, mem, l, dst):
    K = MOE[l]["k"]
    with ExitStack() as c:
        def sb(n, s, t=F32):
            return c.enter_context(nc.sbuf_tensor(f"{n}_f{l}", s, t))

        def sem(n):
            return mem.sem(f"f{l}_{n}")
        NB = 4
        yk = sb("yk", [P, NB, K, C])
        base = sb("base", [P, NB, C])
        gate = sb("gate", [P, B, C])
        acc2 = sb("acc", [P, 2, C])
        res = sb("res", [P, NB, C])
        got = [sem(f"got{k}") for k in range(NB)]
        ld = [sem(f"ld{k}") for k in range(NB)]
        st = [sem(f"st{k}") for k in range(NB)]
        own, done, gates = sem("own"), sem("done"), sem("gates")
        block = c.enter_context(nc.Block())
        src = mem.base_d.rearrange("b (i p) c -> (b i) p c", p=P)
        out = dst.rearrange("b (i p) c -> (b i) p c", p=P)

        @block.gpsimd
        def _(pool):
            for i in range(NT):
                if i >= NB:
                    pool.wait_ge(done, i - NB + 1)
                for k in range(K):
                    nc.gpsimd.indirect_dma_start(out=yk[:, i % NB, k, :], out_offset=None, in_=mem.ys_d[0:SLOTS[l] + 1, :],
                                                 in_offset=bass.IndirectOffsetOnAxis(ap=mem.gidx[:, i, k:k + 1], axis=0)).then_inc(got[i % NB], 16)

        @block.sync
        def _(sp):
            for b in range(B):
                sp.dma_start(gate[:, b, :], mem.mod_d[l, b, 5 * C:6 * C].partition_broadcast(P)).then_inc(gates, 16)
            for i in range(NT + 2):
                if i < NT:
                    if i >= NB:
                        sp.wait_ge(done, i - NB + 1)
                    sp.dma_start(base[:, i % NB, :], src[i]).then_inc(ld[i % NB], 16)
                if i >= 2:
                    n = i - 2
                    sp.wait_ge(done, n + 1)
                    sp.dma_start(out[n], res[:, n % NB, :]).then_inc(st[n % NB], 16)
            for k in range(NB):
                sp.wait_ge(st[k], 16 * (NT // NB))

        @block.vector
        def _(v):
            V = nc.vector
            do = Chain(v, own)
            v.wait_ge(gates, 16 * B)
            for i in range(NT):
                k4, acc = i % NB, acc2[:, i % 2]
                v.wait_ge(got[k4], 16 * K * (i // NB + 1))
                do(V.tensor_scalar(acc[:, :], yk[:, k4, 0, :], mem.wk[:, i, 0:1], None, ALU.mult))
                for k in range(1, K):
                    do(V.scalar_tensor_tensor(out=acc[:, :], in0=yk[:, k4, k, :], scalar=mem.wk[:, i, k:k + 1], in1=acc[:, :],
                                              op0=ALU.mult, op1=ALU.add))
                do(V.tensor_tensor(acc[:, :], acc[:, :], gate[:, i // QB, :], ALU.mult))
                v.wait_ge(ld[k4], 16 * (i // NB + 1))
                if i >= NB:
                    v.wait_ge(st[k4], 16 * (i // NB))
                V.tensor_tensor(res[:, k4, :], acc[:, :], base[:, k4, :], ALU.add).then_inc(done, 1)


class Memory:
    def __init__(self, nc, ctx):
        self.nc, self.ctx, self.named, self.sems = nc, ctx, {}, []

    def sb(self, name, shape, dt):
        return self.ctx.enter_context(self.nc.sbuf_tensor(name, shape, dt))

    def sem(self, name):
        self.sems.append(self.nc.alloc_semaphore(name))
        return self.sems[-1]

    def clear_semaphores(self):
        self.nc.clear_and_free_semaphores(self.sems)
        self.nc.all_engine_barrier()
        self.sems = []

    def dram(self, name, shape, dt):
        return self.nc.dram_tensor(name, shape, dt, kind="Internal").ap()


def adaln_two_layers(nc, A, out):
    with ExitStack() as ctx:
        mem = Memory(nc, ctx)
        mem.A = A
        mem.q_stack = [mem.dram(f"q_stack{l}", [len(a["pairs"]), B, a["g"] * a["d"] * 4, S], BF16) for l, a in enumerate(ATT)]
        mem.k_stack = [mem.dram(f"k_stack{l}", [len(a["pairs"]), B, a["g"] * a["d"], S], BF16) for l, a in enumerate(ATT)]
        mem.v_blocks = [mem.dram(f"v_blocks{l}", [B, a["g"], P, QB, VW], F32) for l, a in enumerate(ATT)]
        mem.att_d = [mem.dram(f"att_d{l}", [B, a["g"], P, QB * 4 * a["d"]], F32) for l, a in enumerate(ATT)]
        mem.amem_d = mem.dram("amem_d", [B, S, C], F32)
        mem.h_d = mem.dram("h_d", [B, S, C], F32)
        mem.hT_d = mem.dram("hT_d", [B, P, CC * S], F32)
        mem.base_d = mem.dram("base_d", [B, S, C], F32)
        mem.x2_d = mem.dram("x2_d", [B, S, C], F32)
        mem.xs_d = mem.dram("xs_d", [SLOTS[0] + 1, C], F32)
        mem.ys_d = mem.dram("ys_d", [SLOTS[0] + 1, C], F32)
        mem.eid_d = mem.dram("eid_d", [MOE[0]["tiles"]], I32)
        mem.scores = mem.sb("scores", [P, NT, 64], F32)
        mem.wk = mem.sb("wk", [P, NT, 8], F32)
        mem.sidx = mem.sb("sidx", [P, NT, 8], I32)
        mem.gidx = mem.sb("gidx", [P, NT, 8], I32)
        mem.zeroed = ctx.enter_context(nc.semaphore("zeroed"))
        mem.zero_count = 16 * (B * ATT[0]["g"] * QB + 2)
        setup(nc, mem, A)
        x = A["L0_attn_x"]
        for l in range(2):
            projections(nc, mem, l, x)
            attention(nc, mem, l)
            after_attention(nc, mem, l, x)
            if l == 0:
                with ExitStack() as c:
                    mem.w1 = c.enter_context(nc.sbuf_tensor("w1_e0", [P, MOE[0]["e"], CC, P], F32))
                    mem.w2 = c.enter_context(nc.sbuf_tensor("w2_e0", [P, MOE[0]["e"], C], F32))
                    mem.w_in = mem.sem("weights")
                    routing(nc, mem, l)
                    spread_and_share(nc, mem, l)
                    experts_any(nc, mem)
            else:
                routing(nc, mem, l)
                spread_and_share(nc, mem, l)
                experts_capped(nc, mem)
            if l == 1:
                combine(nc, mem, l, out)
            x = mem.x2_d
            mem.clear_semaphores()


def kernel(**inputs):
    import numpy as _np
    import concourse.bacc as _bacc
    from concourse import mybir as _mybir
    from concourse.bass_utils import run_bass_kernel_spmd as _run

    nc = _bacc.Bacc("TRN2", target_bir_lowering=False, num_devices=1)
    arrays, A = {}, {}
    for name, value in inputs.items():
        a = _np.ascontiguousarray(value)
        arrays[f"in_{name}"] = a
        A[name] = nc.dram_tensor(f"in_{name}", a.shape, _mybir.dt.from_np(a.dtype), kind="ExternalInput").ap()
    out = nc.dram_tensor("out", [B, S, C], F32, kind="ExternalOutput").ap()
    adaln_two_layers(nc, A, out)
    r = _run(nc, [arrays], core_ids=[0])
    return r.results[0]["out"]
```
